# Optimizing a Trainium2 kernel written in Bass

```python
import numpy as np
import jax
import jax.numpy as jnp

def _softmax(x, axis=-1):
    return jax.nn.softmax(x, axis=axis)

def _gelu(x):
    return jax.nn.gelu(x, approximate=True)

def _silu(x):
    return jax.nn.silu(x)

def _sigmoid(x):
    return jax.nn.sigmoid(x)

def _layernorm(x, axis=-1, eps=1e-05):
    m = jnp.mean(x, axis=axis, keepdims=True)
    v = jnp.var(x, axis=axis, keepdims=True)
    return (x - m) / jnp.sqrt(v + eps)

def _scatter_add(tgt, idx, src, axis=0):
    return tgt.at[idx].add(src)

def _segment_sum(src, seg, n):
    return jax.ops.segment_sum(src, seg, n)
kernel_name = 'mk_gnn_resnorm_d4_gnn_r32_114507'

def setup_inputs(seed: int=0):
    np.random.seed(seed)
    _w = jnp.asarray

    def _rec_inputs():
        import jax
        import jax.numpy as jnp
        _gk = jax.random.key(seed)
        x = -0.0003713 + 1 * jax.random.normal(jax.random.fold_in(_gk, 1), (3125, 128), jnp.float32)
        _s = jax.random.randint(jax.random.fold_in(_gk, 2), (50000,), 0, 3125, jnp.int32)
        _d = jax.random.randint(jax.random.fold_in(_gk, 3), (50000,), 0, 3125, jnp.int32)
        _loop = jnp.arange(3125, dtype=jnp.int32)
        src = jnp.concatenate([_s, _d, _loop])
        dst = jnp.concatenate([_d, _s, _loop])
        _o = jnp.argsort(dst, stable=True)
        src = src[_o]
        dst = dst[_o]
        edge_attr_3 = jax.random.uniform(jax.random.fold_in(_gk, 11), (103125, 3), jnp.float32, 0.0, 0.999999)
        edge_attr_32 = 0.000283511 + 1.00007 * jax.random.normal(jax.random.fold_in(_gk, 12), (103125, 32), jnp.float32)
        edge_type_2 = jax.random.randint(jax.random.fold_in(_gk, 14), (103125,), 0, 2, jnp.int32)
        edge_weight = jax.random.uniform(jax.random.fold_in(_gk, 15), (103125,), jnp.float32, 0.0, 0.999998)
        return (x, src, dst, edge_attr_3, edge_attr_32, edge_type_2, edge_weight)
    x, src, dst, edge_attr_3, edge_attr_32, edge_type_2, edge_weight = _rec_inputs()

    def _L0_gnn_setup():
        import jax, jax.numpy as jnp
        import numpy as np
        N = 3125
        E = 18750
        D = 128
        H = 8
        DH = D // H
        T = 32
        NET = 2

        def _ln(x, g, b, eps=1e-05):
            mu = jnp.mean(x, axis=-1, keepdims=True)
            var = jnp.mean((x - mu) ** 2, axis=-1, keepdims=True)
            return (x - mu) * jax.lax.rsqrt(var + eps) * g + b

        def _expmap(e, c):
            abs_c = jnp.maximum(jnp.abs(c), 1e-15)
            sq = jnp.sqrt(abs_c)
            n = jnp.maximum(jnp.linalg.norm(e, axis=-1, keepdims=True), 1e-15)
            tanh_p = jnp.tanh(sq * n) * e / (sq * n)
            tan_p = jnp.tan(sq * n) * e / (sq * n)
            return jnp.where(c < 0, tanh_p, tan_p)

        def _proj(x, c, eps=1e-05):
            abs_c = jnp.maximum(jnp.abs(c), 1e-15)
            maxnorm = (1.0 - eps) / jnp.sqrt(abs_c)
            norm = jnp.linalg.norm(x, axis=-1, keepdims=True)
            scale = jnp.where(norm > maxnorm, maxnorm / norm, jnp.ones_like(norm))
            return x * scale

        def _forward(x, time_emb, edge_time, Wq, Wk, Wv, rel_q, rel_k, rel_v, Wt, bt, Wd1, bd1, Wd2, bd2, decay_scale, c_mag, hyp_beta, logit_alpha, Wo, bo, g1, be1, g2, be2, Wf1, bf1, Wf2, bf2, src, dst, edge_type):
            n = x.shape[0]
            Q = (x @ Wq).reshape(n, H, DH)
            K = (x @ Wk).reshape(n, H, DH)
            V = (x @ Wv).reshape(n, H, DH)
            q_dst = Q[dst] + rel_q[edge_type].reshape(-1, H, DH)
            k_src = K[src] + rel_k[edge_type].reshape(-1, H, DH)
            v_src = V[src] + rel_v[edge_type].reshape(-1, H, DH)
            k_src = k_src + (time_emb @ Wt + bt).reshape(-1, H, DH)
            euclid = jnp.sum(q_dst * k_src, axis=-1) / np.float32(np.sqrt(DH))
            denom_t = jnp.maximum(1.0, edge_type.max().astype(jnp.float32) + 1.0)
            et = edge_type.astype(jnp.float32)[:, None] / denom_t
            dec_in = jnp.concatenate([edge_time[:, None], et], axis=-1)
            decay_raw = jnp.tanh(jax.nn.relu(dec_in @ Wd1 + bd1) @ Wd2 + bd2)
            decay = jnp.exp(decay_scale[None, :] * decay_raw)
            euclid = euclid * decay
            c = -jnp.abs(c_mag)
            m = _proj(_expmap(x, c), c)
            man_dist = jnp.linalg.norm(m[src] - m[dst], axis=-1)[:, None]
            hyp = -hyp_beta[None, :] * man_dist * decay
            alpha = jax.nn.sigmoid(logit_alpha)[None, :]
            logits = alpha * euclid + (1.0 - alpha) * hyp
            seg_max = jax.ops.segment_max(logits, dst, num_segments=n)
            ex = jnp.exp(logits - seg_max[dst])
            denom = jax.ops.segment_sum(ex, dst, num_segments=n)
            attn = ex / denom[dst]
            agg = jax.ops.segment_sum(v_src * attn[..., None], dst, num_segments=n).reshape(n, D)
            out = agg @ Wo + bo
            x = _ln(x + out, g1, be1)
            ffn = jax.nn.gelu(x @ Wf1 + bf1, approximate=False) @ Wf2 + bf2
            x = _ln(x + ffn, g2, be2)
            return x
        key = jax.random.key(seed)
        ks = jax.random.split(key, 20)

        def lin(k, fi, fo):
            return jax.random.normal(k, (fi, fo), jnp.float32) / np.float32(np.sqrt(fi))
        return {'x': jax.random.normal(ks[0], (N, D), jnp.float32), 'edge_index': jax.random.randint(ks[1], (2, E), 0, N), 'time_emb': jax.random.normal(ks[2], (E, T), jnp.float32), 'edge_type': jax.random.randint(ks[3], (E,), 0, NET), 'edge_time': jax.random.uniform(ks[4], (E,), jnp.float32), 'Wq': lin(ks[5], D, D), 'Wk': lin(ks[6], D, D), 'Wv': lin(ks[7], D, D), 'rel_q': jax.random.normal(ks[8], (NET, D), jnp.float32) * 0.1, 'rel_k': jax.random.normal(ks[9], (NET, D), jnp.float32) * 0.1, 'rel_v': jax.random.normal(ks[10], (NET, D), jnp.float32) * 0.1, 'Wt': lin(ks[11], T, D), 'bt': jnp.zeros((D,), jnp.float32), 'Wd1': lin(ks[12], 2, 64), 'bd1': jnp.zeros((64,), jnp.float32), 'Wd2': lin(ks[13], 64, H), 'bd2': jnp.zeros((H,), jnp.float32), 'decay_scale': jnp.full((H,), 0.5, jnp.float32), 'c_mag': jnp.asarray(1.0, jnp.float32), 'hyp_beta': jnp.ones((H,), jnp.float32), 'logit_alpha': jnp.zeros((H,), jnp.float32), 'Wo': lin(ks[14], D, D), 'bo': jnp.zeros((D,), jnp.float32), 'g1': jnp.ones((D,), jnp.float32), 'be1': jnp.zeros((D,), jnp.float32), 'g2': jnp.ones((D,), jnp.float32), 'be2': jnp.zeros((D,), jnp.float32), 'Wf1': lin(ks[15], D, 4 * D), 'bf1': jnp.zeros((4 * D,), jnp.float32), 'Wf2': lin(ks[16], 4 * D, D), 'bf2': jnp.zeros((D,), jnp.float32)}
    _L0_gnn_all = _L0_gnn_setup()
    _L0_gnn_in = {k: v for k, v in _L0_gnn_all.items() if k in ('Wq', 'Wk', 'Wv', 'rel_q', 'rel_k', 'rel_v', 'Wt', 'bt', 'Wd1', 'bd1', 'Wd2', 'bd2', 'decay_scale', 'c_mag', 'hyp_beta', 'logit_alpha', 'Wo', 'bo', 'g1', 'be1', 'g2', 'be2', 'Wf1', 'bf1', 'Wf2', 'bf2')}
    del _L0_gnn_all

    def _L1_gnn_setup():
        import jax, jax.numpy as jnp
        import numpy as np
        N, E, IN_DIM, D, L, H = (50000, 25000, 128, 128, 4, 8)
        C = D // H
        NEG_SLOPE = 0.2

        def _ln(x, g, b):
            m = x.mean(-1, keepdims=True)
            v = ((x - m) ** 2).mean(-1, keepdims=True)
            return (x - m) / jnp.sqrt(v + 1e-05) * g + b
        key = jax.random.key(seed)
        ks = iter(jax.random.split(key, 32))

        def gl(shape, fan_in):
            return jax.random.normal(next(ks), shape, jnp.float32) / np.sqrt(fan_in)
        inp = {'x': jax.random.normal(next(ks), (N, IN_DIM), jnp.float32), 'edge_index': jax.random.randint(next(ks), (2, E), 0, N, jnp.int32), 'edge_attr': jax.random.uniform(next(ks), (E, 3), jnp.float32), 'Win_w': gl((IN_DIM, D), IN_DIM), 'Win_b': jnp.zeros((D,), jnp.float32), 'ln_in_g': jnp.ones((D,), jnp.float32), 'ln_in_b': jnp.zeros((D,), jnp.float32), 'ln_g': jnp.ones((L, D), jnp.float32), 'ln_b': jnp.zeros((L, D), jnp.float32), 'Wl_w': gl((L, D, D), D), 'Wl_b': jnp.zeros((L, D), jnp.float32), 'Wr_w': gl((L, D, D), D), 'Wr_b': jnp.zeros((L, D), jnp.float32), 'We_w': gl((L, 3, D), 3), 'att': gl((L, H, C), C), 'conv_b': jnp.zeros((L, D), jnp.float32), 'g1_w': gl((L, D, D // 2), D), 'g1_b': jnp.zeros((L, D // 2), jnp.float32), 'g2_w': gl((L, D // 2, D), D // 2), 'g2_b': jnp.zeros((L, D), jnp.float32), 'fn_g': jnp.ones((D,), jnp.float32), 'fn_b': jnp.zeros((D,), jnp.float32)}
        return inp
    _L1_gnn_all = _L1_gnn_setup()
    _L1_gnn_in = {k: v for k, v in _L1_gnn_all.items() if k in ('Win_w', 'Win_b', 'ln_in_g', 'ln_in_b', 'ln_g', 'ln_b', 'Wl_w', 'Wl_b', 'Wr_w', 'Wr_b', 'We_w', 'att', 'conv_b', 'g1_w', 'g1_b', 'g2_w', 'g2_b', 'fn_g', 'fn_b')}
    del _L1_gnn_all

    def _L2_gnn_setup():
        import jax, jax.numpy as jnp
        import numpy as np
        N_NODES = 50000
        N_EDGES = 25000
        D = 128

        def _sage_conv(x, src, dst, Wl, bl, Wr, num_nodes):
            msg = x[src]
            s = jax.ops.segment_sum(msg, dst, num_segments=num_nodes)
            cnt = jax.ops.segment_sum(jnp.ones((src.shape[0],), x.dtype), dst, num_segments=num_nodes)
            agg = s / jnp.maximum(cnt, 1.0)[:, None]
            return agg @ Wl.T + bl + x @ Wr.T
        key = jax.random.key(seed)
        ks = jax.random.split(key, 7)
        scale = 1.0 / np.sqrt(D)
        x = jax.random.normal(ks[0], (N_NODES, D), dtype=jnp.float32)
        edge_index = jax.random.randint(ks[1], (2, N_EDGES), 0, N_NODES, dtype=jnp.int32)
        Wl1 = jax.random.normal(ks[2], (D, D), dtype=jnp.float32) * scale
        bl1 = jnp.zeros((D,), jnp.float32)
        Wr1 = jax.random.normal(ks[3], (D, D), dtype=jnp.float32) * scale
        Wl2 = jax.random.normal(ks[4], (D, D), dtype=jnp.float32) * scale
        bl2 = jnp.zeros((D,), jnp.float32)
        Wr2 = jax.random.normal(ks[5], (D, D), dtype=jnp.float32) * scale
        return {'x': x, 'edge_index': edge_index, 'Wl1': Wl1, 'bl1': bl1, 'Wr1': Wr1, 'Wl2': Wl2, 'bl2': bl2, 'Wr2': Wr2}
    _L2_gnn_all = _L2_gnn_setup()
    _L2_gnn_in = {k: v for k, v in _L2_gnn_all.items() if k in ('Wl1', 'bl1', 'Wr1', 'Wl2', 'bl2', 'Wr2')}
    del _L2_gnn_all

    def _L3_gnn_setup():
        import jax, jax.numpy as jnp
        import numpy as np
        NUM_NODES = 10000
        key = jax.random.key(seed)
        k1, k2, k3, k4 = jax.random.split(key, 4)
        x = jax.random.normal(k1, (NUM_NODES, 128), dtype=jnp.float32)
        edge_index = jax.random.randint(k2, (2, 20000), 0, NUM_NODES, dtype=jnp.int64)
        W = jax.random.normal(k3, (128, 128), dtype=jnp.float32) * (1.0 / np.sqrt(128))
        b = jax.random.normal(k4, (128,), dtype=jnp.float32) * 0.01
        return {'x': x, 'edge_index': edge_index, 'W': W, 'b': b}
    _L3_gnn_all = _L3_gnn_setup()
    _L3_gnn_in = {k: v for k, v in _L3_gnn_all.items() if k in ('W', 'b')}
    del _L3_gnn_all
    return {'x': x, 'src': src, 'dst': dst, 'edge_attr_3': edge_attr_3, 'edge_attr_32': edge_attr_32, 'edge_type_2': edge_type_2, 'edge_weight': edge_weight, 'L0_gnn_Wq': _L0_gnn_in['Wq'], 'L0_gnn_Wk': _L0_gnn_in['Wk'], 'L0_gnn_Wv': _L0_gnn_in['Wv'], 'L0_gnn_rel_q': _L0_gnn_in['rel_q'], 'L0_gnn_rel_k': _L0_gnn_in['rel_k'], 'L0_gnn_rel_v': _L0_gnn_in['rel_v'], 'L0_gnn_Wt': _L0_gnn_in['Wt'], 'L0_gnn_bt': _L0_gnn_in['bt'], 'L0_gnn_Wd1': _L0_gnn_in['Wd1'], 'L0_gnn_bd1': _L0_gnn_in['bd1'], 'L0_gnn_Wd2': _L0_gnn_in['Wd2'], 'L0_gnn_bd2': _L0_gnn_in['bd2'], 'L0_gnn_decay_scale': _L0_gnn_in['decay_scale'], 'L0_gnn_c_mag': _L0_gnn_in['c_mag'], 'L0_gnn_hyp_beta': _L0_gnn_in['hyp_beta'], 'L0_gnn_logit_alpha': _L0_gnn_in['logit_alpha'], 'L0_gnn_Wo': _L0_gnn_in['Wo'], 'L0_gnn_bo': _L0_gnn_in['bo'], 'L0_gnn_g1': _L0_gnn_in['g1'], 'L0_gnn_be1': _L0_gnn_in['be1'], 'L0_gnn_g2': _L0_gnn_in['g2'], 'L0_gnn_be2': _L0_gnn_in['be2'], 'L0_gnn_Wf1': _L0_gnn_in['Wf1'], 'L0_gnn_bf1': _L0_gnn_in['bf1'], 'L0_gnn_Wf2': _L0_gnn_in['Wf2'], 'L0_gnn_bf2': _L0_gnn_in['bf2'], 'L1_gnn_Win_w': _L1_gnn_in['Win_w'], 'L1_gnn_Win_b': _L1_gnn_in['Win_b'], 'L1_gnn_ln_in_g': _L1_gnn_in['ln_in_g'], 'L1_gnn_ln_in_b': _L1_gnn_in['ln_in_b'], 'L1_gnn_ln_g': _L1_gnn_in['ln_g'], 'L1_gnn_ln_b': _L1_gnn_in['ln_b'], 'L1_gnn_Wl_w': _L1_gnn_in['Wl_w'], 'L1_gnn_Wl_b': _L1_gnn_in['Wl_b'], 'L1_gnn_Wr_w': _L1_gnn_in['Wr_w'], 'L1_gnn_Wr_b': _L1_gnn_in['Wr_b'], 'L1_gnn_We_w': _L1_gnn_in['We_w'], 'L1_gnn_att': _L1_gnn_in['att'], 'L1_gnn_conv_b': _L1_gnn_in['conv_b'], 'L1_gnn_g1_w': _L1_gnn_in['g1_w'], 'L1_gnn_g1_b': _L1_gnn_in['g1_b'], 'L1_gnn_g2_w': _L1_gnn_in['g2_w'], 'L1_gnn_g2_b': _L1_gnn_in['g2_b'], 'L1_gnn_fn_g': _L1_gnn_in['fn_g'], 'L1_gnn_fn_b': _L1_gnn_in['fn_b'], 'L2_gnn_Wl1': _L2_gnn_in['Wl1'], 'L2_gnn_bl1': _L2_gnn_in['bl1'], 'L2_gnn_Wr1': _L2_gnn_in['Wr1'], 'L2_gnn_Wl2': _L2_gnn_in['Wl2'], 'L2_gnn_bl2': _L2_gnn_in['bl2'], 'L2_gnn_Wr2': _L2_gnn_in['Wr2'], 'L3_gnn_W': _L3_gnn_in['W'], 'L3_gnn_b': _L3_gnn_in['b']}

def reference(x, src, dst, edge_attr_3, edge_attr_32, edge_type_2, edge_weight, L0_gnn_Wq, L0_gnn_Wk, L0_gnn_Wv, L0_gnn_rel_q, L0_gnn_rel_k, L0_gnn_rel_v, L0_gnn_Wt, L0_gnn_bt, L0_gnn_Wd1, L0_gnn_bd1, L0_gnn_Wd2, L0_gnn_bd2, L0_gnn_decay_scale, L0_gnn_c_mag, L0_gnn_hyp_beta, L0_gnn_logit_alpha, L0_gnn_Wo, L0_gnn_bo, L0_gnn_g1, L0_gnn_be1, L0_gnn_g2, L0_gnn_be2, L0_gnn_Wf1, L0_gnn_bf1, L0_gnn_Wf2, L0_gnn_bf2, L1_gnn_Win_w, L1_gnn_Win_b, L1_gnn_ln_in_g, L1_gnn_ln_in_b, L1_gnn_ln_g, L1_gnn_ln_b, L1_gnn_Wl_w, L1_gnn_Wl_b, L1_gnn_Wr_w, L1_gnn_Wr_b, L1_gnn_We_w, L1_gnn_att, L1_gnn_conv_b, L1_gnn_g1_w, L1_gnn_g1_b, L1_gnn_g2_w, L1_gnn_g2_b, L1_gnn_fn_g, L1_gnn_fn_b, L2_gnn_Wl1, L2_gnn_bl1, L2_gnn_Wr1, L2_gnn_Wl2, L2_gnn_bl2, L2_gnn_Wr2, L3_gnn_W, L3_gnn_b):
    import jax
    import jax.numpy as jnp

    def _L0_gnn_ref(x, edge_index, time_emb, edge_type, edge_time, Wq, Wk, Wv, rel_q, rel_k, rel_v, Wt, bt, Wd1, bd1, Wd2, bd2, decay_scale, c_mag, hyp_beta, logit_alpha, Wo, bo, g1, be1, g2, be2, Wf1, bf1, Wf2, bf2):
        import jax, jax.numpy as jnp
        import numpy as np
        N = 3125
        E = 18750
        D = 128
        H = 8
        DH = D // H
        T = 32
        NET = 2

        def _ln(x, g, b, eps=1e-05):
            mu = jnp.mean(x, axis=-1, keepdims=True)
            var = jnp.mean((x - mu) ** 2, axis=-1, keepdims=True)
            return (x - mu) * jax.lax.rsqrt(var + eps) * g + b

        def _expmap(e, c):
            abs_c = jnp.maximum(jnp.abs(c), 1e-15)
            sq = jnp.sqrt(abs_c)
            n = jnp.maximum(jnp.linalg.norm(e, axis=-1, keepdims=True), 1e-15)
            tanh_p = jnp.tanh(sq * n) * e / (sq * n)
            tan_p = jnp.tan(sq * n) * e / (sq * n)
            return jnp.where(c < 0, tanh_p, tan_p)

        def _proj(x, c, eps=1e-05):
            abs_c = jnp.maximum(jnp.abs(c), 1e-15)
            maxnorm = (1.0 - eps) / jnp.sqrt(abs_c)
            norm = jnp.linalg.norm(x, axis=-1, keepdims=True)
            scale = jnp.where(norm > maxnorm, maxnorm / norm, jnp.ones_like(norm))
            return x * scale

        def _forward(x, time_emb, edge_time, Wq, Wk, Wv, rel_q, rel_k, rel_v, Wt, bt, Wd1, bd1, Wd2, bd2, decay_scale, c_mag, hyp_beta, logit_alpha, Wo, bo, g1, be1, g2, be2, Wf1, bf1, Wf2, bf2, src, dst, edge_type):
            n = x.shape[0]
            Q = (x @ Wq).reshape(n, H, DH)
            K = (x @ Wk).reshape(n, H, DH)
            V = (x @ Wv).reshape(n, H, DH)
            q_dst = Q[dst] + rel_q[edge_type].reshape(-1, H, DH)
            k_src = K[src] + rel_k[edge_type].reshape(-1, H, DH)
            v_src = V[src] + rel_v[edge_type].reshape(-1, H, DH)
            k_src = k_src + (time_emb @ Wt + bt).reshape(-1, H, DH)
            euclid = jnp.sum(q_dst * k_src, axis=-1) / np.float32(np.sqrt(DH))
            denom_t = jnp.maximum(1.0, edge_type.max().astype(jnp.float32) + 1.0)
            et = edge_type.astype(jnp.float32)[:, None] / denom_t
            dec_in = jnp.concatenate([edge_time[:, None], et], axis=-1)
            decay_raw = jnp.tanh(jax.nn.relu(dec_in @ Wd1 + bd1) @ Wd2 + bd2)
            decay = jnp.exp(decay_scale[None, :] * decay_raw)
            euclid = euclid * decay
            c = -jnp.abs(c_mag)
            m = _proj(_expmap(x, c), c)
            man_dist = jnp.linalg.norm(m[src] - m[dst], axis=-1)[:, None]
            hyp = -hyp_beta[None, :] * man_dist * decay
            alpha = jax.nn.sigmoid(logit_alpha)[None, :]
            logits = alpha * euclid + (1.0 - alpha) * hyp
            seg_max = jax.ops.segment_max(logits, dst, num_segments=n)
            ex = jnp.exp(logits - seg_max[dst])
            denom = jax.ops.segment_sum(ex, dst, num_segments=n)
            attn = ex / denom[dst]
            agg = jax.ops.segment_sum(v_src * attn[..., None], dst, num_segments=n).reshape(n, D)
            out = agg @ Wo + bo
            x = _ln(x + out, g1, be1)
            ffn = jax.nn.gelu(x @ Wf1 + bf1, approximate=False) @ Wf2 + bf2
            x = _ln(x + ffn, g2, be2)
            return x
        src, dst = (edge_index[0], edge_index[1])
        return _forward(x, time_emb, edge_time, Wq, Wk, Wv, rel_q, rel_k, rel_v, Wt, bt, Wd1, bd1, Wd2, bd2, decay_scale, c_mag, hyp_beta, logit_alpha, Wo, bo, g1, be1, g2, be2, Wf1, bf1, Wf2, bf2, src, dst, edge_type)

    def _L1_gnn_ref(x, edge_index, edge_attr, Win_w, Win_b, ln_in_g, ln_in_b, ln_g, ln_b, Wl_w, Wl_b, Wr_w, Wr_b, We_w, att, conv_b, g1_w, g1_b, g2_w, g2_b, fn_g, fn_b):
        import jax, jax.numpy as jnp
        import numpy as np
        N, E, IN_DIM, D, L, H = (50000, 25000, 128, 128, 4, 8)
        C = D // H
        NEG_SLOPE = 0.2

        def _ln(x, g, b):
            m = x.mean(-1, keepdims=True)
            v = ((x - m) ** 2).mean(-1, keepdims=True)
            return (x - m) / jnp.sqrt(v + 1e-05) * g + b
        n = x.shape[0]
        src, dst = (edge_index[0], edge_index[1])
        h = _ln(jax.nn.gelu(x @ Win_w + Win_b), ln_in_g, ln_in_b)
        n_layers = Wl_w.shape[0]
        for l in range(n_layers):
            z = _ln(h, ln_g[l], ln_b[l])
            xl = (z @ Wl_w[l] + Wl_b[l]).reshape(n, H, C)
            xr = (z @ Wr_w[l] + Wr_b[l]).reshape(n, H, C)
            ee = (edge_attr @ We_w[l]).reshape(-1, H, C)
            xj = xl[src]
            m = jax.nn.leaky_relu(xj + xr[dst] + ee, NEG_SLOPE)
            logit = jnp.einsum('ehc,hc->eh', m, att[l])
            amax = jax.ops.segment_max(logit, dst, num_segments=n)
            ex = jnp.exp(logit - amax[dst])
            den = jax.ops.segment_sum(ex, dst, num_segments=n)
            alpha = ex / den[dst]
            agg = jax.ops.segment_sum(alpha[:, :, None] * xj, dst, num_segments=n)
            conv_out = agg.reshape(n, D) + conv_b[l]
            delta = jax.nn.gelu(conv_out)
            g = jax.nn.sigmoid(jax.nn.gelu(delta @ g1_w[l] + g1_b[l]) @ g2_w[l] + g2_b[l])
            h = h + g * delta
        return _ln(h, fn_g, fn_b)

    def _L2_gnn_ref(x, edge_index, Wl1, bl1, Wr1, Wl2, bl2, Wr2):
        import jax, jax.numpy as jnp
        import numpy as np
        N_NODES = 50000
        N_EDGES = 25000
        D = 128

        def _sage_conv(x, src, dst, Wl, bl, Wr, num_nodes):
            msg = x[src]
            s = jax.ops.segment_sum(msg, dst, num_segments=num_nodes)
            cnt = jax.ops.segment_sum(jnp.ones((src.shape[0],), x.dtype), dst, num_segments=num_nodes)
            agg = s / jnp.maximum(cnt, 1.0)[:, None]
            return agg @ Wl.T + bl + x @ Wr.T
        src, dst = (edge_index[0], edge_index[1])
        n = x.shape[0]
        h = _sage_conv(x, src, dst, Wl1, bl1, Wr1, n)
        out = _sage_conv(h, src, dst, Wl2, bl2, Wr2, n)
        return out

    def _L3_gnn_ref(x, edge_index, W, b):
        import jax, jax.numpy as jnp
        import numpy as np
        NUM_NODES = 10000
        src, dst = (edge_index[0], edge_index[1])
        num_nodes = x.shape[0]
        aggregated = jax.ops.segment_sum(x[src], dst, num_segments=num_nodes)
        degree = jax.ops.segment_sum(jnp.ones_like(dst, dtype=x.dtype), dst, num_segments=num_nodes)
        degree = jnp.maximum(degree, 1.0)
        aggregated = aggregated / degree[:, None]
        out = jax.nn.relu(jnp.einsum('nd,od->no', aggregated + x, W) + b)
        return out
    edge_index = jnp.stack([src, dst])
    x = _layernorm(x + _L0_gnn_ref(x, edge_index, edge_attr_32, edge_type_2, edge_weight, L0_gnn_Wq, L0_gnn_Wk, L0_gnn_Wv, L0_gnn_rel_q, L0_gnn_rel_k, L0_gnn_rel_v, L0_gnn_Wt, L0_gnn_bt, L0_gnn_Wd1, L0_gnn_bd1, L0_gnn_Wd2, L0_gnn_bd2, L0_gnn_decay_scale, L0_gnn_c_mag, L0_gnn_hyp_beta, L0_gnn_logit_alpha, L0_gnn_Wo, L0_gnn_bo, L0_gnn_g1, L0_gnn_be1, L0_gnn_g2, L0_gnn_be2, L0_gnn_Wf1, L0_gnn_bf1, L0_gnn_Wf2, L0_gnn_bf2), axis=-1)
    x = _layernorm(x + _L1_gnn_ref(x, edge_index, edge_attr_3, L1_gnn_Win_w, L1_gnn_Win_b, L1_gnn_ln_in_g, L1_gnn_ln_in_b, L1_gnn_ln_g, L1_gnn_ln_b, L1_gnn_Wl_w, L1_gnn_Wl_b, L1_gnn_Wr_w, L1_gnn_Wr_b, L1_gnn_We_w, L1_gnn_att, L1_gnn_conv_b, L1_gnn_g1_w, L1_gnn_g1_b, L1_gnn_g2_w, L1_gnn_g2_b, L1_gnn_fn_g, L1_gnn_fn_b), axis=-1)
    x = _layernorm(x + _L2_gnn_ref(x, edge_index, L2_gnn_Wl1, L2_gnn_bl1, L2_gnn_Wr1, L2_gnn_Wl2, L2_gnn_bl2, L2_gnn_Wr2), axis=-1)
    x = _layernorm(x + _L3_gnn_ref(x, edge_index, L3_gnn_W, L3_gnn_b), axis=-1)
    return x

_drawn_inputs = setup_inputs


def setup_inputs(seed=0):
    import zlib

    import numpy as np

    out = dict(_drawn_inputs(seed))
    spreads = {'L0_gnn_bt': (0.0, 2.0),
     'L0_gnn_bd1': (0.0, 0.8),
     'L0_gnn_bd2': (0.0, 2.0),
     'L0_gnn_decay_scale': (0.5, 0.6),
     'L0_gnn_hyp_beta': (1.0, 0.6),
     'L0_gnn_logit_alpha': (0.0, 0.8),
     'L0_gnn_bo': (0.0, 0.1),
     'L0_gnn_g1': (1.0, 0.2),
     'L0_gnn_be1': (0.0, 0.1),
     'L0_gnn_g2': (1.0, 0.2),
     'L0_gnn_be2': (0.0, 0.1),
     'L0_gnn_bf1': (0.0, 0.1),
     'L0_gnn_bf2': (0.0, 0.1),
     'L1_gnn_Win_b': (0.0, 0.1),
     'L1_gnn_ln_in_g': (1.0, 0.2),
     'L1_gnn_ln_in_b': (0.0, 0.1),
     'L1_gnn_ln_g': (1.0, 0.2),
     'L1_gnn_ln_b': (0.0, 0.1),
     'L1_gnn_Wl_b': (0.0, 0.1),
     'L1_gnn_Wr_b': (0.0, 0.8),
     'L1_gnn_conv_b': (0.0, 0.1),
     'L1_gnn_g1_b': (0.0, 0.8),
     'L1_gnn_g2_b': (0.0, 0.71),
     'L1_gnn_fn_g': (1.0, 0.2),
     'L1_gnn_fn_b': (0.0, 0.1),
     'L2_gnn_bl1': (0.0, 0.1),
     'L2_gnn_bl2': (0.0, 0.1)}
    factors = {'edge_attr_3': 3.584,
     'edge_weight': 8.0,
     'L0_gnn_rel_q': 6.37,
     'L0_gnn_rel_k': 8.0,
     'L0_gnn_Wd1': 4.449,
     'L0_gnn_Wd2': 4.623,
     'L1_gnn_g1_w': 3.402,
     'L1_gnn_g2_w': 2.942,
     'L3_gnn_b': 8.0}
    for name, (base, spread) in spreads.items():
        noise = np.random.default_rng([zlib.crc32(name.encode()), seed]).standard_normal(out[name].shape)
        drawn = base * np.exp(spread * noise) if base else spread * noise
        out[name] = jnp.asarray(drawn.astype(out[name].dtype))
    for name, factor in factors.items():
        out[name] = (out[name] * factor).astype(out[name].dtype)
    return out
```

```python
from contextlib import ExitStack

import concourse.bass as bass
import concourse.mybir as mybir

F32 = mybir.dt.float32
I32 = mybir.dt.int32
ALU = mybir.AluOpType
ACT = mybir.ActivationFunctionType
AX = mybir.AxisListType.X

P = 128
D = 128
N = 3125
E = 103125
HEADS = 8
DH = D // HEADS
LAYERS = 4
EPP = 8
CHUNK = P * EPP
NCH = -(-E // CHUNK)
LAST_WIN = N // P
NT = LAST_WIN + 2
NP = NT * P
STEPS = NCH + LAST_WIN // 2
STEPS += STEPS % 2
TURNS = STEPS // 2
HALF = 4 * P
HW = DH + 2
AW = HEADS * HW + HEADS
RC = HEADS * HW
NEG = -1.0e30
PK = 5 * EPP
GROUPS = [(g * 4, min(4, NT - g * 4)) for g in range(-(-NT // 4))]
NG = len(GROUPS)
SUMW = D + 2
LOADS = {"L0": 10, "L1": 7, "sum": 3}
PI = 3.141592653589793

OHT0, TR0, MM0, SM, AGG, HID0 = 0, 0, 2, 5, 6, 4


def build(nc, a, out):
    ctx = ExitStack()
    with ctx:
        def sb(name, shape, dt=F32):
            return ctx.enter_context(nc.sbuf_tensor(name, shape, dt))

        def sem(name):
            return ctx.enter_context(nc.semaphore(name))

        def dram(name, shape, dt=F32):
            return nc.dram_tensor(name, shape, dt, kind="Internal").ap()

        kvm_tab = dram("kvm_tab", (NP, 3 * D))
        qm_tab = dram("qm_tab", (NP, 2 * D))
        xl_tab = dram("xl_tab", (NP, D))
        xr_tab = dram("xr_tab", (NP, D))
        pk_tab = dram("pk_tab", (NCH, P, PK))
        g_tab = dram("g_tab", (2, P, P))
        step_tab = dram("step_tab", (P, 2), I32)
        base_tab = dram("base_tab", (P, 1))

        def node_buf(name):
            return sb(name, [P, NT * D])

        X, H, A, B, C, T = (node_buf(n) for n in ("x_nodes", "h_nodes", "a_nodes", "b_nodes", "c_nodes", "t_chans"))

        def nodes(buf):
            return buf[:, :].rearrange("p (t d) -> p t d", d=D)

        rows = sb("gathered_rows", [P, 2, EPP * 3 * D])
        onehot = sb("onehot", [P, 2, EPP, 2 * P])
        onehot_t = sb("onehot_t", [P, 2, EPP * P])
        weighted = sb("weighted", [P, EPP, AW])
        acc = sb("acc", [P, NT, AW])
        src_ids = sb("src_ids", [P, 2, EPP], I32)
        type_i = sb("type_i", [P, 2, EPP], I32)
        type_f = sb("type_f", [P, 2, EPP])
        pk = sb("pk", [P, 2, PK])
        gp = sb("gp", [P, 2, P])
        win = sb("win_rows", [P, 2, 2, 2 * D])
        wbase = sb("wbase", [P, 2])
        rel = sb("rel", [P, EPP])
        attr = sb("attr", [P, 2, CHUNK])
        chan = sb("chan", [P, 2, HALF])
        prod = sb("prod", [P, 2, HALF])
        sq = sb("sq", [P, HALF])
        dec_h = C[:, 0:2 * HALF].rearrange("p (h e) -> p h e", h=2)
        S64 = EPP * HEADS
        small = {n: sb(n, [P, S64]) for n in ("pen_f", "pen_r", "logit", "run_f", "run_r", "m1", "m2", "dec", "dec2")}
        dist2 = sb("dist2", [P, EPP])
        dist = sb("dist", [P, EPP])
        ab = sb("ab", [P, 40])
        scans = sb("scans", [P, 130])
        delta = sb("delta", [P, S64 + HEADS])
        ex = sb("ex", [P, S64 + HEADS])
        grow = sb("grow", [P, 2, HEADS])
        ident = sb("ident", [P, P])
        iota = sb("iota", [P, 2 * P])
        blk = sb("blk", [P, HEADS])
        blk4 = sb("blk4", [P, HEADS])
        misc = sb("misc", [P, 8])
        steps_i = sb("steps_i", [1, 2 * P], I32)
        cols = sb("cols", [P, 36, NT])
        one_col = sb("one_col", [P, 16])

        def mat(name, k=P, n=D):
            return sb(name, [k, n])

        W = {n: mat("w_" + n) for n in ("Wq", "Wk", "Wv", "Wo", "Win", "Wl", "Wr", "L2_Wl1", "L2_Wr1", "L2_Wl2", "L2_Wr2", "L3_W")}
        Wf1 = mat("w_f1", P, 4 * D)
        Wf2 = sb("w_f2", [P, 4, D])
        bf1 = mat("b_f1", P, 4)
        wk34 = mat("w_k34", P, D)
        relq = mat("w_relq", P, D)
        relv = sb("w_relv", [P, 2, D])
        wd1t = mat("w_d1t", P, 64)
        bd1r = mat("b_d1r", 34, 64)
        bt34 = mat("b_t34", 34, D)
        wd2 = mat("w_d2", 65, HEADS)
        hp = sb("head_params", [P, 6, HEADS])
        cm = sb("c_params", [P, 8])
        V = {n: mat("v_" + n) for n in ("bo", "g1", "be1", "g2", "be2", "bf2", "Win_b", "ln_in_g", "ln_in_b",
                                          "ln_g", "ln_b", "Wl_b", "Wr_b", "conv_b", "g2_b", "fn_g", "fn_b",
                                          "L2_bl1", "L2_bl2", "L3_b")}
        We = mat("w_e", P, D)
        att = mat("att_col", P, 1)
        attb = mat("att_blk", P, HEADS)
        g1w = mat("w_g1", P, 64)
        g1b = mat("b_g1", 64, 1)
        g2w = mat("w_g2", 64, D)

        ps = ctx.enter_context(nc.psum_tensor("ps", [P, 8, 512], F32))

        loaded = sem("loaded")
        pre_asked = sem("pre_asked")
        pre_tr = sem("pre_tr")
        pre_done = sem("pre_done")
        steps_in = sem("steps_in")
        layer_in = sem("layer_in")
        layer_used = sem("layer_used")
        src_ready = sem("src_ready")
        tr_done, tr_copied = sem("tr_done"), sem("tr_copied")
        mm_done, mm_copied = sem("mm_done"), sem("mm_copied")
        hid_mm, hid_act = sem("hid_mm"), sem("hid_act")
        ask_act, act_gave = sem("ask_act"), sem("act_gave")
        store_ask, stored = sem("store_ask"), sem("stored")
        in_ready = {n: [sem(f"in_{n}{b}") for b in range(2)] for n in ("L0", "L1", "sum")}
        gathered = [sem(f"gathered{b}") for b in range(2)]
        PER_STEP = {"oh_ready": 1, "oht_mm": 4, "oht_ready": 4, "z_mm": 2, "z_copied": 2, "z_used": 2, "logit_mm": 1,
                    "ab_ready": 1, "ab_mm": 1, "scan_ready": 1, "back_mm": 1, "delta_ready": 1,
                    "ex_ready": 1, "weighted_ready": 1, "agg_mm": 1, "acc_done": 1, "types_ready": 1, "dech_mm": 2,
                    "dech_ready": 2, "tanh_ready": 1, "decs_ready": 1, "decay_ready": 1, "dist_asked": 1, "dist_ready": 1}
        s = {n: sem(n) for n in PER_STEP}
        OF = {"sp": (), "act": ("oht_ready", "z_copied", "ex_ready", "dech_ready", "tanh_ready", "decay_ready", "dist_ready"),
              "pe": ("oht_mm", "z_mm", "logit_mm", "ab_mm", "back_mm", "agg_mm", "dech_mm"),
              "dve": ("oh_ready", "z_used", "ab_ready", "scan_ready", "delta_ready", "weighted_ready", "acc_done",
                      "types_ready", "decs_ready", "dist_asked")}

        def start_up(eng, who):
            for n in OF[who]:
                eng.sem_inc(s[n], 2 * PER_STEP[n])

        def after(eng, name, k, part=None):
            n = PER_STEP[name]
            eng.wait_ge(s[name], k * n + (n if part is None else part + 1))

        def hold(eng, which, value):
            eng.wait_ge(which, value)
            eng.nop(nofuse=True)

        def first_step(edge_pass):
            return edge_pass * STEPS + 2

        bcast = lambda ap: ap.partition_broadcast(P)
        vec = lambda name: bcast(a[name])
        lvec = lambda name, l: bcast(a[name][l])
        const_loads = [
            (ident[:, :], a["c_ident"]), (iota[:, :], a["c_iota"]), (blk[:, :], a["c_blk"]),
            (misc[:, :], a["c_misc"]),
            (X[:, :].rearrange("p (t d) -> p t d", d=D), a["x"].rearrange("(t p) d -> p t d", p=P)),
            (Wf1[:, :], a["L0_gnn_Wf1"]), (Wf2[:, :, :], a["L0_gnn_Wf2"].rearrange("(p k) n -> p k n", p=P)),
            (bf1[:, :], a["L0_gnn_bf1"].rearrange("(p k) -> p k", p=P)),
            (relv[:, 0, :], bcast(a["L0_gnn_rel_v"][0])), (relv[:, 1, :], bcast(a["L0_gnn_rel_v"][1])),
            (bd1r[32:34, :], a["L0_gnn_bd1"].partition_broadcast(2)),
            (bt34[32:34, :], a["L0_gnn_bt"].partition_broadcast(2)),
            (wd2[0:64, :], a["L0_gnn_Wd2"]), (wd2[64:65, :], a["L0_gnn_bd2"].partition_broadcast(1)),
            (hp[:, 0, :], vec("L0_gnn_decay_scale")), (hp[:, 1, :], vec("L0_gnn_hyp_beta")),
            (hp[:, 2, :], vec("L0_gnn_logit_alpha")),
            (cm[:, 0:1], bcast(a["L0_gnn_c_mag"])),
        ]
        row_loads = [
            (wk34[0:32, :], a["L0_gnn_Wt"]), (wk34[32:33, :], a["L0_gnn_rel_k"][1:2]),
            (wk34[33:34, :], a["L0_gnn_rel_k"][0:1]),
            (relq[32:33, :], a["L0_gnn_rel_q"][1:2]), (relq[33:34, :], a["L0_gnn_rel_q"][0:1]),
            (wd1t[32:33, :], a["L0_gnn_Wd1"][1:2]), (wd1t[34:35, :], a["L0_gnn_Wd1"][0:1]),
        ]
        for n in ("Wq", "Wk", "Wv", "Wo"):
            const_loads.append((W[n][:, :], a["L0_gnn_" + n]))
        const_loads.append((W["Win"][:, :], a["L1_gnn_Win_w"]))
        for n in ("Wl1", "Wr1", "Wl2", "Wr2"):
            const_loads.append((W["L2_" + n][:, :], a["L2_gnn_" + n + "_T"]))
        const_loads.append((W["L3_W"][:, :], a["L3_gnn_W_T"]))
        for n in ("bo", "g1", "be1", "g2", "be2", "bf2"):
            const_loads.append((V[n][:, :], vec("L0_gnn_" + n)))
        for n in ("Win_b", "ln_in_g", "ln_in_b", "fn_g", "fn_b"):
            const_loads.append((V[n][:, :], vec("L1_gnn_" + n)))
        for n in ("bl1", "bl2"):
            const_loads.append((V["L2_" + n][:, :], vec("L2_gnn_" + n)))
        const_loads.append((V["L3_b"][:, :], vec("L3_gnn_b")))

        dst_i = T[:, 0:NCH * (EPP + 2)].bitcast(I32).rearrange("p (c k) -> p c k", k=EPP + 2)
        dst_f = A[:, 0:NCH * (EPP + 2)].rearrange("p (c k) -> p c k", k=EPP + 2)
        same = B[:, 0:NCH * (EPP + 1)].rearrange("p (c k) -> p c k", k=EPP + 1)
        pk_all = rows[:, :, :].rearrange("p b n -> p (b n)")[:, 0:NCH * PK].rearrange("p (c k) -> p c k", k=PK)
        g_all = C[:, 0:2 * NCH].rearrange("p (g c) -> p g c", g=2)
        g_out = C[:, 1024:1024 + 2 * P].rearrange("p (g c) -> p g c", g=2)
        types_all = H[:, 0:NCH * EPP].bitcast(I32)
        ends_i = H[:, 1024:1024 + 2 * NCH].bitcast(I32).rearrange("p (g c) -> p g c", g=2)
        ends = H[:, 1280:1280 + 16 * P].rearrange("p (g c) -> p g c", g=16)
        pre_loads = [
            (dst_i, a["dst_win"]), (types_all.rearrange("p (c k) -> p c k", k=EPP), a["type_edges"].rearrange("c p k -> p c k")),
            (ends_i, a["dst_ends"].partition_broadcast(P)),
        ]

        block = ctx.enter_context(nc.Block())

        @block.sync
        def _(sp):
            for dst_ap, src_ap in const_loads + pre_loads:
                sp.dma_start(dst_ap, src_ap).then_inc(loaded, 16)
            sp.wait_ge(pre_asked, 1)
            for dst_ap, src_ap in row_loads:
                sp.dma_start(dst_ap, src_ap).then_inc(loaded, 16)
            sp.wait_ge(pre_asked, 3)
            sp.dma_start(pk_tab.rearrange("c p k -> p c k"), pk_all).then_inc(pre_done, 16)
            sp.dma_start(g_tab.rearrange("g c p -> c g p")[0:NCH], g_out[0:NCH]).then_inc(pre_done, 16)
            sp.dma_start(step_tab, ends[:, 15, 0:2].bitcast(I32)).then_inc(pre_done, 16)
            sp.dma_start(base_tab, ends[:, 15, 2:3]).then_inc(pre_done, 16)
            sp.wait_ge(pre_done, 4 * 16)
            sp.dma_start(steps_i[:, :], step_tab.rearrange("p k -> (p k)").partition_broadcast(1)).then_inc(steps_in, 16)

            def step_inputs(kind, k, turn, uses, b, number):
                r = turn * 2 + b
                hold(sp, s["acc_done"], k - 2 + 1)
                c = sp.value_load(steps_i[0:1, bass.ds(r * 2, 1)], min_val=0, max_val=NCH - 1)
                ready = in_ready[kind][b]
                sp.dma_start(src_ids[:, b, :], a["src_edges"][c]).then_inc(ready, 16)
                sp.dma_start(pk[:, b, :], pk_tab[c]).then_inc(ready, 16)
                sp.dma_start(wbase[:, b:b + 1], base_tab[r].partition_broadcast(P)).then_inc(ready, 16)
                if kind == "sum":
                    return
                w = sp.value_load(steps_i[0:1, bass.ds(r * 2 + 1, 1)], min_val=0, max_val=LAST_WIN)
                for g in range(2):
                    sp.dma_start(gp[32 * g:32 * g + HEADS, b, :], g_tab[g, c].partition_broadcast(HEADS)).then_inc(ready, 16)
                if kind == "L0":
                    sp.dma_start(win[:, b, :, :], qm_tab.rearrange("(w p) d -> w p d", p=P)[bass.ds(w, 2)].rearrange("w p d -> p w d")).then_inc(ready, 16)
                    sp.dma_start(attr[0:32, b, :], a["time_edges"][c]).then_inc(ready, 16)
                    sp.dma_start(attr[96:98, b, :].bitcast(I32), a["type_rows"][c].partition_broadcast(2)).then_inc(ready, 16)
                    sp.dma_start(type_i[:, b, :], a["type_edges"][c]).then_inc(ready, 16)
                    sp.dma_start(attr[34:35, b, :], a["weight_rows"][c].partition_broadcast(1)).then_inc(ready, 16)
                else:
                    sp.dma_start(win[:, b, :, 0:D], xr_tab.rearrange("(w p) d -> w p d", p=P)[bass.ds(w, 2)].rearrange("w p d -> p w d")).then_inc(ready, 16)
                    sp.dma_start(attr[0:3, b, :], a["attr_edges"][c]).then_inc(ready, 16)

            sp.wait_ge(steps_in, 16)
            sp.wait_ge(store_ask, 1)
            for i, buf in enumerate((A, B, C)):
                sp.dma_start(kvm_tab.rearrange("(t p) d -> p t d", p=P)[:, :, i * D:(i + 1) * D], nodes(buf)).then_inc(stored, 16)
            for i, buf in enumerate((H, T)):
                sp.dma_start(qm_tab.rearrange("(t p) d -> p t d", p=P)[:, :, i * D:(i + 1) * D], nodes(buf)).then_inc(stored, 16)
            sp.wait_ge(stored, 5 * 16)
            with sp.Fori(0, TURNS) as i:
                for b in range(2):
                    step_inputs("L0", first_step(0) + i * 2 + b, i, None, b, None)

            with sp.Fori(0, LAYERS) as l:
                hold(sp, layer_used, l + 1)
                for dst_ap, src_ap in (
                    (W["Wl"][:, :], a["L1_gnn_Wl_w"][l]), (W["Wr"][:, :], a["L1_gnn_Wr_w"][l]), (We[0:3, :], a["L1_gnn_We_w"][l]),
                    (att[:, :], a["L1_gnn_att"][l]), (g1w[:, :], a["L1_gnn_g1_w"][l]), (g1b[:, :], a["L1_gnn_g1_b"][l]),
                    (g2w[:, :], a["L1_gnn_g2_w"][l]), (V["ln_g"][:, :], lvec("L1_gnn_ln_g", l)), (V["ln_b"][:, :], lvec("L1_gnn_ln_b", l)),
                    (V["Wl_b"][:, :], lvec("L1_gnn_Wl_b", l)), (V["Wr_b"][:, :], lvec("L1_gnn_Wr_b", l)),
                    (V["conv_b"][:, :], lvec("L1_gnn_conv_b", l)), (V["g2_b"][:, :], lvec("L1_gnn_g2_b", l))):
                    sp.dma_start(dst_ap, src_ap).then_inc(layer_in, 16)
                hold(sp, store_ask, l + 2)
                sp.dma_start(xl_tab.rearrange("(t p) d -> p t d", p=P), nodes(B)).then_inc(stored, 16)
                sp.dma_start(xr_tab.rearrange("(t p) d -> p t d", p=P), nodes(C)).then_inc(stored, 16)
                hold(sp, stored, (l + 1) * 32 + 5 * 16)
                with sp.Fori(0, TURNS) as i:
                    for b in range(2):
                        step_inputs("L1", first_step(1) + l * STEPS + i * 2 + b, i, None, b, None)

            for n, buf in enumerate((X, B, X)):
                sp.wait_ge(store_ask, 2 + LAYERS + n)
                sp.dma_start(xl_tab.rearrange("(t p) d -> p t d", p=P), nodes(buf)).then_inc(stored, 16)
                sp.wait_ge(stored, 5 * 16 + LAYERS * 32 + (n + 1) * 16)
                with sp.Fori(0, TURNS) as i:
                    for b in range(2):
                        step_inputs("sum", first_step(1 + LAYERS + n) + i * 2 + b, i, None, b, None)

            sp.wait_ge(store_ask, 2 + LAYERS + 3)
            sp.dma_start(out[0:LAST_WIN * P].rearrange("(t p) d -> p t d", p=P), nodes(X)[:, 0:LAST_WIN, :]).then_inc(stored, 16)
            sp.dma_start(out[LAST_WIN * P:N], X[0:N - LAST_WIN * P, LAST_WIN * D:(LAST_WIN + 1) * D]).then_inc(stored, 16)
            sp.wait_ge(stored, 5 * 16 + LAYERS * 32 + 3 * 16 + 32)

        @block.gpsimd
        def _(pool):
            def gather(kind, table, width, uses, b, pitch=None):
                pitch = pitch or width
                hold(pool, in_ready[kind][b], (uses + 1) * 16 * LOADS[kind])
                for j in range(EPP):
                    pool.indirect_dma_start(rows[:, b, j * pitch:j * pitch + width], None, table,
                                            bass.IndirectOffsetOnAxis(ap=src_ids[:, b, j:j + 1], axis=0)).then_inc(gathered[b], 16)

            with pool.Fori(0, TURNS) as i:
                for b in range(2):
                    gather("L0", kvm_tab, 3 * D, i, b)
            with pool.Fori(0, LAYERS) as l:
                with pool.Fori(0, TURNS) as i:
                    for b in range(2):
                        gather("L1", xl_tab, D, l * TURNS + i, b)
            for n in range(3):
                with pool.Fori(0, TURNS) as i:
                    for b in range(2):
                        gather("sum", xl_tab, D, i + n * TURNS, b, SUMW)

        @block.scalar
        def _(act):
            start_up(act, "act")

            def copy_turned(n):
                for g, (t0, nt) in enumerate(GROUPS):
                    act.wait_ge(tr_done, n * NG + g + 1)
                    act.copy(T[:, t0 * D:(t0 + nt) * D], ps[:, TR0 + g % 2, 0:nt * D]).then_inc(tr_copied, 1)

            def asked(n):
                act.wait_ge(ask_act, n + 1)

            col = lambda i: cols[:, i, :]
            asked(0)
            act.activation(hp[:, 3, :], hp[:, 2, :], ACT.Sigmoid)
            act.activation(cm[:, 2:3], cm[:, 1:2], ACT.Sqrt)
            act.activation(col(1), col(0), ACT.Sqrt).then_inc(act_gave, 1)
            asked(1)
            act.activation(col(7), col(3), ACT.Tanh)
            act.activation(col(8), col(4), ACT.Sin)
            act.activation(col(9), col(5), ACT.Sin).then_inc(act_gave, 1)
            asked(2)
            act.activation(col(13), col(12), ACT.Sqrt).then_inc(act_gave, 1)
            copy_turned(0)

            def step_turned(k, b):
                for q in range(4):
                    after(act, "oht_mm", k, q)
                    act.copy(onehot_t[:, :, q * 2 * P:(q + 1) * 2 * P].rearrange("p w (j e) -> p j w e", e=P),
                             ps[:, OHT0 + q % 2, :].rearrange("p (j w e) -> p j w e", j=2, w=2)).then_inc(s["oht_ready"], 1)

            def exps(k):
                after(act, "delta_ready", k)
                act.activation(ex[:, :], delta[:, :], ACT.Exp).then_inc(s["ex_ready"], 1)

            with act.Fori(0, TURNS) as i:
                for b in range(2):
                    k = first_step(0) + i * 2 + b
                    step_turned(k, b)
                    for h in range(2):
                        after(act, "dech_mm", k, h)
                        act.activation(dec_h[0:64, h, :], ps[0:64, OHT0 + h, :], ACT.Relu).then_inc(s["dech_ready"], 1)
                    for h in range(2):
                        after(act, "z_mm", k, h)
                        act.copy(chan[:, h, :], ps[:, MM0 + 1, :])
                        act.activation(sq[:, :], ps[:, MM0 + 2, :], ACT.Square).then_inc(s["z_copied"], 1)
                    after(act, "dist_asked", k)
                    act.activation(small["dec"][:, :], ps[:, SM, 256:256 + S64], ACT.Tanh).then_inc(s["tanh_ready"], 1)
                    after(act, "decs_ready", k)
                    act.activation(small["dec"][:, :], small["dec2"][:, :], ACT.Exp).then_inc(s["decay_ready"], 1)
                    act.activation(dist[:, :], dist2[:, :], ACT.Sqrt).then_inc(s["dist_ready"], 1)
                    exps(k)

            copy_turned(1)
            asked(3)
            act.activation(col(2), col(1), ACT.Sqrt).then_inc(act_gave, 1)
            copy_turned(2)
            for g, (t0, nt) in enumerate(GROUPS):
                act.wait_ge(hid_mm, g + 1)
                if g:
                    act.wait_ge(mm_done, 4 * NG + g)
                for c in range(4):
                    ins = act.activation(rows[:, 0, c * 512:c * 512 + nt * D], ps[:, HID0 + c, 0:nt * D], ACT.Gelu, bias=bf1[:, c:c + 1])
                ins.then_inc(hid_act, 1)
            for n in (4, 5):
                asked(n)
                act.activation(col(2), col(1), ACT.Sqrt).then_inc(act_gave, 1)
            copy_turned(3)
            asked(6)
            act.activation(A[:, :], A[:, :], ACT.Gelu_apprx_tanh).then_inc(act_gave, 1)
            asked(7)
            act.activation(col(2), col(1), ACT.Sqrt).then_inc(act_gave, 1)
            with act.Fori(0, LAYERS) as l:
                asked(8 + l * 3)
                act.activation(col(2), col(1), ACT.Sqrt).then_inc(act_gave, 1)
                copy_turned(4 + l * 2)
                with act.Fori(0, TURNS) as i:
                    for b in range(2):
                        k = first_step(1) + l * STEPS + i * 2 + b
                        step_turned(k, b)
                        for h in range(2):
                            after(act, "z_mm", k, h)
                            act.activation(chan[:, h, :], ps[:, MM0 + h, :], ACT.Copy, scale=0.2).then_inc(s["z_copied"], 1)
                        exps(k)
                asked(9 + l * 3)
                act.activation(A[:, :], A[:, :], ACT.Gelu_apprx_tanh).then_inc(act_gave, 1)
                copy_turned(5 + l * 2)
                for g, (t0, nt) in enumerate(GROUPS):
                    act.wait_ge(hid_mm, NG + l * NG + g + 1)
                    act.activation(C[0:64, t0 * D:(t0 + nt) * D], ps[0:64, HID0 + g % 2, 0:nt * D], ACT.Gelu_apprx_tanh,
                                   bias=g1b[:, 0:1]).then_inc(hid_act, 1)
                asked(10 + l * 3)
                act.activation(B[:, :], B[:, :], ACT.Sigmoid).then_inc(act_gave, 1)
            n0 = 8 + 3 * LAYERS
            for n in (n0, n0 + 1):
                asked(n)
                act.activation(col(2), col(1), ACT.Sqrt).then_inc(act_gave, 1)
            for n in range(3):
                t = 4 + 2 * LAYERS
                if n < 2:
                    for g, (t0, nt) in enumerate(GROUPS):
                        act.wait_ge(tr_done, (t + 2 * n) * NG + g + 1)
                        act.copy(T[:, t0 * D:(t0 + nt) * D], ps[:, TR0 + g % 2, 0:nt * D]).then_inc(tr_copied, 1)
                    for g, (t0, nt) in enumerate(GROUPS):
                        act.wait_ge(tr_done, (t + 2 * n + 1) * NG + g + 1)
                        act.copy(C[:, t0 * D:(t0 + nt) * D], ps[:, TR0 + g % 2, 0:nt * D]).then_inc(tr_copied, 1)
                else:
                    copy_turned(t + 4)
                if n:
                    asked(n0 + 1 + n)
                    act.activation(col(2), col(1), ACT.Sqrt).then_inc(act_gave, 1)

        @block.tensor
        def _(pe):
            start_up(pe, "pe")
            pe.wait_ge(loaded, 16 * len(const_loads + pre_loads + row_loads))

            def turn(n, buf):
                pe.wait_ge(src_ready, n + 1)
                for g, (t0, nt) in enumerate(GROUPS):
                    if g >= 2:
                        pe.wait_ge(tr_copied, n * NG + g - 1)
                    elif g == 0 and not (isinstance(n, int) and n == 0):
                        pe.wait_ge(tr_copied, n * NG)
                    for t in range(nt):
                        ins = pe.transpose(ps[:, TR0 + g % 2, t * D:(t + 1) * D], buf[:, (t0 + t) * D:(t0 + t + 1) * D], ident[:, :])
                    ins.then_inc(tr_done, 1)

            def product(n, pairs, turned, first_turned=None):
                for g, (t0, nt) in enumerate(GROUPS):
                    pe.wait_ge(tr_copied, turned * NG + g + 1)
                    if g >= 2:
                        pe.wait_ge(mm_copied, n * NG + g - 1)
                    elif g == 0 and not (isinstance(n, int) and n == 0):
                        pe.wait_ge(mm_copied, n * NG)
                    for t in range(nt):
                        for i, (buf, w) in enumerate(pairs):
                            ins = pe.matmul(ps[:, MM0 + g % 2, t * D:(t + 1) * D], buf[:, (t0 + t) * D:(t0 + t + 1) * D], w[:, :],
                                            start=i == 0, stop=i == len(pairs) - 1)
                    ins.then_inc(mm_done, 1)

            def onehots_turned(k, b):
                after(pe, "oh_ready", k)
                for q in range(4):
                    if q < 2:
                        after(pe, "oht_ready", k - 1, q + 2)
                    else:
                        after(pe, "oht_ready", k, q - 2)
                    for r in range(4):
                        j, w = q * 2 + r // 2, r % 2
                        ins = pe.transpose(ps[:, OHT0 + q % 2, r * P:(r + 1) * P], onehot[:, b, j, w * P:(w + 1) * P], ident[:, :])
                    ins.then_inc(s["oht_mm"], 1)

            def spread(bank, b, h, c0, begins=False):
                for w in range(2):
                    ins = pe.matmul(ps[:, bank, :], win[:, b, w, c0:c0 + D], onehot_t[:, w, h * HALF:(h + 1) * HALF],
                                    start=begins and w == 0, stop=not begins and w == 1, skip_group_check=not begins)
                return ins

            def add_rows(bank, b, h, width, c0):
                for r in range(4):
                    j = h * 4 + r
                    ins = pe.matmul(ps[:, bank, r * P:(r + 1) * P], rows[:, b, j * width + c0:j * width + c0 + D], ident[:, :],
                                    start=r == 0, stop=False, skip_group_check=True)

            def softmax_turns(k):
                after(pe, "ab_ready", k)
                pe.nop(nofuse=True)
                pe.transpose(ps[0:40, SM, 64:192], ab[:, :], ident[:, :]).then_inc(s["ab_mm"], 1)
                after(pe, "scan_ready", k)
                pe.nop(nofuse=True)
                pe.transpose(ps[:, SM, 192:232], scans[0:40, 1:129], ident[0:40, 0:40]).then_inc(s["back_mm"], 1)

            def aggregate(k, b, width, src, ready):
                ready()
                for w in range(2):
                    for j in reversed(range(EPP)):
                        n = width if j == 0 else min(width, RC)
                        ins = pe.matmul(ps[:, AGG + w, 0:n], onehot[:, b, j, w * P:(w + 1) * P], src(j, n),
                                        start=j == EPP - 1, stop=j == 0, skip_group_check=True)
                ins.then_inc(s["agg_mm"], 1)

            pe.wait_ge(pre_asked, 2)
            for g in range(2):
                ins = pe.transpose(ps[0:NCH, SM, g * P:(g + 1) * P], g_all[:, g, :], ident[:, :])
            pe.transpose(ps[0:1, SM, 256:384], cm[:, 3:4], ident[:, :]).then_inc(pre_tr, 1)
            pe.wait_ge(pre_asked, 3)
            pe.matmul(ps[:, SM, 400:401], one_col[0:1, 0:1].broadcast_to([1, P]), cm[0:1, 3:4], start=True, stop=True).then_inc(pre_tr, 1)

            turn(0, X)
            for n, w in enumerate(("Wq", "Wk", "Wv")):
                product(n, [(T, W[w])], 0)

            with pe.Fori(0, TURNS) as i:
                for b in range(2):
                    k = first_step(0) + i * 2 + b
                    onehots_turned(k, b)
                    after(pe, "types_ready", k)
                    for h in range(2):
                        e = slice(h * HALF, (h + 1) * HALF)
                        after(pe, "oht_ready", k, 2 + h)
                        pe.nop(nofuse=True)
                        pe.matmul(ps[0:64, OHT0 + h, :], wd1t[:, :], attr[:, b, e], start=True, stop=True).then_inc(s["dech_mm"], 1)
                    hold(pe, gathered[b], (i + 1) * 16 * EPP)
                    for h in range(2):
                        e = slice(h * HALF, (h + 1) * HALF)
                        after(pe, "z_used", k - 1 + h, 1 - h)
                        spread(MM0, b, h, 0, True)
                        pe.matmul(ps[:, MM0, :], relq[:, :], attr[:, b, e], start=False, stop=True)
                        add_rows(MM0 + 1, b, h, 3 * D, 0)
                        pe.matmul(ps[:, MM0 + 1, :], wk34[:, :], attr[:, b, e], start=False, stop=True, skip_group_check=True)
                        add_rows(MM0 + 2, b, h, 3 * D, 2 * D)
                        spread(MM0 + 2, b, h, D).then_inc(s["z_mm"], 1)
                        after(pe, "z_used", k, h)
                        if h == 0:
                            after(pe, "dech_ready", k)
                        for r in range(4):
                            j = h * 4 + r
                            t = slice(r * P, (r + 1) * P)
                            pe.matmul(ps[:, SM, j:S64:EPP], prod[:, h, t], blk4[:, :], start=True, stop=True)
                            pe.matmul(ps[:, SM, 320 + j:321 + j], sq[:, t], misc[:, 2:3], start=True, stop=True)
                            ins = pe.matmul(ps[:, SM, 256 + j:256 + S64:EPP], dec_h[0:65, h, t], wd2[:, :], start=True, stop=True)
                    ins.then_inc(s["logit_mm"], 1)
                    softmax_turns(k)
                    aggregate(k, b, AW, lambda j, n: weighted[:, j, 0:n], lambda: after(pe, "weighted_ready", k))

            turn(1, A)
            product(3, [(T, W["Wo"])], 1)
            turn(2, H)
            for g, (t0, nt) in enumerate(GROUPS):
                pe.wait_ge(tr_copied, 2 * NG + g + 1)
                if g:
                    pe.wait_ge(hid_act, g)
                for c in range(4):
                    ins = pe.matmul(ps[:, HID0 + c, 0:nt * D], Wf1[:, c:4 * D:4], T[:, t0 * D:(t0 + nt) * D], start=True, stop=True)
                ins.then_inc(hid_mm, 1)
                pe.wait_ge(hid_act, g + 1)
                pe.wait_ge(mm_copied, 4 * NG + max(g - 1, 0))
                for t in range(nt):
                    for c in range(4):
                        ins = pe.matmul(ps[:, MM0 + g % 2, t * D:(t + 1) * D], rows[:, 0, c * 512 + t * D:c * 512 + (t + 1) * D],
                                        Wf2[:, c, :], start=c == 0, stop=c == 3)
                ins.then_inc(mm_done, 1)

            turn(3, X)
            product(5, [(T, W["Win"])], 3)
            with pe.Fori(0, LAYERS) as l:
                pe.wait_ge(layer_in, (l + 1) * 16 * 13)
                turn(4 + l * 2, A)
                product(6 + l * 3, [(T, W["Wl"])], 4 + l * 2)
                product(7 + l * 3, [(T, W["Wr"])], 4 + l * 2)
                with pe.Fori(0, TURNS) as i:
                    for b in range(2):
                        k = first_step(1) + l * STEPS + i * 2 + b
                        onehots_turned(k, b)
                        hold(pe, gathered[b], (TURNS + l * TURNS + i + 1) * 16 * EPP)
                        for h in range(2):
                            e = slice(h * HALF, (h + 1) * HALF)
                            if h == 0:
                                after(pe, "oht_ready", k, 3)
                                after(pe, "z_used", k - 1)
                            add_rows(MM0 + h, b, h, D, 0)
                            pe.matmul(ps[:, MM0 + h, :], We[:, :], attr[:, b, e], start=False, stop=False, skip_group_check=True)
                            spread(MM0 + h, b, h, 0).then_inc(s["z_mm"], 1)
                        for h in range(2):
                            after(pe, "z_used", k, h)
                            for r in range(4):
                                j = h * 4 + r
                                ins = pe.matmul(ps[:, SM, j:S64:EPP], prod[:, h, r * P:(r + 1) * P], attb[:, :], start=True, stop=True)
                        ins.then_inc(s["logit_mm"], 1)
                        softmax_turns(k)
                        aggregate(k, b, AW, lambda j, n: weighted[:, j, 0:n], lambda: after(pe, "weighted_ready", k))
                turn(5 + l * 2, A)
                for g, (t0, nt) in enumerate(GROUPS):
                    pe.wait_ge(tr_copied, (5 + l * 2) * NG + g + 1)
                    if g >= 2:
                        pe.wait_ge(hid_act, NG + l * NG + g - 1)
                    pe.matmul(ps[0:64, HID0 + g % 2, 0:nt * D], g1w[:, :], T[:, t0 * D:(t0 + nt) * D], start=True, stop=True).then_inc(hid_mm, 1)
                for g, (t0, nt) in enumerate(GROUPS):
                    pe.wait_ge(hid_act, NG + l * NG + g + 1)
                    pe.wait_ge(mm_copied, (8 + l * 3) * NG + max(g - 1, 0))
                    for t in range(nt):
                        ins = pe.matmul(ps[:, MM0 + g % 2, t * D:(t + 1) * D], C[0:64, (t0 + t) * D:(t0 + t + 1) * D], g2w[:, :], start=True, stop=True)
                    ins.then_inc(mm_done, 1)

            for n in range(3):
                with pe.Fori(0, TURNS) as i:
                    for b in range(2):
                        k = first_step(1 + LAYERS + n) + i * 2 + b

                        def ready():
                            hold(pe, gathered[b], (TURNS * (1 + LAYERS + n) + i + 1) * 16 * EPP)
                            after(pe, "oh_ready", k)
                            after(pe, "acc_done", k - 1)
                        aggregate(k, b, D + 1, lambda j, m: rows[:, b, j * SUMW:j * SUMW + D + 1], ready)
                t, m = 4 + 2 * LAYERS, 6 + 3 * LAYERS
                if n < 2:
                    turn(t + 2 * n, A)
                    turn(t + 2 * n + 1, (X, B)[n])
                    product(m + n, [(T, W[f"L2_Wl{n + 1}"]), (C, W[f"L2_Wr{n + 1}"])], t + 2 * n + 1)
                else:
                    turn(t + 4, A)
                    product(m + 2, [(T, W["L3_W"])], t + 4)

        @block.vector
        def _(dve):
            start_up(dve, "dve")
            v = nc.vector
            col = lambda i: cols[:, i, :]
            onto = lambda ap: ap.unsqueeze(2).broadcast_to([P, NT, D])
            along = lambda t: t[:, :].unsqueeze(1).broadcast_to([P, NT, D])
            asks = [0]

            def ask(n):
                dve.drain().then_inc(ask_act, 1)
                dve.wait_ge(act_gave, n + 1)

            def norm(dst, src, n, gain=None, shift=None):
                dve.drain()
                v.tensor_reduce(col(0), nodes(src), AX, ALU.add)
                dve.drain()
                v.tensor_scalar(col(0), col(0), -1.0 / D, None, ALU.mult)
                dve.drain()
                v.tensor_tensor(nodes(dst), nodes(src), onto(col(0)), ALU.add)
                dve.drain()
                v.tensor_tensor(T[:, :], dst[:, :], dst[:, :], ALU.mult)
                dve.drain()
                v.tensor_reduce(col(1), nodes(T), AX, ALU.add)
                dve.drain()
                v.tensor_scalar(col(1), col(1), 1.0 / D, 1e-5, ALU.mult, ALU.add)
                ask(n)
                v.reciprocal(col(2), col(2))
                dve.drain()
                v.tensor_tensor(nodes(dst), nodes(dst), onto(col(2)), ALU.mult)
                if gain is not None:
                    dve.drain()
                    v.tensor_tensor(nodes(dst), nodes(dst), along(gain), ALU.mult)
                    dve.drain()
                    v.tensor_tensor(nodes(dst), nodes(dst), along(shift), ALU.add)
                dve.drain()

            def give(what, _n=None):
                dve.drain().then_inc(what, 1)

            def evacuate(n, dst, plus):
                for g, (t0, nt) in enumerate(GROUPS):
                    dve.wait_ge(mm_done, n * NG + g + 1)
                    o = nodes(dst)[:, t0:t0 + nt, :]
                    i = ps[:, MM0 + g % 2, 0:nt * D].rearrange("p (t d) -> p t d", d=D)
                    if plus is None:
                        v.tensor_copy(o, i).then_inc(mm_copied, 1)
                    else:
                        v.tensor_tensor(o, i, plus(t0, nt), ALU.add).then_inc(mm_copied, 1)
                dve.drain()

            bias = lambda t: (lambda t0, nt: t[:, :].unsqueeze(1).broadcast_to([P, nt, D]))
            of = lambda buf: (lambda t0, nt: nodes(buf)[:, t0:t0 + nt, :])

            v.memset(wd1t[:, :], 0.0)
            v.memset(relq[:, :], 0.0)
            v.memset(wk34[:, :], 0.0)
            v.memset(We[:, :], 0.0)
            v.memset(attr[:, :, :], 0.0)
            v.memset(ab[:, :], 0.0)
            v.memset(scans[:, :], NEG)
            v.memset(one_col[:, :], 1.0)
            v.memset(weighted[:, :, :], 0.0)
            give(pre_asked)
            dve.wait_ge(loaded, 16 * len(const_loads + pre_loads + row_loads))
            v.tensor_copy(dst_f, dst_i)
            v.tensor_copy(types_all.bitcast(F32), types_all)
            v.tensor_copy(ends[:, 0:2, 0:NCH], ends_i)
            v.memset(g_out, 0.0)
            dve.drain()
            v.tensor_tensor(same, dst_f[:, :, 1:EPP + 2], dst_f[:, :, 0:EPP + 1], ALU.is_equal)
            v.tensor_copy(pk_all[:, :, 0:EPP], dst_f[:, :, 1:EPP + 1])
            ones = lambda ap, n: ap.broadcast_to([P, NCH, n])
            v.tensor_tensor(pk_all[:, :, 3 * EPP:4 * EPP], dst_f[:, :, 1:EPP + 1], ones(dst_f[:, :, 0:1], EPP), ALU.is_equal)
            v.tensor_tensor(pk_all[:, :, 4 * EPP:5 * EPP], dst_f[:, :, 1:EPP + 1], ones(dst_f[:, :, EPP + 1:EPP + 2], EPP), ALU.is_equal)
            v.tensor_tensor(g_all[:, 0, :], dst_f[:, :, EPP], dst_f[:, :, 0], ALU.is_equal)
            v.tensor_tensor(g_all[:, 1, :], dst_f[:, :, 1], dst_f[:, :, EPP + 1], ALU.is_equal)
            dve.drain()
            pen = lambda o, i: v.tensor_scalar(o, i, -1.0, -NEG, ALU.add, ALU.mult)
            pen(pk_all[:, :, EPP:2 * EPP], same[:, :, 0:EPP])
            pen(pk_all[:, :, 2 * EPP:3 * EPP], same[:, :, 1:EPP + 1])
            pen(pk_all[:, :, 3 * EPP:5 * EPP], pk_all[:, :, 3 * EPP:5 * EPP])
            pen(g_all, g_all)
            dve.drain()
            v.memset(pk_all[:, :, EPP:EPP + 1], NEG)
            v.memset(pk_all[:, :, 3 * EPP - 1:3 * EPP], NEG)
            E_ = lambda i: ends[:, i, 0:NCH]
            Ei = lambda i: ends[:, i, 0:NCH].bitcast(I32)
            v.tensor_scalar(ends_i, ends_i, 7, None, ALU.arith_shift_right)
            dve.drain()
            v.tensor_copy(ends[:, 2:4, 0:NCH], ends_i)
            dve.drain()
            v.tensor_tensor(E_(4), E_(3), E_(2), ALU.subtract)
            dve.drain()
            v.tensor_copy(Ei(5), E_(4))
            dve.drain()
            v.tensor_scalar(Ei(5), Ei(5), 1, None, ALU.arith_shift_right)
            dve.drain()
            v.tensor_copy(E_(6), Ei(5))
            dve.drain()
            v.tensor_scalar(E_(6), E_(6), 1.0, None, ALU.add)
            v.memset(E_(7), 1.0)
            dve.drain()
            v.tensor_tensor_scan(E_(8), E_(7), E_(6), 0.0, ALU.mult, ALU.add)
            dve.drain()
            v.tensor_tensor(E_(9), E_(8), E_(6), ALU.subtract)
            dve.drain()
            v.tensor_scalar(E_(10), E_(9), misc[:, 0:1], None, ALU.is_le)
            v.tensor_scalar(E_(11), E_(9), -2.0, None, ALU.mult)
            dve.drain()
            v.tensor_tensor(E_(11), E_(11), E_(2), ALU.add)
            v.tensor_copy(E_(12), E_(10))
            dve.drain()
            v.tensor_tensor(ends[:, 12, 0:NCH - 1], ends[:, 10, 0:NCH - 1], ends[:, 10, 1:NCH], ALU.subtract)
            v.tensor_reduce(ends[:, 14, 0:1], E_(10), AX, ALU.add)
            dve.drain()
            v.tensor_tensor(E_(13), E_(12), E_(11), ALU.mult)
            v.tensor_scalar(ends[:, 14, 0:1], ends[:, 14, 0:1], -1.0, None, ALU.add)
            dve.drain()
            v.tensor_reduce(ends[:, 14, 1:2], E_(13), AX, ALU.add)
            dve.drain()
            v.scalar_tensor_tensor(ends[:, 14, 2:3], misc[:, 0:1], 2.0, ends[:, 14, 1:2], ALU.mult, ALU.add)
            dve.drain()
            v.tensor_scalar(ends[:, 15, 2:3], ends[:, 14, 2:3], float(P), None, ALU.mult)
            v.tensor_scalar(ends[:, 14, 1:2], ends[:, 14, 2:3], float(LAST_WIN), None, ALU.min)
            dve.drain()
            v.tensor_copy(ends[:, 15, 0:2].bitcast(I32), ends[:, 14, 0:2])
            v.tensor_reduce(cm[:, 3:4], types_all.bitcast(F32), AX, ALU.max)
            v.tensor_tensor(wk34[32:34, :], wk34[32:34, :], bt34[32:34, :], ALU.add)
            v.tensor_scalar(blk4[:, :], blk[:, :], float(DH) ** -0.5, None, ALU.mult)
            v.tensor_scalar(cm[:, 4:5], cm[:, 0:1], -1.0, None, ALU.mult)
            dve.drain()
            v.tensor_tensor(cm[:, 1:2], cm[:, 0:1], cm[:, 4:5], ALU.max)
            dve.drain()
            v.tensor_scalar(cm[:, 5:6], cm[:, 1:2], 0.0, None, ALU.is_gt)
            v.tensor_scalar(cm[:, 6:7], cm[:, 1:2], 0.0, None, ALU.is_le)
            dve.drain()
            v.tensor_scalar(cm[:, 1:2], cm[:, 1:2], 1e-15, None, ALU.max)
            give(pre_asked)
            dve.wait_ge(pre_tr, 1)
            v.tensor_copy(g_out[0:NCH], ps[0:NCH, SM, 0:2 * P].rearrange("p (g c) -> p g c", g=2))
            v.tensor_reduce(cm[0:1, 3:4], ps[0:1, SM, 256:384], AX, ALU.max)
            give(pre_asked)
            dve.wait_ge(pre_tr, 2)
            v.tensor_scalar(cm[:, 7:8], ps[:, SM, 400:401], 1.0, 1.0, ALU.add, ALU.max)
            dve.drain()
            v.reciprocal(cm[:, 7:8], cm[:, 7:8])
            dve.wait_ge(steps_in, 16)
            dve.drain()
            v.tensor_scalar(wd1t[32:34, :], wd1t[32:34, :], cm[32:34, 7:8], None, ALU.mult)
            dve.drain()
            v.tensor_tensor(wd1t[32:34, :], wd1t[32:34, :], bd1r[32:34, :], ALU.add)
            v.tensor_tensor(B[:, :], X[:, :], X[:, :], ALU.mult)
            dve.drain().then_inc(src_ready, 1)
            v.tensor_reduce(col(0), nodes(B), AX, ALU.add)
            ask(0)
            v.tensor_scalar(col(1), col(1), 1e-15, None, ALU.max)
            v.tensor_scalar(hp[:, 5, :], hp[:, 3, :], -1.0, 1.0, ALU.mult, ALU.add)
            dve.drain()
            v.tensor_tensor(hp[:, 4, :], hp[:, 5, :], hp[:, 1, :], ALU.mult)
            v.tensor_scalar(col(3), col(1), cm[:, 2:3], None, ALU.mult)
            dve.drain()
            v.tensor_scalar(col(10), col(3), 1.0 / PI, None, ALU.mult)
            dve.drain()
            v.tensor_copy(col(14).bitcast(I32), col(10))
            dve.drain()
            v.tensor_copy(col(11), col(14).bitcast(I32))
            dve.drain()
            v.scalar_tensor_tensor(col(4), col(11), -PI, col(3), ALU.mult, ALU.add)
            dve.drain()
            v.tensor_scalar(col(4), col(4), 3.1415925, -3.1415925, ALU.min, ALU.max)
            dve.drain()
            v.scalar_tensor_tensor(col(6), col(4), -1.0, col(4), ALU.mult, ALU.max)
            dve.drain()
            v.tensor_scalar(col(5), col(6), -1.0, PI / 2, ALU.mult, ALU.add)
            ask(1)
            v.tensor_scalar(col(7), col(7), cm[:, 5:6], None, ALU.mult)
            v.tensor_scalar(col(8), col(8), cm[:, 6:7], None, ALU.mult)
            v.tensor_scalar(col(9), col(9), cm[:, 6:7], cm[:, 5:6], ALU.mult, ALU.add)
            dve.drain()
            v.tensor_tensor(col(7), col(7), col(8), ALU.add)
            v.tensor_tensor(col(9), col(9), col(3), ALU.mult)
            dve.drain()
            v.reciprocal(col(9), col(9))
            dve.drain()
            v.tensor_tensor(col(7), col(7), col(9), ALU.mult)
            dve.drain()
            v.tensor_tensor(nodes(C), nodes(X), onto(col(7)), ALU.mult)
            dve.drain()
            v.tensor_tensor(B[:, :], C[:, :], C[:, :], ALU.mult)
            dve.drain()
            v.tensor_reduce(col(12), nodes(B), AX, ALU.add)
            v.reciprocal(cm[:, 2:3], cm[:, 2:3])
            dve.drain()
            v.tensor_scalar(cm[:, 2:3], cm[:, 2:3], 1.0 - 1e-5, None, ALU.mult)
            ask(2)
            v.tensor_scalar(col(15), col(13), cm[:, 2:3], None, ALU.is_gt)
            v.tensor_scalar(col(16), col(13), cm[:, 2:3], None, ALU.max)
            dve.drain()
            v.reciprocal(col(16), col(16))
            dve.drain()
            v.tensor_scalar(col(16), col(16), cm[:, 2:3], -1.0, ALU.mult, ALU.add)
            dve.drain()
            v.tensor_tensor(col(16), col(16), col(15), ALU.mult)
            dve.drain()
            v.tensor_scalar(col(16), col(16), 1.0, None, ALU.add)
            dve.drain()
            v.tensor_tensor(nodes(C), nodes(C), onto(col(16)), ALU.mult)
            evacuate(0, H, None)
            evacuate(1, A, None)
            evacuate(2, B, None)
            v.tensor_scalar(T[:, :], C[:, :], -1.0, None, ALU.mult)
            give(store_ask)

            def onehots(kind, k, uses, b):
                dve.wait_ge(in_ready[kind][b], (uses + 1) * 16 * LOADS[kind])
                v.tensor_scalar(rel[:, :], pk[:, b, 0:EPP], wbase[:, b:b + 1], None, ALU.subtract)
                dve.drain()
                for j in range(EPP):
                    ins = v.tensor_scalar(onehot[:, b, j, :], iota[:, :], rel[:, j:j + 1], None, ALU.is_equal)
                ins.then_inc(s["oh_ready"], 1)

            heads_first = lambda t: t.rearrange("p (h j) -> p h j", j=EPP)
            per_edge = lambda ap: ap.unsqueeze(1).broadcast_to([P, HEADS, EPP])
            per_head = lambda ap: ap.unsqueeze(2).broadcast_to([P, HEADS, EPP])

            def softmax(k, b):
                q = {n: t[:, :] for n, t in small.items()}
                v.tensor_copy(heads_first(q["pen_f"]), per_edge(pk[:, b, EPP:2 * EPP]))
                v.tensor_copy(heads_first(q["pen_r"]), per_edge(pk[:, b, 2 * EPP:3 * EPP]))
                v.tensor_copy(scans[0:HEADS, 1:2], scans[0:HEADS, 129:130])
                dve.drain()
                v.tensor_tensor_scan(q["run_f"], q["pen_f"], q["logit"], NEG, ALU.add, ALU.max)
                dve.drain()
                v.tensor_tensor_scan(q["run_r"][:, ::-1], q["pen_r"][:, ::-1], q["run_f"][:, ::-1], NEG, ALU.add, ALU.max)
                dve.drain()
                v.tensor_copy(ab[:, 0:HEADS], heads_first(q["run_f"])[:, :, EPP - 1])
                v.tensor_copy(ab[:, 32:32 + HEADS], heads_first(q["run_r"])[:, :, 0])
                give(s["ab_ready"])
                after(dve, "ab_mm", k)
                v.tensor_tensor_scan(scans[0:HEADS, 2:130], gp[0:HEADS, b, :], ps[0:HEADS, SM, 64:192],
                                     scans[0:HEADS, 1:2], ALU.add, ALU.max)
                v.tensor_tensor_scan(scans[32:32 + HEADS, 127::-1], gp[32:32 + HEADS, b, ::-1], ps[32:32 + HEADS, SM, 191:63:-1],
                                     NEG, ALU.add, ALU.max)
                give(s["scan_ready"])
                after(dve, "back_mm", k)
                before, behind = ps[:, SM, 192:192 + HEADS], ps[:, SM, 224:224 + HEADS]
                v.tensor_tensor(heads_first(q["m1"]), per_head(before), per_edge(pk[:, b, 3 * EPP:4 * EPP]), ALU.add)
                v.tensor_tensor(heads_first(q["m2"]), per_head(behind), per_edge(pk[:, b, 4 * EPP:5 * EPP]), ALU.add)
                dve.drain()
                v.tensor_tensor(q["m1"], q["m1"], q["run_r"], ALU.max)
                dve.drain()
                v.tensor_tensor(q["m1"], q["m1"], q["m2"], ALU.max)
                dve.drain()
                v.tensor_tensor(delta[:, 0:S64], q["logit"], q["m1"], ALU.subtract)
                v.tensor_tensor(delta[:, S64:], before, heads_first(q["m1"])[:, :, 0], ALU.subtract)
                dve.drain()
                v.tensor_scalar(delta[:, S64:], delta[:, S64:], 0.0, None, ALU.min)
                give(s["delta_ready"])

            def rows_weighted(k, b, uses, width, c0, typed):
                after(dve, "ex_ready", k)
                dve.wait_ge(gathered[b], (uses + 1) * 16 * EPP)
                by_head = weighted[:, :, 0:RC].rearrange("p j (h c) -> p j h c", c=HW)
                e = ex[:, 0:S64].rearrange("p (h j) -> p j h", j=EPP)
                vals = rows[:, b, 0:EPP * width].rearrange("p (j r) -> p j r", r=width)[:, :, c0:c0 + D].rearrange("p j (h c) -> p j h c", c=DH)
                v.tensor_tensor(by_head[:, :, :, 0:DH], vals, e.unsqueeze(3).broadcast_to([P, EPP, HEADS, DH]), ALU.mult)
                v.tensor_scalar(weighted[:, 0, RC:AW], ex[:, S64:], -1.0, misc[:, 1:2], ALU.add, ALU.mult)
                if typed:
                    v.tensor_tensor(by_head[:, :, :, DH + 1], e, type_f[:, b, :].unsqueeze(2).broadcast_to([P, EPP, HEADS]), ALU.mult)
                    dve.drain()
                    v.tensor_tensor(by_head[:, :, :, DH], e, by_head[:, :, :, DH + 1], ALU.subtract)
                else:
                    v.tensor_copy(by_head[:, :, :, DH], e)
                give(s["weighted_ready"])

            def accumulate(k, r, width, rescaled):
                after(dve, "agg_mm", k)
                w = dve.value_load(steps_i[0:1, bass.ds(r * 2 + 1, 1)], min_val=0, max_val=LAST_WIN)
                own = acc[:, bass.ds(w, 2), :]
                if rescaled:
                    v.tensor_scalar(grow[:, :, :], ps[:, AGG:AGG + 2, RC:AW], 1.0, None, ALU.add)
                    dve.drain()
                    by_head = own[:, :, 0:RC].rearrange("p w (h c) -> p w h c", c=HW)
                    v.tensor_tensor(by_head, by_head, grow[:, :, :].unsqueeze(3).broadcast_to([P, 2, HEADS, HW]), ALU.mult)
                    dve.drain()
                v.tensor_tensor(own[:, :, 0:width], own[:, :, 0:width], ps[:, AGG:AGG + 2, 0:width], ALU.add)
                give(s["acc_done"])

            def clear(kind):
                v.memset(acc[:, :, :], 0.0)
                if kind == "sum":
                    for b in range(2):
                        v.memset(rows[:, b, 0:EPP * SUMW].rearrange("p (j r) -> p j r", r=SUMW)[:, :, D:], 1.0)
                else:
                    v.memset(scans[0:HEADS, 129:130], NEG)
                    v.memset(weighted[:, :, :], 0.0)
                dve.drain()

            dve.wait_ge(stored, 5 * 16)
            v.memset(dec_h[64:65, :, :], 1.0)
            clear("L0")
            with dve.Fori(0, TURNS) as i:
                for b in range(2):
                    k = first_step(0) + i * 2 + b
                    onehots("L0", k, i, b)
                    v.tensor_copy(type_f[:, b, :], type_i[:, b, :])
                    v.tensor_scalar(attr[32:34, b, :], attr[96:98, b, :].bitcast(I32), misc[96:98, 3:4], misc[96:98, 4:5], ALU.mult, ALU.add)
                    give(s["types_ready"])
                    for h in range(2):
                        after(dve, "z_copied", k, h)
                        v.tensor_tensor(prod[:, h, :], ps[:, MM0, :], chan[:, h, :], ALU.mult).then_inc(s["z_used"], 1)
                    after(dve, "logit_mm", k)
                    v.tensor_copy(dist2[:, :], ps[:, SM, 320:320 + EPP])
                    v.tensor_tensor(heads_first(small["m1"][:, :]), heads_first(ps[:, SM, 0:S64]), per_head(hp[:, 3, :]), ALU.mult)
                    give(s["dist_asked"])
                    after(dve, "tanh_ready", k)
                    v.tensor_tensor(heads_first(small["dec2"][:, :]), heads_first(small["dec"][:, :]), per_head(hp[:, 0, :]), ALU.mult)
                    give(s["decs_ready"])
                    after(dve, "dist_ready", k)
                    v.tensor_tensor(heads_first(small["m2"][:, :]), per_head(hp[:, 4, :]), per_edge(dist[:, :]), ALU.mult)
                    dve.drain()
                    v.tensor_tensor(small["m1"][:, :], small["m1"][:, :], small["m2"][:, :], ALU.subtract)
                    dve.drain()
                    v.tensor_tensor(small["logit"][:, :], small["m1"][:, :], small["dec"][:, :], ALU.mult)
                    dve.drain()
                    softmax(k, b)
                    rows_weighted(k, b, i, 3 * D, D, True)
                    accumulate(k, i * 2 + b, RC, True)

            def head_means(dst):
                by_head = acc[:, :, 0:RC].rearrange("p t (h c) -> p t h c", c=HW)
                v.tensor_tensor(den, by_head[:, :, :, DH], by_head[:, :, :, DH + 1], ALU.add)
                dve.drain()
                v.tensor_scalar(den, den, 1e-30, None, ALU.max)
                dve.drain()
                v.reciprocal(den, den)
                dve.drain()
                v.tensor_tensor(dst[:, :].rearrange("p (t h c) -> p t h c", h=HEADS, c=DH), by_head[:, :, :, 0:DH],
                                den.unsqueeze(3).broadcast_to([P, NT, HEADS, DH]), ALU.mult)
                dve.drain()

            den = cols[:, 20:28, :].rearrange("p h t -> p (h t)").rearrange("p (t h) -> p t h", h=HEADS)
            part = cols[:, 28:36, :].rearrange("p h t -> p (h t)").rearrange("p (t h) -> p t h", h=HEADS)
            head_means(A)
            for t in range(2):
                v.tensor_tensor(part, acc[:, :, 0:RC].rearrange("p t (h c) -> p t h c", c=HW)[:, :, :, DH + t], den, ALU.mult)
                dve.drain()
                v.tensor_tensor(B[:, :].rearrange("p (t h c) -> p t h c", h=HEADS, c=DH),
                                relv[:, t, :].rearrange("p (h c) -> p h c", c=DH).unsqueeze(1).broadcast_to([P, NT, HEADS, DH]),
                                part.unsqueeze(3).broadcast_to([P, NT, HEADS, DH]), ALU.mult)
                dve.drain()
                v.tensor_tensor(A[:, :], A[:, :], B[:, :], ALU.add)
                dve.drain()
            give(src_ready)
            evacuate(3, B, of(X))
            v.tensor_tensor(nodes(B), nodes(B), along(V["bo"]), ALU.add)
            norm(H, B, 3, V["g1"], V["be1"])
            give(src_ready)
            evacuate(4, B, of(H))
            v.tensor_tensor(nodes(B), nodes(B), along(V["bf2"]), ALU.add)
            norm(H, B, 4, V["g2"], V["be2"])
            v.tensor_tensor(B[:, :], X[:, :], H[:, :], ALU.add)
            norm(X, B, 5)
            give(src_ready)
            evacuate(5, A, bias(V["Win_b"]))
            ask(6)
            norm(H, A, 7, V["ln_in_g"], V["ln_in_b"])
            with dve.Fori(0, LAYERS) as l:
                give(layer_used)
                dve.wait_ge(layer_in, (l + 1) * 16 * 13)
                v.tensor_scalar(attb[:, :], blk[:, :], att[:, 0:1], None, ALU.mult)
                norm(A, H, 8 + l * 3, V["ln_g"], V["ln_b"])
                give(src_ready)
                evacuate(6 + l * 3, B, bias(V["Wl_b"]))
                evacuate(7 + l * 3, C, bias(V["Wr_b"]))
                give(store_ask)
                clear("L1")
                with dve.Fori(0, TURNS) as i:
                    for b in range(2):
                        k = first_step(1) + l * STEPS + i * 2 + b
                        onehots("L1", k, l * TURNS + i, b)
                        for h in range(2):
                            after(dve, "z_copied", k, h)
                            v.tensor_tensor(prod[:, h, :], ps[:, MM0 + h, :], chan[:, h, :], ALU.max).then_inc(s["z_used"], 1)
                        after(dve, "logit_mm", k)
                        v.tensor_copy(small["logit"][:, :], ps[:, SM, 0:S64])
                        softmax(k, b)
                        rows_weighted(k, b, TURNS + l * TURNS + i, D, 0, False)
                        accumulate(k, i * 2 + b, RC, True)
                head_means(A)
                v.tensor_tensor(nodes(A), nodes(A), along(V["conv_b"]), ALU.add)
                ask(9 + l * 3)
                dve.sem_inc(src_ready, 1)
                evacuate(8 + l * 3, B, bias(V["g2_b"]))
                ask(10 + l * 3)
                v.tensor_tensor(B[:, :], B[:, :], A[:, :], ALU.mult)
                dve.drain()
                v.tensor_tensor(H[:, :], H[:, :], B[:, :], ALU.add)
                dve.drain()
            n0 = 8 + 3 * LAYERS
            norm(A, H, n0, V["fn_g"], V["fn_b"])
            v.tensor_tensor(B[:, :], X[:, :], A[:, :], ALU.add)
            norm(X, B, n0 + 1)
            for n in range(3):
                clear("sum")
                give(store_ask)
                with dve.Fori(0, TURNS) as i:
                    for b in range(2):
                        k = first_step(1 + LAYERS + n) + i * 2 + b
                        onehots("sum", k, n * TURNS + i, b)
                        accumulate(k, i * 2 + b, D + 1, False)
                v.tensor_scalar(col(3), acc[:, :, D], 1.0, None, ALU.max)
                dve.drain()
                v.reciprocal(col(3), col(3))
                dve.drain()
                v.tensor_tensor(nodes(A), acc[:, :, 0:D], onto(col(3)), ALU.mult)
                if n == 2:
                    dve.drain()
                    v.tensor_tensor(A[:, :], A[:, :], X[:, :], ALU.add)
                give(src_ready)
                m = 6 + 3 * LAYERS + n
                if n < 2:
                    dve.sem_inc(src_ready, 1)
                evacuate(m, B, bias(V[("L2_bl1", "L2_bl2", "L3_b")[n]]))
                if n == 2:
                    v.tensor_scalar(B[:, :], B[:, :], 0.0, None, ALU.max)
                    dve.drain()
                if n:
                    v.tensor_tensor(B[:, :], B[:, :], X[:, :], ALU.add)
                    norm(X, B, n0 + 1 + n)
            give(store_ask)


NAMES = ["x", "src_edges", "type_edges", "dst_win", "dst_ends", "type_rows", "weight_rows", "time_edges", "attr_edges",
         "c_ident", "c_iota", "c_blk", "c_misc",
         "L0_gnn_Wq", "L0_gnn_Wk", "L0_gnn_Wv", "L0_gnn_rel_q", "L0_gnn_rel_k", "L0_gnn_rel_v", "L0_gnn_Wt", "L0_gnn_bt",
         "L0_gnn_Wd1", "L0_gnn_bd1", "L0_gnn_Wd2", "L0_gnn_bd2", "L0_gnn_decay_scale", "L0_gnn_c_mag", "L0_gnn_hyp_beta",
         "L0_gnn_logit_alpha", "L0_gnn_Wo", "L0_gnn_bo", "L0_gnn_g1", "L0_gnn_be1", "L0_gnn_g2", "L0_gnn_be2",
         "L0_gnn_Wf1", "L0_gnn_bf1", "L0_gnn_Wf2", "L0_gnn_bf2",
         "L1_gnn_Win_w", "L1_gnn_Win_b", "L1_gnn_ln_in_g", "L1_gnn_ln_in_b", "L1_gnn_ln_g", "L1_gnn_ln_b", "L1_gnn_Wl_w",
         "L1_gnn_Wl_b", "L1_gnn_Wr_w", "L1_gnn_Wr_b", "L1_gnn_We_w", "L1_gnn_att", "L1_gnn_conv_b", "L1_gnn_g1_w",
         "L1_gnn_g1_b", "L1_gnn_g2_w", "L1_gnn_g2_b", "L1_gnn_fn_g", "L1_gnn_fn_b",
         "L2_gnn_Wl1_T", "L2_gnn_bl1", "L2_gnn_Wr1_T", "L2_gnn_Wl2_T", "L2_gnn_bl2", "L2_gnn_Wr2_T", "L3_gnn_W_T", "L3_gnn_b"]


def lay_out(inputs):
    import numpy as np

    a = {k: np.asarray(v) for k, v in inputs.items()}
    extra = NCH * CHUNK - E

    def padded(v, fill=0):
        return np.concatenate([v, np.full((extra,) + v.shape[1:], fill, v.dtype)])

    def by_partition(v):
        return np.ascontiguousarray(padded(v).reshape(NCH, P, EPP))

    def by_tile(v):
        w = padded(v).reshape(NCH, P, EPP, v.shape[1])
        return np.ascontiguousarray(w.transpose(0, 3, 2, 1)).reshape(NCH, v.shape[1], CHUNK)

    o = dict(a)
    o["x"] = np.concatenate([a["x"], np.zeros((NP - N, D), a["x"].dtype)])
    o["src_edges"] = by_partition(a["src"])
    dst = padded(a["dst"], N)
    around = np.concatenate([np.full(1, -1, dst.dtype), dst, np.full(1, -1, dst.dtype)])
    windows = [around[k:k + NCH * CHUNK:EPP].reshape(NCH, P) for k in range(EPP + 2)]
    o["dst_win"] = np.ascontiguousarray(np.stack(windows, axis=-1).transpose(1, 0, 2))
    o["dst_ends"] = np.ascontiguousarray(dst.reshape(NCH, CHUNK)[:, [0, CHUNK - 1]].T)
    o["type_edges"] = by_partition(a["edge_type_2"])
    o["type_rows"] = by_tile(a["edge_type_2"][:, None])[:, 0]
    o["weight_rows"] = by_tile(a["edge_weight"][:, None])[:, 0]
    o["time_edges"] = by_tile(a["edge_attr_32"])
    o["attr_edges"] = by_tile(a["edge_attr_3"])
    o["L1_gnn_att"] = a["L1_gnn_att"].reshape(LAYERS, D, 1)
    o["L1_gnn_g1_b"] = a["L1_gnn_g1_b"].reshape(LAYERS, 64, 1)
    o["L0_gnn_c_mag"] = a["L0_gnn_c_mag"].reshape(1)
    for n in ("Wl1", "Wr1", "Wl2", "Wr2"):
        o[f"L2_gnn_{n}_T"] = np.ascontiguousarray(a["L2_gnn_" + n].T)
    o["L3_gnn_W_T"] = np.ascontiguousarray(a["L3_gnn_W"].T)
    p = np.arange(P)
    o["c_ident"] = np.eye(P, dtype=np.float32)
    o["c_iota"] = np.ascontiguousarray(np.broadcast_to(np.arange(2 * P, dtype=np.float32), (P, 2 * P)))
    o["c_blk"] = (p[:, None] // DH == np.arange(HEADS)).astype(np.float32)
    misc = np.zeros((P, 8), np.float32)
    misc[:, 0] = p
    misc[0, 1] = 1
    misc[:, 2] = 1
    misc[96:98, 3] = (1, -1)
    misc[96:98, 4] = (0, 1)
    o["c_misc"] = misc
    return {n: o[n] for n in NAMES}


def program(nc, arrays):
    a = {n: nc.dram_tensor("in_" + n, v.shape, mybir.dt.from_np(v.dtype), kind="ExternalInput").ap() for n, v in arrays.items()}
    out = nc.dram_tensor("out_nodes", (N, D), F32, kind="ExternalOutput").ap()
    build(nc, a, out)


def kernel(**inputs):
    import concourse.bacc as bacc
    from concourse.bass_utils import run_bass_kernel_spmd

    arrays = lay_out(inputs)
    nc = bacc.Bacc("TRN2", target_bir_lowering=False, num_devices=1)
    program(nc, arrays)
    r = run_bass_kernel_spmd(nc, [{"in_" + n: v for n, v in arrays.items()}], core_ids=[0])
    return r.results[0]["out_nodes"]
```

```python
from contextlib import ExitStack

import concourse.bass as bass
import concourse.mybir as mybir

F32 = mybir.dt.float32
I32 = mybir.dt.int32
ALU = mybir.AluOpType
ACT = mybir.ActivationFunctionType
AX = mybir.AxisListType.X

P = 128
D = 128
N = 3125
E = 103125
HEADS = 8
DH = D // HEADS
LAYERS = 4
EPP = 8
CHUNK = P * EPP
NCH = -(-E // CHUNK)
LAST_WIN = N // P
NT = LAST_WIN + 2
NP = NT * P
STEPS = NCH + LAST_WIN // 2
RING = 3
STEPS += -STEPS % RING
TURNS = STEPS // RING
ALWAYS = -(-NCH // RING)
HALF = 4 * P
HW = DH + 2
AW = HEADS * HW + HEADS
RC = HEADS * HW
NEG = -1.0e30
PK = 5 * EPP
GROUPS = [(g * 4, min(4, NT - g * 4)) for g in range(-(-NT // 4))]
NG = len(GROUPS)
SUMW = D + 2
LOADS = {"L0": 10, "L1": 7, "sum": 3}
PI = 3.141592653589793

OHT0, TR0, MM0, SM, AGG, HID0 = 0, 0, 2, 5, 6, 4


def build(nc, a, out):
    ctx = ExitStack()
    with ctx:
        def sb(name, shape, dt=F32):
            return ctx.enter_context(nc.sbuf_tensor(name, shape, dt))

        def sem(name):
            return ctx.enter_context(nc.semaphore(name))

        def dram(name, shape, dt=F32):
            return nc.dram_tensor(name, shape, dt, kind="Internal").ap()

        kvm_tab = dram("kvm_tab", (NP, 3 * D))
        qm_tab = dram("qm_tab", (NP, 2 * D))
        xl_tab = dram("xl_tab", (NP, D))
        xr_tab = dram("xr_tab", (NP, D))
        pk_tab = dram("pk_tab", (NCH, P, PK))
        g_tab = dram("g_tab", (2, P, P))
        step_tab = dram("step_tab", (P, 2), I32)
        base_tab = dram("base_tab", (P, 1))

        def node_buf(name):
            return sb(name, [P, NT * D])

        X, H, A, B, C, T = (node_buf(n) for n in ("x_nodes", "h_nodes", "a_nodes", "b_nodes", "c_nodes", "t_chans"))

        def nodes(buf):
            return buf[:, :].rearrange("p (t d) -> p t d", d=D)

        rows = [buf[:, 0:EPP * 3 * D] for buf in (A, B, C)]
        onehot = sb("onehot", [P, RING, EPP, 2 * P])
        onehot_t = sb("onehot_t", [P, 2, EPP * P])
        weighted = sb("weighted", [P, EPP, AW])
        acc = sb("acc", [P, NT, AW])
        src_ids = sb("src_ids", [P, RING, EPP], I32)
        type_i = sb("type_i", [P, RING, EPP], I32)
        type_f = sb("type_f", [P, RING, EPP])
        pk = sb("pk", [P, RING, PK])
        gp = sb("gp", [P, RING, P])
        win = sb("win_rows", [P, RING, 2, 2 * D])
        wbase = sb("wbase", [P, RING])
        rel = sb("rel", [P, RING, EPP])
        attr = sb("attr", [P, RING, CHUNK])
        chan = sb("chan", [P, 2, HALF])
        prod = sb("prod", [P, 2, HALF])
        sq = sb("sq", [P, 2, HALF])
        dec_h = T[:, 0:2 * HALF].rearrange("p (h e) -> p h e", h=2)
        S64 = EPP * HEADS
        small = {n: sb(n, [P, S64]) for n in ("pen_f", "pen_r", "logit", "run_f", "run_r", "m1", "m2", "dec", "dec2")}
        dist2 = sb("dist2", [P, EPP])
        dist = sb("dist", [P, EPP])
        ab = sb("ab", [P, 40])
        scans = sb("scans", [P, 130])
        delta = sb("delta", [P, S64 + HEADS])
        ex = sb("ex", [P, S64 + HEADS])
        grow = sb("grow", [P, 2, HEADS])
        ident = sb("ident", [P, P])
        iota = sb("iota", [P, 2 * P])
        blk = sb("blk", [P, HEADS])
        blk4 = sb("blk4", [P, HEADS])
        misc = sb("misc", [P, 8])
        steps_i = sb("steps_i", [1, 2 * P], I32)
        steps_left = sb("steps_left", [1, 1], I32)
        cols = sb("cols", [P, 36, NT])
        one_col = sb("one_col", [P, 16])

        def mat(name, k=P, n=D):
            return sb(name, [k, n])

        W = {n: mat("w_" + n) for n in ("Wq", "Wk", "Wv", "Wo", "Win", "Wl", "Wr", "L2_Wl1", "L2_Wr1", "L2_Wl2", "L2_Wr2", "L3_W")}
        Wf1 = mat("w_f1", P, 4 * D)
        Wf2 = sb("w_f2", [P, 4, D])
        bf1 = mat("b_f1", P, 4)
        wk34 = mat("w_k34", P, D)
        relq = mat("w_relq", P, D)
        relv = sb("w_relv", [P, 2, D])
        wd1t = mat("w_d1t", P, 64)
        bd1r = mat("b_d1r", 34, 64)
        bt34 = mat("b_t34", 34, D)
        wd2 = mat("w_d2", 65, HEADS)
        hp = sb("head_params", [P, 6, HEADS])
        cm = sb("c_params", [P, 8])
        V = {n: mat("v_" + n) for n in ("bo", "g1", "be1", "g2", "be2", "bf2", "Win_b", "ln_in_g", "ln_in_b",
                                          "ln_g", "ln_b", "Wl_b", "Wr_b", "conv_b", "g2_b", "fn_g", "fn_b",
                                          "L2_bl1", "L2_bl2", "L3_b")}
        We = mat("w_e", P, D)
        att = mat("att_col", P, 1)
        attb = mat("att_blk", P, HEADS)
        g1w = mat("w_g1", P, 64)
        g1b = mat("b_g1", 64, 1)
        g2w = mat("w_g2", 64, D)

        ps = ctx.enter_context(nc.psum_tensor("ps", [P, 8, 512], F32))

        loaded = sem("loaded")
        pre_asked = sem("pre_asked")
        pre_tr = sem("pre_tr")
        pre_done = sem("pre_done")
        steps_in = sem("steps_in")
        layer_in = sem("layer_in")
        layer_used = sem("layer_used")
        src_ready = sem("src_ready")
        tr_done, tr_copied = sem("tr_done"), sem("tr_copied")
        mm_done, mm_copied = sem("mm_done"), sem("mm_copied")
        hid_mm, hid_act = sem("hid_mm"), sem("hid_act")
        ask_act, act_gave = sem("ask_act"), sem("act_gave")
        store_ask, stored = sem("store_ask"), sem("stored")
        in_ready = {n: [[sem(f"in_{n}_{part}{b}") for b in range(RING)] for part in ("main", "more")] for n in ("L0", "L1", "sum")}
        gathered = [[sem(f"gathered_{part}{b}") for b in range(RING)] for part in ("main", "more")]
        PER_STEP = {"oh_ready": 1, "oht_mm": 4, "oht_ready": 4, "z_mm": 2, "z_copied": 2, "z_used": 2, "logit_mm": 1,
                    "ab_ready": 1, "ab_mm": 1, "scan_ready": 1, "back_mm": 1, "delta_ready": 1,
                    "ex_ready": 1, "weighted_ready": 1, "agg_mm": 1, "acc_done": 1, "types_ready": 1, "dech_mm": 2,
                    "dech_ready": 2, "dec_mm": 1, "tanh_ready": 1, "decs_ready": 1, "decay_ready": 1, "dist_asked": 1, "dist_ready": 1}
        s = {n: sem(n) for n in PER_STEP}
        OF = {"sp": (), "act": ("oht_ready", "z_copied", "ex_ready", "dech_ready", "tanh_ready", "decay_ready", "dist_ready"),
              "pe": ("oht_mm", "z_mm", "logit_mm", "ab_mm", "back_mm", "agg_mm", "dech_mm", "dec_mm"),
              "dve": ("oh_ready", "z_used", "ab_ready", "scan_ready", "delta_ready", "weighted_ready", "acc_done",
                      "types_ready", "decs_ready", "dist_asked")}

        def start_up(eng, who):
            for n in OF[who]:
                eng.sem_inc(s[n], RING * PER_STEP[n])

        def after(eng, name, k, part=None):
            n = PER_STEP[name]
            eng.wait_ge(s[name], k * n + (n if part is None else part + 1))

        def hold(eng, which, value):
            eng.wait_ge(which, value)
            eng.nop(nofuse=True)

        def first_step(edge_pass):
            return edge_pass * STEPS + RING

        def later(i, b, n):
            return i + (b + n) // RING, (b + n) % RING

        nothing = lambda i, part: None

        def turns(eng, one, begin=nothing, skip=None):
            def some(first, end, part):
                begin(first, part)
                with eng.Fori(first, end - 1) as i:
                    for b in range(RING):
                        one(i, b, 2, part)
                for b in range(RING):
                    one(end - 1, b, min(2, RING - 1 - b), part)

            some(0, ALWAYS, 0)
            left = eng.value_load(steps_left[0:1, 0:1], min_val=0, max_val=1)
            with eng.If(left > 0):
                some(ALWAYS, TURNS, 1)
            if skip:
                with eng.Else():
                    skip()

        SKIPPED = (TURNS - ALWAYS) * RING
        L0_ONLY = ("dech_ready", "tanh_ready", "decay_ready", "dist_ready", "dech_mm", "dec_mm", "types_ready", "decs_ready", "dist_asked")

        def skip_steps(eng, who, kind):
            def skip():
                eng.drain()
                for n in OF[who]:
                    if kind == "L0" or kind == "L1" and n not in L0_ONLY or n in ("oh_ready", "acc_done", "agg_mm"):
                        eng.sem_inc(s[n], SKIPPED * PER_STEP[n])
            return skip

        def count(passes, i, more_turns):
            return passes * (TURNS - ALWAYS) + i - ALWAYS + 1 if more_turns else passes * ALWAYS + i + 1


        bcast = lambda ap: ap.partition_broadcast(P)
        vec = lambda name: bcast(a[name])
        lvec = lambda name, l: bcast(a[name][l])
        const_loads = [
            (ident[:, :], a["c_ident"]), (iota[:, :], a["c_iota"]), (blk[:, :], a["c_blk"]),
            (misc[:, :], a["c_misc"]),
            (X[:, :].rearrange("p (t d) -> p t d", d=D), a["x"].rearrange("(t p) d -> p t d", p=P)),
            (Wf1[:, :], a["L0_gnn_Wf1"]), (Wf2[:, :, :], a["L0_gnn_Wf2"].rearrange("(p k) n -> p k n", p=P)),
            (bf1[:, :], a["L0_gnn_bf1"].rearrange("(p k) -> p k", p=P)),
            (relv[:, 0, :], bcast(a["L0_gnn_rel_v"][0])), (relv[:, 1, :], bcast(a["L0_gnn_rel_v"][1])),
            (bd1r[32:34, :], a["L0_gnn_bd1"].partition_broadcast(2)),
            (bt34[32:34, :], a["L0_gnn_bt"].partition_broadcast(2)),
            (wd2[0:64, :], a["L0_gnn_Wd2"]), (wd2[64:65, :], a["L0_gnn_bd2"].partition_broadcast(1)),
            (hp[:, 0, :], vec("L0_gnn_decay_scale")), (hp[:, 1, :], vec("L0_gnn_hyp_beta")),
            (hp[:, 2, :], vec("L0_gnn_logit_alpha")),
            (cm[:, 0:1], bcast(a["L0_gnn_c_mag"])),
        ]
        row_loads = [
            (wk34[0:32, :], a["L0_gnn_Wt"]), (wk34[32:33, :], a["L0_gnn_rel_k"][1:2]),
            (wk34[33:34, :], a["L0_gnn_rel_k"][0:1]),
            (relq[32:33, :], a["L0_gnn_rel_q"][1:2]), (relq[33:34, :], a["L0_gnn_rel_q"][0:1]),
            (wd1t[32:33, :], a["L0_gnn_Wd1"][1:2]), (wd1t[34:35, :], a["L0_gnn_Wd1"][0:1]),
        ]
        for n in ("Wq", "Wk", "Wv", "Wo"):
            const_loads.append((W[n][:, :], a["L0_gnn_" + n]))
        const_loads.append((W["Win"][:, :], a["L1_gnn_Win_w"]))
        for n in ("Wl1", "Wr1", "Wl2", "Wr2"):
            const_loads.append((W["L2_" + n][:, :], a["L2_gnn_" + n + "_T"]))
        const_loads.append((W["L3_W"][:, :], a["L3_gnn_W_T"]))
        for n in ("bo", "g1", "be1", "g2", "be2", "bf2"):
            const_loads.append((V[n][:, :], vec("L0_gnn_" + n)))
        for n in ("Win_b", "ln_in_g", "ln_in_b", "fn_g", "fn_b"):
            const_loads.append((V[n][:, :], vec("L1_gnn_" + n)))
        for n in ("bl1", "bl2"):
            const_loads.append((V["L2_" + n][:, :], vec("L2_gnn_" + n)))
        const_loads.append((V["L3_b"][:, :], vec("L3_gnn_b")))

        dst_i = T[:, 0:NCH * (EPP + 2)].bitcast(I32).rearrange("p (c k) -> p c k", k=EPP + 2)
        dst_f = A[:, 0:NCH * (EPP + 2)].rearrange("p (c k) -> p c k", k=EPP + 2)
        same = B[:, 0:NCH * (EPP + 1)].rearrange("p (c k) -> p c k", k=EPP + 1)
        pk_all = onehot[:, :, :, :].rearrange("p b j n -> p (b j n)")[:, 0:NCH * PK].rearrange("p (c k) -> p c k", k=PK)
        g_all = C[:, 0:2 * NCH].rearrange("p (g c) -> p g c", g=2)
        g_out = C[:, 1024:1024 + 2 * P].rearrange("p (g c) -> p g c", g=2)
        types_all = H[:, 0:NCH * EPP].bitcast(I32)
        ends_i = H[:, 1024:1024 + 2 * NCH].bitcast(I32).rearrange("p (g c) -> p g c", g=2)
        ends = H[:, 1280:1280 + 16 * P].rearrange("p (g c) -> p g c", g=16)
        pre_loads = [
            (dst_i, a["dst_win"]), (types_all.rearrange("p (c k) -> p c k", k=EPP), a["type_edges"].rearrange("c p k -> p c k")),
            (ends_i, a["dst_ends"].partition_broadcast(P)),
        ]

        block = ctx.enter_context(nc.Block())

        @block.sync
        def _(sp):
            for dst_ap, src_ap in const_loads + pre_loads:
                sp.dma_start(dst_ap, src_ap).then_inc(loaded, 16)
            sp.wait_ge(pre_asked, 1)
            for dst_ap, src_ap in row_loads:
                sp.dma_start(dst_ap, src_ap).then_inc(loaded, 16)
            sp.wait_ge(pre_asked, 3)
            sp.dma_start(pk_tab.rearrange("c p k -> p c k"), pk_all).then_inc(pre_done, 16)
            sp.dma_start(g_tab.rearrange("g c p -> c g p")[0:NCH], g_out[0:NCH]).then_inc(pre_done, 16)
            sp.dma_start(step_tab, ends[:, 15, 0:2].bitcast(I32)).then_inc(pre_done, 16)
            sp.dma_start(base_tab, ends[:, 15, 2:3]).then_inc(pre_done, 16)
            sp.wait_ge(pre_done, 4 * 16)
            sp.dma_start(steps_i[:, :], step_tab.rearrange("p k -> (p k)").partition_broadcast(1)).then_inc(steps_in, 16)

            def step_inputs(kind, k, turn, b, part):
                r = turn * RING + b
                hold(sp, s["acc_done" if kind == "sum" else "weighted_ready"], k - RING + 1)
                c = sp.value_load(steps_i[0:1, bass.ds(r * 2, 1)], min_val=0, max_val=NCH - 1)
                ready = in_ready[kind][part][b]
                sp.dma_start(src_ids[:, b, :], a["src_edges"][c]).then_inc(ready, 16)
                sp.dma_start(pk[:, b, :], pk_tab[c]).then_inc(ready, 16)
                sp.dma_start(wbase[:, b:b + 1], base_tab[r].partition_broadcast(P)).then_inc(ready, 16)
                if kind == "sum":
                    return
                w = sp.value_load(steps_i[0:1, bass.ds(r * 2 + 1, 1)], min_val=0, max_val=LAST_WIN)
                for g in range(2):
                    sp.dma_start(gp[32 * g:32 * g + HEADS, b, :], g_tab[g, c].partition_broadcast(HEADS)).then_inc(ready, 16)
                if kind == "L0":
                    sp.dma_start(win[:, b, :, :], qm_tab.rearrange("(w p) d -> w p d", p=P)[bass.ds(w, 2)].rearrange("w p d -> p w d")).then_inc(ready, 16)
                    sp.dma_start(attr[0:32, b, :], a["time_edges"][c]).then_inc(ready, 16)
                    sp.dma_start(attr[96:98, b, :].bitcast(I32), a["type_rows"][c].partition_broadcast(2)).then_inc(ready, 16)
                    sp.dma_start(type_i[:, b, :], a["type_edges"][c]).then_inc(ready, 16)
                    sp.dma_start(attr[34:35, b, :], a["weight_rows"][c].partition_broadcast(1)).then_inc(ready, 16)
                else:
                    sp.dma_start(win[:, b, :, 0:D], xr_tab.rearrange("(w p) d -> w p d", p=P)[bass.ds(w, 2)].rearrange("w p d -> p w d")).then_inc(ready, 16)
                    sp.dma_start(attr[0:3, b, :], a["attr_edges"][c]).then_inc(ready, 16)

            sp.wait_ge(steps_in, 16)
            sp.wait_ge(store_ask, 1)
            for i, buf in enumerate((A, B, C)):
                sp.dma_start(kvm_tab.rearrange("(t p) d -> p t d", p=P)[:, :, i * D:(i + 1) * D], nodes(buf)).then_inc(stored, 16)
            for i, buf in enumerate((H, T)):
                sp.dma_start(qm_tab.rearrange("(t p) d -> p t d", p=P)[:, :, i * D:(i + 1) * D], nodes(buf)).then_inc(stored, 16)
            sp.wait_ge(stored, 5 * 16)
            turns(sp, lambda i, b, more, part: step_inputs("L0", first_step(0) + i * RING + b, i, b, part))

            with sp.Fori(0, LAYERS) as l:
                hold(sp, layer_used, l + 1)
                for dst_ap, src_ap in (
                    (W["Wl"][:, :], a["L1_gnn_Wl_w"][l]), (W["Wr"][:, :], a["L1_gnn_Wr_w"][l]), (We[0:3, :], a["L1_gnn_We_w"][l]),
                    (att[:, :], a["L1_gnn_att"][l]), (g1w[:, :], a["L1_gnn_g1_w"][l]), (g1b[:, :], a["L1_gnn_g1_b"][l]),
                    (g2w[:, :], a["L1_gnn_g2_w"][l]), (V["ln_g"][:, :], lvec("L1_gnn_ln_g", l)), (V["ln_b"][:, :], lvec("L1_gnn_ln_b", l)),
                    (V["Wl_b"][:, :], lvec("L1_gnn_Wl_b", l)), (V["Wr_b"][:, :], lvec("L1_gnn_Wr_b", l)),
                    (V["conv_b"][:, :], lvec("L1_gnn_conv_b", l)), (V["g2_b"][:, :], lvec("L1_gnn_g2_b", l))):
                    sp.dma_start(dst_ap, src_ap).then_inc(layer_in, 16)
                hold(sp, store_ask, l + 2)
                sp.dma_start(xl_tab.rearrange("(t p) d -> p t d", p=P), nodes(B)).then_inc(stored, 16)
                sp.dma_start(xr_tab.rearrange("(t p) d -> p t d", p=P), nodes(C)).then_inc(stored, 16)
                hold(sp, stored, (l + 1) * 32 + 5 * 16)
                turns(sp, lambda i, b, more, part: step_inputs("L1", first_step(1) + l * STEPS + i * RING + b, i, b, part))

            for n, buf in enumerate((X, H, X)):
                sp.wait_ge(store_ask, 2 + LAYERS + n)
                sp.dma_start(xl_tab.rearrange("(t p) d -> p t d", p=P), nodes(buf)).then_inc(stored, 16)
                sp.wait_ge(stored, 5 * 16 + LAYERS * 32 + (n + 1) * 16)
                turns(sp, lambda i, b, more, part: step_inputs("sum", first_step(1 + LAYERS + n) + i * RING + b, i, b, part))

            sp.wait_ge(store_ask, 2 + LAYERS + 3)
            sp.dma_start(out[0:LAST_WIN * P].rearrange("(t p) d -> p t d", p=P), nodes(X)[:, 0:LAST_WIN, :]).then_inc(stored, 16)
            sp.dma_start(out[LAST_WIN * P:N], X[0:N - LAST_WIN * P, LAST_WIN * D:(LAST_WIN + 1) * D]).then_inc(stored, 16)
            sp.wait_ge(stored, 5 * 16 + LAYERS * 32 + 3 * 16 + 32)

        @block.gpsimd
        def _(pool):
            def gather(kind, table, width, passes, i, b, part, pitch=None):
                pitch = pitch or width
                hold(pool, in_ready[kind][part][b], count(passes, i, part) * 16 * LOADS[kind])
                for j in range(EPP):
                    pool.indirect_dma_start(rows[b][:, j * pitch:j * pitch + width], None, table,
                                            bass.IndirectOffsetOnAxis(ap=src_ids[:, b, j:j + 1], axis=0)).then_inc(gathered[part][b], 16)

            turns(pool, lambda i, b, more, part: gather("L0", kvm_tab, 3 * D, 0, i, b, part))
            with pool.Fori(0, LAYERS) as l:
                turns(pool, lambda i, b, more, part: gather("L1", xl_tab, D, l, i, b, part))
            for n in range(3):
                turns(pool, lambda i, b, more, part: gather("sum", xl_tab, D, n, i, b, part, SUMW))

        @block.scalar
        def _(act):
            start_up(act, "act")

            def copy_turned(n):
                for g, (t0, nt) in enumerate(GROUPS):
                    act.wait_ge(tr_done, n * NG + g + 1)
                    act.copy(T[:, t0 * D:(t0 + nt) * D], ps[:, TR0 + g % 2, 0:nt * D]).then_inc(tr_copied, 1)

            def asked(n):
                act.wait_ge(ask_act, n + 1)

            col = lambda i: cols[:, i, :]
            asked(0)
            act.activation(hp[:, 3, :], hp[:, 2, :], ACT.Sigmoid)
            act.activation(cm[:, 2:3], cm[:, 1:2], ACT.Sqrt)
            act.activation(col(1), col(0), ACT.Sqrt).then_inc(act_gave, 1)
            asked(1)
            act.activation(col(7), col(3), ACT.Tanh)
            act.activation(col(8), col(4), ACT.Sin)
            act.activation(col(9), col(5), ACT.Sin).then_inc(act_gave, 1)
            asked(2)
            act.activation(col(13), col(12), ACT.Sqrt).then_inc(act_gave, 1)
            copy_turned(0)

            def step_turned(k):
                for q in range(4):
                    after(act, "oht_mm", k, q)
                    act.copy(onehot_t[:, :, q * 2 * P:(q + 1) * 2 * P].rearrange("p w (j e) -> p j w e", e=P),
                             ps[:, OHT0 + q % 2, :].rearrange("p (j w e) -> p j w e", j=2, w=2)).then_inc(s["oht_ready"], 1)

            def exps(k):
                after(act, "delta_ready", k)
                act.activation(ex[:, :], delta[:, :], ACT.Exp).then_inc(s["ex_ready"], 1)

            def l0_relu(k):
                for h in range(2):
                    after(act, "dech_mm", k, h)
                    act.activation(dec_h[0:64, h, :], ps[0:64, OHT0 + h, :], ACT.Relu).then_inc(s["dech_ready"], 1)

            def l0_copy(k, h):
                after(act, "z_mm", k, h)
                act.copy(chan[:, h, :], ps[:, MM0 + 1, :])
                act.activation(sq[:, h, :], ps[:, MM0 + 2, :], ACT.Square).then_inc(s["z_copied"], 1)

            def l0_tanh(k):
                after(act, "dec_mm", k)
                act.activation(small["dec"][:, :], ps[:, OHT0, 0:S64], ACT.Tanh).then_inc(s["tanh_ready"], 1)

            def l0_decay(k):
                after(act, "decs_ready", k)
                act.activation(small["dec"][:, :], small["dec2"][:, :], ACT.Exp).then_inc(s["decay_ready"], 1)

            def l0_dist(k):
                after(act, "dist_asked", k)
                act.activation(dist[:, :], dist2[:, :], ACT.Sqrt).then_inc(s["dist_ready"], 1)

            def l0_begin(i, part):
                k = first_step(0) + i * RING
                step_turned(k)
                l0_relu(k)
                l0_copy(k, 0)
                l0_tanh(k)
                l0_copy(k, 1)
                l0_decay(k)
                step_turned(k + 1)
                l0_dist(k)

            def l0_step(i, b, more, part):
                k = first_step(0) + i * RING + b
                if more:
                    l0_relu(k + 1)
                    l0_copy(k + 1, 0)
                exps(k)
                if more:
                    l0_tanh(k + 1)
                    l0_copy(k + 1, 1)
                    l0_decay(k + 1)
                if more > 1:
                    step_turned(k + 2)
                if more:
                    l0_dist(k + 1)

            turns(act, l0_step, l0_begin, skip_steps(act, "act", "L0"))

            copy_turned(1)
            asked(3)
            act.activation(col(2), col(1), ACT.Sqrt).then_inc(act_gave, 1)
            copy_turned(2)
            for g, (t0, nt) in enumerate(GROUPS):
                act.wait_ge(hid_mm, g + 1)
                if g:
                    act.wait_ge(mm_done, 4 * NG + g)
                for c in range(4):
                    ins = act.activation(A[:, c * 512:c * 512 + nt * D], ps[:, HID0 + c, 0:nt * D], ACT.Gelu, bias=bf1[:, c:c + 1])
                ins.then_inc(hid_act, 1)
            for n in (4, 5):
                asked(n)
                act.activation(col(2), col(1), ACT.Sqrt).then_inc(act_gave, 1)
            copy_turned(3)
            asked(6)
            act.activation(A[:, :], A[:, :], ACT.Gelu_apprx_tanh).then_inc(act_gave, 1)
            asked(7)
            act.activation(col(2), col(1), ACT.Sqrt).then_inc(act_gave, 1)
            with act.Fori(0, LAYERS) as l:
                asked(8 + l * 3)
                act.activation(col(2), col(1), ACT.Sqrt).then_inc(act_gave, 1)
                copy_turned(4 + l * 2)

                def l1_scaled(k, h):
                    after(act, "z_mm", k, h)
                    act.activation(chan[:, h, :], ps[:, MM0 + h, :], ACT.Copy, scale=0.2).then_inc(s["z_copied"], 1)

                def l1_begin(i, part):
                    k = first_step(1) + l * STEPS + i * RING
                    step_turned(k)
                    l1_scaled(k, 0)
                    l1_scaled(k, 1)
                    step_turned(k + 1)

                def l1_step(i, b, more, part):
                    k = first_step(1) + l * STEPS + i * RING + b
                    if more:
                        l1_scaled(k + 1, 0)
                    exps(k)
                    if more:
                        l1_scaled(k + 1, 1)
                    if more > 1:
                        step_turned(k + 2)

                turns(act, l1_step, l1_begin, skip_steps(act, "act", "L1"))
                asked(9 + l * 3)
                act.activation(A[:, :], A[:, :], ACT.Gelu_apprx_tanh).then_inc(act_gave, 1)
                copy_turned(5 + l * 2)
                for g, (t0, nt) in enumerate(GROUPS):
                    act.wait_ge(hid_mm, NG + l * NG + g + 1)
                    act.activation(C[0:64, t0 * D:(t0 + nt) * D], ps[0:64, HID0 + g % 2, 0:nt * D], ACT.Gelu_apprx_tanh,
                                   bias=g1b[:, 0:1]).then_inc(hid_act, 1)
                asked(10 + l * 3)
                act.activation(B[:, :], B[:, :], ACT.Sigmoid).then_inc(act_gave, 1)
            n0 = 8 + 3 * LAYERS
            for n in (n0, n0 + 1):
                asked(n)
                act.activation(col(2), col(1), ACT.Sqrt).then_inc(act_gave, 1)
            for n in range(3):
                t = 4 + 2 * LAYERS
                if n < 2:
                    for g, (t0, nt) in enumerate(GROUPS):
                        act.wait_ge(tr_done, (t + 2 * n) * NG + g + 1)
                        act.copy(T[:, t0 * D:(t0 + nt) * D], ps[:, TR0 + g % 2, 0:nt * D]).then_inc(tr_copied, 1)
                    for g, (t0, nt) in enumerate(GROUPS):
                        act.wait_ge(tr_done, (t + 2 * n + 1) * NG + g + 1)
                        act.copy(C[:, t0 * D:(t0 + nt) * D], ps[:, TR0 + g % 2, 0:nt * D]).then_inc(tr_copied, 1)
                else:
                    copy_turned(t + 4)
                if n:
                    asked(n0 + 1 + n)
                    act.activation(col(2), col(1), ACT.Sqrt).then_inc(act_gave, 1)

        @block.tensor
        def _(pe):
            start_up(pe, "pe")
            pe.wait_ge(loaded, 16 * len(const_loads + pre_loads + row_loads))

            def turn(n, buf):
                pe.wait_ge(src_ready, n + 1)
                for g, (t0, nt) in enumerate(GROUPS):
                    if g >= 2:
                        pe.wait_ge(tr_copied, n * NG + g - 1)
                    elif g == 0 and not (isinstance(n, int) and n == 0):
                        pe.wait_ge(tr_copied, n * NG)
                    for t in range(nt):
                        ins = pe.transpose(ps[:, TR0 + g % 2, t * D:(t + 1) * D], buf[:, (t0 + t) * D:(t0 + t + 1) * D], ident[:, :])
                    ins.then_inc(tr_done, 1)

            def product(n, pairs, turned, first_turned=None):
                for g, (t0, nt) in enumerate(GROUPS):
                    pe.wait_ge(tr_copied, turned * NG + g + 1)
                    if g >= 2:
                        pe.wait_ge(mm_copied, n * NG + g - 1)
                    elif g == 0 and not (isinstance(n, int) and n == 0):
                        pe.wait_ge(mm_copied, n * NG)
                    for t in range(nt):
                        for i, (buf, w) in enumerate(pairs):
                            ins = pe.matmul(ps[:, MM0 + g % 2, t * D:(t + 1) * D], buf[:, (t0 + t) * D:(t0 + t + 1) * D], w[:, :],
                                            start=i == 0, stop=i == len(pairs) - 1)
                    ins.then_inc(mm_done, 1)

            def onehots_turned(kind, k, b):
                after(pe, "oh_ready", k)
                for q in range(4):
                    if q < 2:
                        after(pe, "oht_ready", k - 1, q + 2)
                    else:
                        after(pe, "oht_ready", k, q - 2)
                    if kind == "L0" and q == 0:
                        after(pe, "tanh_ready", k - 1)
                    for r in range(4):
                        j, w = q * 2 + r // 2, r % 2
                        ins = pe.transpose(ps[:, OHT0 + q % 2, r * P:(r + 1) * P], onehot[:, b, j, w * P:(w + 1) * P], ident[:, :])
                    ins.then_inc(s["oht_mm"], 1)

            def spread(bank, b, h, c0, begins=False):
                for w in range(2):
                    ins = pe.matmul(ps[:, bank, :], win[:, b, w, c0:c0 + D], onehot_t[:, w, h * HALF:(h + 1) * HALF],
                                    start=begins and w == 0, stop=not begins and w == 1, skip_group_check=not begins)
                return ins

            def add_rows(bank, b, h, width, c0):
                for r in range(4):
                    j = h * 4 + r
                    ins = pe.matmul(ps[:, bank, r * P:(r + 1) * P], rows[b][:, j * width + c0:j * width + c0 + D], ident[:, :],
                                    start=r == 0, stop=False, skip_group_check=True)

            def ends_turned(k):
                after(pe, "ab_ready", k)
                pe.nop(nofuse=True)
                pe.transpose(ps[0:40, SM, 64:192], ab[:, :], ident[:, :]).then_inc(s["ab_mm"], 1)

            def maxima_turned(k):
                after(pe, "scan_ready", k)
                pe.nop(nofuse=True)
                pe.transpose(ps[:, SM, 192:232], scans[0:40, 1:129], ident[0:40, 0:40]).then_inc(s["back_mm"], 1)

            def aggregate(k, b, width, src, ready):
                ready()
                for w in range(2):
                    for j in reversed(range(EPP)):
                        n = width if j == 0 else min(width, RC)
                        ins = pe.matmul(ps[:, AGG + w, 0:n], onehot[:, b, j, w * P:(w + 1) * P], src(j, n),
                                        start=j == EPP - 1, stop=j == 0, skip_group_check=True)
                ins.then_inc(s["agg_mm"], 1)

            pe.wait_ge(pre_asked, 2)
            for g in range(2):
                ins = pe.transpose(ps[0:NCH, SM, g * P:(g + 1) * P], g_all[:, g, :], ident[:, :])
            pe.transpose(ps[0:1, SM, 256:384], cm[:, 3:4], ident[:, :]).then_inc(pre_tr, 1)
            pe.wait_ge(pre_asked, 3)
            pe.matmul(ps[:, SM, 400:401], one_col[0:1, 0:1].broadcast_to([1, P]), cm[0:1, 3:4], start=True, stop=True).then_inc(pre_tr, 1)

            turn(0, X)
            for n, w in enumerate(("Wq", "Wk", "Wv")):
                product(n, [(T, W[w])], 0)

            def l0_hidden(k, b):
                after(pe, "types_ready", k)
                for h in range(2):
                    after(pe, "oht_ready", k, 2 + h)
                    pe.nop(nofuse=True)
                    pe.matmul(ps[0:64, OHT0 + h, :], wd1t[:, :], attr[:, b, h * HALF:(h + 1) * HALF], start=True, stop=True).then_inc(s["dech_mm"], 1)

            def l0_z(k, i, b, h, part):
                if h == 0:
                    hold(pe, gathered[part][b], count(0, i, part) * 16 * EPP)
                e = slice(h * HALF, (h + 1) * HALF)
                after(pe, "z_used", k - 1 + h, 1 - h)
                spread(MM0, b, h, 0, True)
                pe.matmul(ps[:, MM0, :], relq[:, :], attr[:, b, e], start=False, stop=True)
                add_rows(MM0 + 1, b, h, 3 * D, 0)
                pe.matmul(ps[:, MM0 + 1, :], wk34[:, :], attr[:, b, e], start=False, stop=True, skip_group_check=True)
                add_rows(MM0 + 2, b, h, 3 * D, 2 * D)
                spread(MM0 + 2, b, h, D).then_inc(s["z_mm"], 1)

            def l0_decays(k):
                after(pe, "dech_ready", k)
                for j in range(EPP):
                    ins = pe.matmul(ps[:, OHT0, j:S64:EPP], dec_h[0:65, j // 4, j % 4 * P:(j % 4 + 1) * P], wd2[:, :], start=True, stop=True)
                ins.then_inc(s["dec_mm"], 1)

            def l0_scores(k):
                after(pe, "z_used", k)
                for j in range(EPP):
                    h, t = j // 4, slice(j % 4 * P, (j % 4 + 1) * P)
                    pe.matmul(ps[:, SM, j:S64:EPP], prod[:, h, t], blk4[:, :], start=True, stop=True)
                    ins = pe.matmul(ps[:, SM, 320 + j:321 + j], sq[:, h, t], misc[:, 2:3], start=True, stop=True)
                ins.then_inc(s["logit_mm"], 1)

            def weighted_sums(k, b):
                aggregate(k, b, AW, lambda j, n: weighted[:, j, 0:n], lambda: after(pe, "weighted_ready", k))

            def l0_begin(i, part):
                k = first_step(0) + i * RING
                onehots_turned("L0", k, 0)
                l0_hidden(k, 0)
                l0_z(k, i, 0, 0, part)
                l0_decays(k)
                l0_z(k, i, 0, 1, part)
                onehots_turned("L0", k + 1, 1)
                l0_scores(k)

            def l0_step(i, b, more, part):
                k = first_step(0) + i * RING + b
                i1, b1 = later(i, b, 1)
                ends_turned(k)
                if more:
                    l0_hidden(k + 1, b1)
                    l0_z(k + 1, i1, b1, 0, part)
                maxima_turned(k)
                if more:
                    l0_decays(k + 1)
                    l0_z(k + 1, i1, b1, 1, part)
                if more > 1:
                    onehots_turned("L0", k + 2, later(i, b, 2)[1])
                if more:
                    l0_scores(k + 1)
                weighted_sums(k, b)

            turns(pe, l0_step, l0_begin, skip_steps(pe, "pe", "L0"))

            turn(1, A)
            product(3, [(T, W["Wo"])], 1)
            turn(2, H)
            for g, (t0, nt) in enumerate(GROUPS):
                pe.wait_ge(tr_copied, 2 * NG + g + 1)
                if g:
                    pe.wait_ge(hid_act, g)
                for c in range(4):
                    ins = pe.matmul(ps[:, HID0 + c, 0:nt * D], Wf1[:, c:4 * D:4], T[:, t0 * D:(t0 + nt) * D], start=True, stop=True)
                ins.then_inc(hid_mm, 1)
                pe.wait_ge(hid_act, g + 1)
                pe.wait_ge(mm_copied, 4 * NG + max(g - 1, 0))
                for t in range(nt):
                    for c in range(4):
                        ins = pe.matmul(ps[:, MM0 + g % 2, t * D:(t + 1) * D], A[:, c * 512 + t * D:c * 512 + (t + 1) * D],
                                        Wf2[:, c, :], start=c == 0, stop=c == 3)
                ins.then_inc(mm_done, 1)

            turn(3, X)
            product(5, [(T, W["Win"])], 3)
            with pe.Fori(0, LAYERS) as l:
                pe.wait_ge(layer_in, (l + 1) * 16 * 13)
                turn(4 + l * 2, A)
                product(6 + l * 3, [(T, W["Wl"])], 4 + l * 2)
                product(7 + l * 3, [(T, W["Wr"])], 4 + l * 2)

                def l1_z(k, i, b, h, part):
                    if h == 0:
                        hold(pe, gathered[part][b], count(l + 1, i, part) * 16 * EPP)
                        after(pe, "oht_ready", k, 3)
                        after(pe, "z_used", k - 1)
                    add_rows(MM0 + h, b, h, D, 0)
                    pe.matmul(ps[:, MM0 + h, :], We[:, :], attr[:, b, h * HALF:(h + 1) * HALF], start=False, stop=False, skip_group_check=True)
                    spread(MM0 + h, b, h, 0).then_inc(s["z_mm"], 1)

                def l1_scores(k):
                    after(pe, "delta_ready", k - 1)
                    pe.nop(nofuse=True)
                    for h in range(2):
                        after(pe, "z_used", k, h)
                        for r in range(4):
                            j = h * 4 + r
                            ins = pe.matmul(ps[:, SM, j:S64:EPP], prod[:, h, r * P:(r + 1) * P], attb[:, :], start=True, stop=True)
                    ins.then_inc(s["logit_mm"], 1)

                def l1_begin(i, part):
                    k = first_step(1) + l * STEPS + i * RING
                    onehots_turned("L1", k, 0)
                    l1_z(k, i, 0, 0, part)
                    l1_z(k, i, 0, 1, part)
                    onehots_turned("L1", k + 1, 1)
                    l1_scores(k)

                def l1_step(i, b, more, part):
                    k = first_step(1) + l * STEPS + i * RING + b
                    i1, b1 = later(i, b, 1)
                    ends_turned(k)
                    if more:
                        l1_z(k + 1, i1, b1, 0, part)
                    maxima_turned(k)
                    if more:
                        l1_z(k + 1, i1, b1, 1, part)
                    if more > 1:
                        onehots_turned("L1", k + 2, later(i, b, 2)[1])
                    if more:
                        l1_scores(k + 1)
                    weighted_sums(k, b)

                turns(pe, l1_step, l1_begin, skip_steps(pe, "pe", "L1"))
                turn(5 + l * 2, A)
                for g, (t0, nt) in enumerate(GROUPS):
                    pe.wait_ge(tr_copied, (5 + l * 2) * NG + g + 1)
                    if g >= 2:
                        pe.wait_ge(hid_act, NG + l * NG + g - 1)
                    pe.matmul(ps[0:64, HID0 + g % 2, 0:nt * D], g1w[:, :], T[:, t0 * D:(t0 + nt) * D], start=True, stop=True).then_inc(hid_mm, 1)
                for g, (t0, nt) in enumerate(GROUPS):
                    pe.wait_ge(hid_act, NG + l * NG + g + 1)
                    pe.wait_ge(mm_copied, (8 + l * 3) * NG + max(g - 1, 0))
                    for t in range(nt):
                        ins = pe.matmul(ps[:, MM0 + g % 2, t * D:(t + 1) * D], C[0:64, (t0 + t) * D:(t0 + t + 1) * D], g2w[:, :], start=True, stop=True)
                    ins.then_inc(mm_done, 1)

            for n in range(3):
                def sum_step(i, b, more, part):
                    k = first_step(1 + LAYERS + n) + i * RING + b

                    def ready():
                        hold(pe, gathered[part][b], count(1 + LAYERS + n, i, part) * 16 * EPP)
                        after(pe, "oh_ready", k)
                        after(pe, "acc_done", k - 1)
                    aggregate(k, b, D + 1, lambda j, m: rows[b][:, j * SUMW:j * SUMW + D + 1], ready)

                turns(pe, sum_step, nothing, skip_steps(pe, "pe", "sum"))
                t, m = 4 + 2 * LAYERS, 6 + 3 * LAYERS
                if n < 2:
                    turn(t + 2 * n, A)
                    turn(t + 2 * n + 1, (X, H)[n])
                    product(m + n, [(T, W[f"L2_Wl{n + 1}"]), (C, W[f"L2_Wr{n + 1}"])], t + 2 * n + 1)
                else:
                    turn(t + 4, A)
                    product(m + 2, [(T, W["L3_W"])], t + 4)

        @block.vector
        def _(dve):
            start_up(dve, "dve")
            v = nc.vector
            col = lambda i: cols[:, i, :]
            onto = lambda ap: ap.unsqueeze(2).broadcast_to([P, NT, D])
            along = lambda t: t[:, :].unsqueeze(1).broadcast_to([P, NT, D])
            asks = [0]

            def ask(n):
                dve.drain().then_inc(ask_act, 1)
                dve.wait_ge(act_gave, n + 1)

            def norm(dst, src, n, gain=None, shift=None):
                dve.drain()
                v.tensor_reduce(col(0), nodes(src), AX, ALU.add)
                dve.drain()
                v.tensor_scalar(col(0), col(0), -1.0 / D, None, ALU.mult)
                dve.drain()
                v.tensor_tensor(nodes(dst), nodes(src), onto(col(0)), ALU.add)
                dve.drain()
                v.tensor_tensor(T[:, :], dst[:, :], dst[:, :], ALU.mult)
                dve.drain()
                v.tensor_reduce(col(1), nodes(T), AX, ALU.add)
                dve.drain()
                v.tensor_scalar(col(1), col(1), 1.0 / D, 1e-5, ALU.mult, ALU.add)
                ask(n)
                v.reciprocal(col(2), col(2))
                dve.drain()
                v.tensor_tensor(nodes(dst), nodes(dst), onto(col(2)), ALU.mult)
                if gain is not None:
                    dve.drain()
                    v.tensor_tensor(nodes(dst), nodes(dst), along(gain), ALU.mult)
                    dve.drain()
                    v.tensor_tensor(nodes(dst), nodes(dst), along(shift), ALU.add)
                dve.drain()

            def give(what, _n=None):
                dve.drain().then_inc(what, 1)

            def evacuate(n, dst, plus):
                for g, (t0, nt) in enumerate(GROUPS):
                    dve.wait_ge(mm_done, n * NG + g + 1)
                    o = nodes(dst)[:, t0:t0 + nt, :]
                    i = ps[:, MM0 + g % 2, 0:nt * D].rearrange("p (t d) -> p t d", d=D)
                    if plus is None:
                        v.tensor_copy(o, i).then_inc(mm_copied, 1)
                    else:
                        v.tensor_tensor(o, i, plus(t0, nt), ALU.add).then_inc(mm_copied, 1)
                dve.drain()

            bias = lambda t: (lambda t0, nt: t[:, :].unsqueeze(1).broadcast_to([P, nt, D]))
            of = lambda buf: (lambda t0, nt: nodes(buf)[:, t0:t0 + nt, :])

            v.memset(wd1t[:, :], 0.0)
            v.memset(relq[:, :], 0.0)
            v.memset(wk34[:, :], 0.0)
            v.memset(We[:, :], 0.0)
            v.memset(attr[:, :, :], 0.0)
            v.memset(ab[:, :], 0.0)
            v.memset(scans[:, :], NEG)
            v.memset(one_col[:, :], 1.0)
            v.memset(weighted[:, :, :], 0.0)
            give(pre_asked)
            dve.wait_ge(loaded, 16 * len(const_loads + pre_loads + row_loads))
            v.tensor_copy(dst_f, dst_i)
            v.tensor_copy(types_all.bitcast(F32), types_all)
            v.tensor_copy(ends[:, 0:2, 0:NCH], ends_i)
            v.memset(g_out, 0.0)
            dve.drain()
            v.tensor_tensor(same, dst_f[:, :, 1:EPP + 2], dst_f[:, :, 0:EPP + 1], ALU.is_equal)
            v.tensor_copy(pk_all[:, :, 0:EPP], dst_f[:, :, 1:EPP + 1])
            ones = lambda ap, n: ap.broadcast_to([P, NCH, n])
            v.tensor_tensor(pk_all[:, :, 3 * EPP:4 * EPP], dst_f[:, :, 1:EPP + 1], ones(dst_f[:, :, 0:1], EPP), ALU.is_equal)
            v.tensor_tensor(pk_all[:, :, 4 * EPP:5 * EPP], dst_f[:, :, 1:EPP + 1], ones(dst_f[:, :, EPP + 1:EPP + 2], EPP), ALU.is_equal)
            v.tensor_tensor(g_all[:, 0, :], dst_f[:, :, EPP], dst_f[:, :, 0], ALU.is_equal)
            v.tensor_tensor(g_all[:, 1, :], dst_f[:, :, 1], dst_f[:, :, EPP + 1], ALU.is_equal)
            dve.drain()
            pen = lambda o, i: v.tensor_scalar(o, i, -1.0, -NEG, ALU.add, ALU.mult)
            pen(pk_all[:, :, EPP:2 * EPP], same[:, :, 0:EPP])
            pen(pk_all[:, :, 2 * EPP:3 * EPP], same[:, :, 1:EPP + 1])
            pen(pk_all[:, :, 3 * EPP:5 * EPP], pk_all[:, :, 3 * EPP:5 * EPP])
            pen(g_all, g_all)
            dve.drain()
            v.memset(pk_all[:, :, EPP:EPP + 1], NEG)
            v.memset(pk_all[:, :, 3 * EPP - 1:3 * EPP], NEG)
            E_ = lambda i: ends[:, i, 0:NCH]
            Ei = lambda i: ends[:, i, 0:NCH].bitcast(I32)
            v.tensor_scalar(ends_i, ends_i, 7, None, ALU.arith_shift_right)
            dve.drain()
            v.tensor_copy(ends[:, 2:4, 0:NCH], ends_i)
            dve.drain()
            v.tensor_tensor(E_(4), E_(3), E_(2), ALU.subtract)
            dve.drain()
            v.tensor_copy(Ei(5), E_(4))
            dve.drain()
            v.tensor_scalar(Ei(5), Ei(5), 1, None, ALU.arith_shift_right)
            dve.drain()
            v.tensor_copy(E_(6), Ei(5))
            dve.drain()
            v.tensor_scalar(E_(6), E_(6), 1.0, None, ALU.add)
            v.memset(E_(7), 1.0)
            dve.drain()
            v.tensor_tensor_scan(E_(8), E_(7), E_(6), 0.0, ALU.mult, ALU.add)
            dve.drain()
            v.tensor_tensor(E_(9), E_(8), E_(6), ALU.subtract)
            dve.drain()
            v.tensor_scalar(E_(10), E_(9), misc[:, 0:1], None, ALU.is_le)
            v.tensor_scalar(E_(11), E_(9), -2.0, None, ALU.mult)
            dve.drain()
            v.tensor_tensor(E_(11), E_(11), E_(2), ALU.add)
            v.tensor_copy(E_(12), E_(10))
            dve.drain()
            v.tensor_tensor(ends[:, 12, 0:NCH - 1], ends[:, 10, 0:NCH - 1], ends[:, 10, 1:NCH], ALU.subtract)
            v.tensor_reduce(ends[:, 14, 0:1], E_(10), AX, ALU.add)
            dve.drain()
            v.tensor_tensor(E_(13), E_(12), E_(11), ALU.mult)
            v.tensor_scalar(ends[:, 14, 0:1], ends[:, 14, 0:1], -1.0, None, ALU.add)
            dve.drain()
            v.tensor_reduce(ends[:, 14, 1:2], E_(13), AX, ALU.add)
            dve.drain()
            v.scalar_tensor_tensor(ends[:, 14, 2:3], misc[:, 0:1], 2.0, ends[:, 14, 1:2], ALU.mult, ALU.add)
            dve.drain()
            v.tensor_scalar(ends[:, 15, 2:3], ends[:, 14, 2:3], float(P), None, ALU.mult)
            v.tensor_scalar(ends[:, 14, 1:2], ends[:, 14, 2:3], float(LAST_WIN), None, ALU.min)
            dve.drain()
            v.tensor_copy(ends[:, 15, 0:2].bitcast(I32), ends[:, 14, 0:2])
            v.tensor_scalar(ends[0:1, 15, 4:5], ends[0:1, 8, NCH - 1:NCH], float(ALWAYS * RING), None, ALU.is_gt)
            dve.drain()
            v.tensor_copy(steps_left[:, :], ends[0:1, 15, 4:5])
            v.tensor_reduce(cm[:, 3:4], types_all.bitcast(F32), AX, ALU.max)
            v.tensor_tensor(wk34[32:34, :], wk34[32:34, :], bt34[32:34, :], ALU.add)
            v.tensor_scalar(blk4[:, :], blk[:, :], float(DH) ** -0.5, None, ALU.mult)
            v.tensor_scalar(cm[:, 4:5], cm[:, 0:1], -1.0, None, ALU.mult)
            dve.drain()
            v.tensor_tensor(cm[:, 1:2], cm[:, 0:1], cm[:, 4:5], ALU.max)
            dve.drain()
            v.tensor_scalar(cm[:, 5:6], cm[:, 1:2], 0.0, None, ALU.is_gt)
            v.tensor_scalar(cm[:, 6:7], cm[:, 1:2], 0.0, None, ALU.is_le)
            dve.drain()
            v.tensor_scalar(cm[:, 1:2], cm[:, 1:2], 1e-15, None, ALU.max)
            give(pre_asked)
            dve.wait_ge(pre_tr, 1)
            v.tensor_copy(g_out[0:NCH], ps[0:NCH, SM, 0:2 * P].rearrange("p (g c) -> p g c", g=2))
            v.tensor_reduce(cm[0:1, 3:4], ps[0:1, SM, 256:384], AX, ALU.max)
            give(pre_asked)
            dve.wait_ge(pre_tr, 2)
            v.tensor_scalar(cm[:, 7:8], ps[:, SM, 400:401], 1.0, 1.0, ALU.add, ALU.max)
            dve.drain()
            v.reciprocal(cm[:, 7:8], cm[:, 7:8])
            dve.wait_ge(steps_in, 16)
            dve.drain()
            v.tensor_scalar(wd1t[32:34, :], wd1t[32:34, :], cm[32:34, 7:8], None, ALU.mult)
            dve.drain()
            v.tensor_tensor(wd1t[32:34, :], wd1t[32:34, :], bd1r[32:34, :], ALU.add)
            v.tensor_tensor(B[:, :], X[:, :], X[:, :], ALU.mult)
            dve.drain().then_inc(src_ready, 1)
            v.tensor_reduce(col(0), nodes(B), AX, ALU.add)
            ask(0)
            v.tensor_scalar(col(1), col(1), 1e-15, None, ALU.max)
            v.tensor_scalar(hp[:, 5, :], hp[:, 3, :], -1.0, 1.0, ALU.mult, ALU.add)
            dve.drain()
            v.tensor_tensor(hp[:, 4, :], hp[:, 5, :], hp[:, 1, :], ALU.mult)
            v.tensor_scalar(col(3), col(1), cm[:, 2:3], None, ALU.mult)
            dve.drain()
            v.tensor_scalar(col(10), col(3), 1.0 / PI, None, ALU.mult)
            dve.drain()
            v.tensor_copy(col(14).bitcast(I32), col(10))
            dve.drain()
            v.tensor_copy(col(11), col(14).bitcast(I32))
            dve.drain()
            v.scalar_tensor_tensor(col(4), col(11), -PI, col(3), ALU.mult, ALU.add)
            dve.drain()
            v.tensor_scalar(col(4), col(4), 3.1415925, -3.1415925, ALU.min, ALU.max)
            dve.drain()
            v.scalar_tensor_tensor(col(6), col(4), -1.0, col(4), ALU.mult, ALU.max)
            dve.drain()
            v.tensor_scalar(col(5), col(6), -1.0, PI / 2, ALU.mult, ALU.add)
            ask(1)
            v.tensor_scalar(col(7), col(7), cm[:, 5:6], None, ALU.mult)
            v.tensor_scalar(col(8), col(8), cm[:, 6:7], None, ALU.mult)
            v.tensor_scalar(col(9), col(9), cm[:, 6:7], cm[:, 5:6], ALU.mult, ALU.add)
            dve.drain()
            v.tensor_tensor(col(7), col(7), col(8), ALU.add)
            v.tensor_tensor(col(9), col(9), col(3), ALU.mult)
            dve.drain()
            v.reciprocal(col(9), col(9))
            dve.drain()
            v.tensor_tensor(col(7), col(7), col(9), ALU.mult)
            dve.drain()
            v.tensor_tensor(nodes(C), nodes(X), onto(col(7)), ALU.mult)
            dve.drain()
            v.tensor_tensor(B[:, :], C[:, :], C[:, :], ALU.mult)
            dve.drain()
            v.tensor_reduce(col(12), nodes(B), AX, ALU.add)
            v.reciprocal(cm[:, 2:3], cm[:, 2:3])
            dve.drain()
            v.tensor_scalar(cm[:, 2:3], cm[:, 2:3], 1.0 - 1e-5, None, ALU.mult)
            ask(2)
            v.tensor_scalar(col(15), col(13), cm[:, 2:3], None, ALU.is_gt)
            v.tensor_scalar(col(16), col(13), cm[:, 2:3], None, ALU.max)
            dve.drain()
            v.reciprocal(col(16), col(16))
            dve.drain()
            v.tensor_scalar(col(16), col(16), cm[:, 2:3], -1.0, ALU.mult, ALU.add)
            dve.drain()
            v.tensor_tensor(col(16), col(16), col(15), ALU.mult)
            dve.drain()
            v.tensor_scalar(col(16), col(16), 1.0, None, ALU.add)
            dve.drain()
            v.tensor_tensor(nodes(C), nodes(C), onto(col(16)), ALU.mult)
            evacuate(0, H, None)
            evacuate(1, A, None)
            evacuate(2, B, None)
            v.tensor_scalar(T[:, :], C[:, :], -1.0, None, ALU.mult)
            give(store_ask)

            def onehots(kind, k, passes, i, b, part):
                dve.wait_ge(in_ready[kind][part][b], count(passes, i, part) * 16 * LOADS[kind])
                v.tensor_scalar(rel[:, b, :], pk[:, b, 0:EPP], wbase[:, b:b + 1], None, ALU.subtract)
                dve.drain()
                for j in range(EPP):
                    ins = v.tensor_scalar(onehot[:, b, j, :], iota[:, :], rel[:, b, j:j + 1], None, ALU.is_equal)
                ins.then_inc(s["oh_ready"], 1)

            heads_first = lambda t: t.rearrange("p (h j) -> p h j", j=EPP)
            per_edge = lambda ap: ap.unsqueeze(1).broadcast_to([P, HEADS, EPP])
            per_head = lambda ap: ap.unsqueeze(2).broadcast_to([P, HEADS, EPP])

            q = {n: t[:, :] for n, t in small.items()}

            def own_maxima(k, b):
                v.tensor_copy(heads_first(q["pen_f"]), per_edge(pk[:, b, EPP:2 * EPP]))
                v.tensor_copy(heads_first(q["pen_r"]), per_edge(pk[:, b, 2 * EPP:3 * EPP]))
                v.tensor_copy(scans[0:HEADS, 1:2], scans[0:HEADS, 129:130])
                dve.drain()
                v.tensor_tensor_scan(q["run_f"], q["pen_f"], q["logit"], NEG, ALU.add, ALU.max)
                dve.drain()
                v.tensor_tensor_scan(q["run_r"][:, ::-1], q["pen_r"][:, ::-1], q["run_f"][:, ::-1], NEG, ALU.add, ALU.max)
                dve.drain()
                v.tensor_copy(ab[:, 0:HEADS], heads_first(q["run_f"])[:, :, EPP - 1])
                v.tensor_copy(ab[:, 32:32 + HEADS], heads_first(q["run_r"])[:, :, 0])
                give(s["ab_ready"])

            def between(k, b):
                after(dve, "ab_mm", k)
                v.tensor_tensor_scan(scans[0:HEADS, 2:130], gp[0:HEADS, b, :], ps[0:HEADS, SM, 64:192],
                                     scans[0:HEADS, 1:2], ALU.add, ALU.max)
                v.tensor_tensor_scan(scans[32:32 + HEADS, 127::-1], gp[32:32 + HEADS, b, ::-1], ps[32:32 + HEADS, SM, 191:63:-1],
                                     NEG, ALU.add, ALU.max)
                give(s["scan_ready"])

            def less_maxima(k, b):
                after(dve, "back_mm", k)
                before, behind = ps[:, SM, 192:192 + HEADS], ps[:, SM, 224:224 + HEADS]
                v.tensor_tensor(heads_first(q["m1"]), per_head(before), per_edge(pk[:, b, 3 * EPP:4 * EPP]), ALU.add)
                v.tensor_tensor(heads_first(q["m2"]), per_head(behind), per_edge(pk[:, b, 4 * EPP:5 * EPP]), ALU.add)
                dve.drain()
                v.tensor_tensor(q["m1"], q["m1"], q["run_r"], ALU.max)
                dve.drain()
                v.tensor_tensor(q["m1"], q["m1"], q["m2"], ALU.max)
                dve.drain()
                v.tensor_tensor(delta[:, 0:S64], q["logit"], q["m1"], ALU.subtract)
                v.tensor_tensor(delta[:, S64:], before, heads_first(q["m1"])[:, :, 0], ALU.subtract)
                dve.drain()
                v.tensor_scalar(delta[:, S64:], delta[:, S64:], 0.0, None, ALU.min)
                give(s["delta_ready"])

            def rows_weighted(k, b, passes, i, part, width, c0, typed):
                after(dve, "ex_ready", k)
                dve.wait_ge(gathered[part][b], count(passes, i, part) * 16 * EPP)
                by_head = weighted[:, :, 0:RC].rearrange("p j (h c) -> p j h c", c=HW)
                e = ex[:, 0:S64].rearrange("p (h j) -> p j h", j=EPP)
                vals = rows[b][:, 0:EPP * width].rearrange("p (j r) -> p j r", r=width)[:, :, c0:c0 + D].rearrange("p j (h c) -> p j h c", c=DH)
                v.tensor_tensor(by_head[:, :, :, 0:DH], vals, e.unsqueeze(3).broadcast_to([P, EPP, HEADS, DH]), ALU.mult)
                v.tensor_scalar(weighted[:, 0, RC:AW], ex[:, S64:], -1.0, misc[:, 1:2], ALU.add, ALU.mult)
                if typed:
                    v.tensor_tensor(by_head[:, :, :, DH + 1], e, type_f[:, b, :].unsqueeze(2).broadcast_to([P, EPP, HEADS]), ALU.mult)
                    dve.drain()
                    v.tensor_tensor(by_head[:, :, :, DH], e, by_head[:, :, :, DH + 1], ALU.subtract)
                else:
                    v.tensor_copy(by_head[:, :, :, DH], e)
                give(s["weighted_ready"])

            def accumulate(k, r, width, rescaled):
                w = dve.value_load(steps_i[0:1, bass.ds(r * 2 + 1, 1)], min_val=0, max_val=LAST_WIN)
                after(dve, "agg_mm", k)
                own = acc[:, bass.ds(w, 2), :]
                if rescaled:
                    v.tensor_scalar(grow[:, :, :], ps[:, AGG:AGG + 2, RC:AW], 1.0, None, ALU.add)
                    dve.drain()
                    by_head = own[:, :, 0:RC].rearrange("p w (h c) -> p w h c", c=HW)
                    v.tensor_tensor(by_head, by_head, grow[:, :, :].unsqueeze(3).broadcast_to([P, 2, HEADS, HW]), ALU.mult)
                    dve.drain()
                v.tensor_tensor(own[:, :, 0:width], own[:, :, 0:width], ps[:, AGG:AGG + 2, 0:width], ALU.add)
                give(s["acc_done"])

            def clear(kind):
                v.memset(acc[:, :, :], 0.0)
                if kind == "sum":
                    for b in range(RING):
                        v.memset(rows[b][:, 0:EPP * SUMW].rearrange("p (j r) -> p j r", r=SUMW)[:, :, D:], 1.0)
                else:
                    v.memset(scans[0:HEADS, 129:130], NEG)
                    v.memset(weighted[:, :, :], 0.0)
                dve.drain()

            dve.wait_ge(stored, 5 * 16)
            v.memset(dec_h[64:65, :, :], 1.0)
            clear("L0")
            def l0_types(k, b):
                v.tensor_copy(type_f[:, b, :], type_i[:, b, :])
                v.tensor_scalar(attr[32:34, b, :], attr[96:98, b, :].bitcast(I32), misc[96:98, 3:4], misc[96:98, 4:5], ALU.mult, ALU.add)
                give(s["types_ready"])

            def l0_product(k, h):
                after(dve, "z_copied", k, h)
                v.tensor_tensor(prod[:, h, :], ps[:, MM0, :], chan[:, h, :], ALU.mult).then_inc(s["z_used"], 1)

            def l0_scaled_decay(k):
                after(dve, "tanh_ready", k)
                v.tensor_tensor(heads_first(q["dec2"]), heads_first(q["dec"]), per_head(hp[:, 0, :]), ALU.mult)
                give(s["decs_ready"])

            def l0_logits(k):
                after(dve, "logit_mm", k)
                v.tensor_copy(dist2[:, :], ps[:, SM, 320:320 + EPP])
                give(s["dist_asked"])
                v.tensor_tensor(heads_first(q["m1"]), heads_first(ps[:, SM, 0:S64]), per_head(hp[:, 3, :]), ALU.mult)
                after(dve, "decay_ready", k)
                after(dve, "dist_ready", k)
                v.tensor_tensor(heads_first(q["m2"]), per_head(hp[:, 4, :]), per_edge(dist[:, :]), ALU.mult)
                dve.drain()
                v.tensor_tensor(q["m1"], q["m1"], q["m2"], ALU.subtract)
                dve.drain()
                v.tensor_tensor(q["logit"], q["m1"], q["dec"], ALU.mult)
                dve.drain()

            def l0_begin(i, part):
                k = first_step(0) + i * RING
                for b in range(2):
                    onehots("L0", k + b, 0, i, b, part)
                    l0_types(k + b, b)
                l0_product(k, 0)
                l0_scaled_decay(k)
                l0_product(k, 1)
                l0_logits(k)
                own_maxima(k, 0)

            def l0_step(i, b, more, part):
                k = first_step(0) + i * RING + b
                i2, b2 = later(i, b, 2)
                between(k, b)
                if more > 1:
                    onehots("L0", k + 2, 0, i2, b2, part)
                    l0_types(k + 2, b2)
                if more:
                    l0_product(k + 1, 0)
                less_maxima(k, b)
                if more:
                    l0_scaled_decay(k + 1)
                    l0_product(k + 1, 1)
                rows_weighted(k, b, 0, i, part, 3 * D, D, True)
                if more:
                    l0_logits(k + 1)
                    own_maxima(k + 1, later(i, b, 1)[1])
                accumulate(k, i * RING + b, RC, True)

            turns(dve, l0_step, l0_begin, skip_steps(dve, "dve", "L0"))

            def head_means(dst):
                by_head = acc[:, :, 0:RC].rearrange("p t (h c) -> p t h c", c=HW)
                v.tensor_tensor(den, by_head[:, :, :, DH], by_head[:, :, :, DH + 1], ALU.add)
                dve.drain()
                v.tensor_scalar(den, den, 1e-30, None, ALU.max)
                dve.drain()
                v.reciprocal(den, den)
                dve.drain()
                v.tensor_tensor(dst[:, :].rearrange("p (t h c) -> p t h c", h=HEADS, c=DH), by_head[:, :, :, 0:DH],
                                den.unsqueeze(3).broadcast_to([P, NT, HEADS, DH]), ALU.mult)
                dve.drain()

            den = cols[:, 20:28, :].rearrange("p h t -> p (h t)").rearrange("p (t h) -> p t h", h=HEADS)
            part = cols[:, 28:36, :].rearrange("p h t -> p (h t)").rearrange("p (t h) -> p t h", h=HEADS)
            head_means(A)
            for t in range(2):
                v.tensor_tensor(part, acc[:, :, 0:RC].rearrange("p t (h c) -> p t h c", c=HW)[:, :, :, DH + t], den, ALU.mult)
                dve.drain()
                v.tensor_tensor(B[:, :].rearrange("p (t h c) -> p t h c", h=HEADS, c=DH),
                                relv[:, t, :].rearrange("p (h c) -> p h c", c=DH).unsqueeze(1).broadcast_to([P, NT, HEADS, DH]),
                                part.unsqueeze(3).broadcast_to([P, NT, HEADS, DH]), ALU.mult)
                dve.drain()
                v.tensor_tensor(A[:, :], A[:, :], B[:, :], ALU.add)
                dve.drain()
            give(src_ready)
            evacuate(3, B, of(X))
            v.tensor_tensor(nodes(B), nodes(B), along(V["bo"]), ALU.add)
            norm(H, B, 3, V["g1"], V["be1"])
            give(src_ready)
            evacuate(4, B, of(H))
            v.tensor_tensor(nodes(B), nodes(B), along(V["bf2"]), ALU.add)
            norm(H, B, 4, V["g2"], V["be2"])
            v.tensor_tensor(B[:, :], X[:, :], H[:, :], ALU.add)
            norm(X, B, 5)
            give(src_ready)
            evacuate(5, A, bias(V["Win_b"]))
            ask(6)
            norm(H, A, 7, V["ln_in_g"], V["ln_in_b"])
            with dve.Fori(0, LAYERS) as l:
                give(layer_used)
                dve.wait_ge(layer_in, (l + 1) * 16 * 13)
                v.tensor_scalar(attb[:, :], blk[:, :], att[:, 0:1], None, ALU.mult)
                norm(A, H, 8 + l * 3, V["ln_g"], V["ln_b"])
                give(src_ready)
                evacuate(6 + l * 3, B, bias(V["Wl_b"]))
                evacuate(7 + l * 3, C, bias(V["Wr_b"]))
                give(store_ask)
                clear("L1")

                def l1_leaky(k, h):
                    after(dve, "z_copied", k, h)
                    v.tensor_tensor(prod[:, h, :], ps[:, MM0 + h, :], chan[:, h, :], ALU.max).then_inc(s["z_used"], 1)

                def l1_logits(k):
                    after(dve, "logit_mm", k)
                    v.tensor_copy(q["logit"], ps[:, SM, 0:S64])

                def l1_begin(i, part):
                    k = first_step(1) + l * STEPS + i * RING
                    for b in range(2):
                        onehots("L1", k + b, l, i, b, part)
                    l1_leaky(k, 0)
                    l1_leaky(k, 1)
                    l1_logits(k)
                    own_maxima(k, 0)

                def l1_step(i, b, more, part):
                    k = first_step(1) + l * STEPS + i * RING + b
                    i2, b2 = later(i, b, 2)
                    between(k, b)
                    if more > 1:
                        onehots("L1", k + 2, l, i2, b2, part)
                    if more:
                        l1_leaky(k + 1, 0)
                    less_maxima(k, b)
                    if more:
                        l1_leaky(k + 1, 1)
                    rows_weighted(k, b, l + 1, i, part, D, 0, False)
                    if more:
                        l1_logits(k + 1)
                        own_maxima(k + 1, later(i, b, 1)[1])
                    accumulate(k, i * RING + b, RC, True)

                turns(dve, l1_step, l1_begin, skip_steps(dve, "dve", "L1"))
                head_means(A)
                v.tensor_tensor(nodes(A), nodes(A), along(V["conv_b"]), ALU.add)
                ask(9 + l * 3)
                dve.sem_inc(src_ready, 1)
                evacuate(8 + l * 3, B, bias(V["g2_b"]))
                ask(10 + l * 3)
                v.tensor_tensor(B[:, :], B[:, :], A[:, :], ALU.mult)
                dve.drain()
                v.tensor_tensor(H[:, :], H[:, :], B[:, :], ALU.add)
                dve.drain()
            n0 = 8 + 3 * LAYERS
            norm(A, H, n0, V["fn_g"], V["fn_b"])
            v.tensor_tensor(B[:, :], X[:, :], A[:, :], ALU.add)
            norm(X, B, n0 + 1)
            for n in range(3):
                clear("sum")
                give(store_ask)
                def sum_begin(i, part):
                    onehots("sum", first_step(1 + LAYERS + n) + i * RING, n, i, 0, part)

                def sum_step(i, b, more, part):
                    k = first_step(1 + LAYERS + n) + i * RING + b
                    i1, b1 = later(i, b, 1)
                    if more:
                        onehots("sum", k + 1, n, i1, b1, part)
                    accumulate(k, i * RING + b, D + 1, False)

                turns(dve, sum_step, sum_begin, skip_steps(dve, "dve", "sum"))
                v.tensor_scalar(col(3), acc[:, :, D], 1.0, None, ALU.max)
                dve.drain()
                v.reciprocal(col(3), col(3))
                dve.drain()
                v.tensor_tensor(nodes(A), acc[:, :, 0:D], onto(col(3)), ALU.mult)
                if n == 2:
                    dve.drain()
                    v.tensor_tensor(A[:, :], A[:, :], X[:, :], ALU.add)
                give(src_ready)
                m = 6 + 3 * LAYERS + n
                if n < 2:
                    dve.sem_inc(src_ready, 1)
                evacuate(m, B if n else H, bias(V[("L2_bl1", "L2_bl2", "L3_b")[n]]))
                if n == 2:
                    v.tensor_scalar(B[:, :], B[:, :], 0.0, None, ALU.max)
                    dve.drain()
                if n:
                    v.tensor_tensor(B[:, :], B[:, :], X[:, :], ALU.add)
                    norm(X, B, n0 + 1 + n)
            give(store_ask)


NAMES = ["x", "src_edges", "type_edges", "dst_win", "dst_ends", "type_rows", "weight_rows", "time_edges", "attr_edges",
         "c_ident", "c_iota", "c_blk", "c_misc",
         "L0_gnn_Wq", "L0_gnn_Wk", "L0_gnn_Wv", "L0_gnn_rel_q", "L0_gnn_rel_k", "L0_gnn_rel_v", "L0_gnn_Wt", "L0_gnn_bt",
         "L0_gnn_Wd1", "L0_gnn_bd1", "L0_gnn_Wd2", "L0_gnn_bd2", "L0_gnn_decay_scale", "L0_gnn_c_mag", "L0_gnn_hyp_beta",
         "L0_gnn_logit_alpha", "L0_gnn_Wo", "L0_gnn_bo", "L0_gnn_g1", "L0_gnn_be1", "L0_gnn_g2", "L0_gnn_be2",
         "L0_gnn_Wf1", "L0_gnn_bf1", "L0_gnn_Wf2", "L0_gnn_bf2",
         "L1_gnn_Win_w", "L1_gnn_Win_b", "L1_gnn_ln_in_g", "L1_gnn_ln_in_b", "L1_gnn_ln_g", "L1_gnn_ln_b", "L1_gnn_Wl_w",
         "L1_gnn_Wl_b", "L1_gnn_Wr_w", "L1_gnn_Wr_b", "L1_gnn_We_w", "L1_gnn_att", "L1_gnn_conv_b", "L1_gnn_g1_w",
         "L1_gnn_g1_b", "L1_gnn_g2_w", "L1_gnn_g2_b", "L1_gnn_fn_g", "L1_gnn_fn_b",
         "L2_gnn_Wl1_T", "L2_gnn_bl1", "L2_gnn_Wr1_T", "L2_gnn_Wl2_T", "L2_gnn_bl2", "L2_gnn_Wr2_T", "L3_gnn_W_T", "L3_gnn_b"]


def lay_out(inputs):
    import numpy as np

    a = {k: np.asarray(v) for k, v in inputs.items()}
    extra = NCH * CHUNK - E

    def padded(v, fill=0):
        return np.concatenate([v, np.full((extra,) + v.shape[1:], fill, v.dtype)])

    def by_partition(v):
        return np.ascontiguousarray(padded(v).reshape(NCH, P, EPP))

    def by_tile(v):
        w = padded(v).reshape(NCH, P, EPP, v.shape[1])
        return np.ascontiguousarray(w.transpose(0, 3, 2, 1)).reshape(NCH, v.shape[1], CHUNK)

    o = dict(a)
    o["x"] = np.concatenate([a["x"], np.zeros((NP - N, D), a["x"].dtype)])
    o["src_edges"] = by_partition(a["src"])
    dst = padded(a["dst"], N)
    around = np.concatenate([np.full(1, -1, dst.dtype), dst, np.full(1, -1, dst.dtype)])
    windows = [around[k:k + NCH * CHUNK:EPP].reshape(NCH, P) for k in range(EPP + 2)]
    o["dst_win"] = np.ascontiguousarray(np.stack(windows, axis=-1).transpose(1, 0, 2))
    o["dst_ends"] = np.ascontiguousarray(dst.reshape(NCH, CHUNK)[:, [0, CHUNK - 1]].T)
    o["type_edges"] = by_partition(a["edge_type_2"])
    o["type_rows"] = by_tile(a["edge_type_2"][:, None])[:, 0]
    o["weight_rows"] = by_tile(a["edge_weight"][:, None])[:, 0]
    o["time_edges"] = by_tile(a["edge_attr_32"])
    o["attr_edges"] = by_tile(a["edge_attr_3"])
    o["L1_gnn_att"] = a["L1_gnn_att"].reshape(LAYERS, D, 1)
    o["L1_gnn_g1_b"] = a["L1_gnn_g1_b"].reshape(LAYERS, 64, 1)
    o["L0_gnn_c_mag"] = a["L0_gnn_c_mag"].reshape(1)
    for n in ("Wl1", "Wr1", "Wl2", "Wr2"):
        o[f"L2_gnn_{n}_T"] = np.ascontiguousarray(a["L2_gnn_" + n].T)
    o["L3_gnn_W_T"] = np.ascontiguousarray(a["L3_gnn_W"].T)
    p = np.arange(P)
    o["c_ident"] = np.eye(P, dtype=np.float32)
    o["c_iota"] = np.ascontiguousarray(np.broadcast_to(np.arange(2 * P, dtype=np.float32), (P, 2 * P)))
    o["c_blk"] = (p[:, None] // DH == np.arange(HEADS)).astype(np.float32)
    misc = np.zeros((P, 8), np.float32)
    misc[:, 0] = p
    misc[0, 1] = 1
    misc[:, 2] = 1
    misc[96:98, 3] = (1, -1)
    misc[96:98, 4] = (0, 1)
    o["c_misc"] = misc
    return {n: o[n] for n in NAMES}


def program(nc, arrays):
    a = {n: nc.dram_tensor("in_" + n, v.shape, mybir.dt.from_np(v.dtype), kind="ExternalInput").ap() for n, v in arrays.items()}
    out = nc.dram_tensor("out_nodes", (N, D), F32, kind="ExternalOutput").ap()
    build(nc, a, out)


def kernel(**inputs):
    import concourse.bacc as bacc
    from concourse.bass_utils import run_bass_kernel_spmd

    arrays = lay_out(inputs)
    nc = bacc.Bacc("TRN2", target_bir_lowering=False, num_devices=1)
    program(nc, arrays)
    r = run_bass_kernel_spmd(nc, [{"in_" + n: v for n, v in arrays.items()}], core_ids=[0])
    return r.results[0]["out_nodes"]
```

```python
from contextlib import ExitStack

import concourse.bass as bass
import concourse.mybir as mybir

F32 = mybir.dt.float32
I32 = mybir.dt.int32
ALU = mybir.AluOpType
ACT = mybir.ActivationFunctionType
AX = mybir.AxisListType.X

P = 128
D = 128
N = 3125
E = 103125
HEADS = 8
DH = D // HEADS
LAYERS = 4
EPP = 8
CHUNK = P * EPP
NCH = -(-E // CHUNK)
LAST_WIN = N // P
NT = LAST_WIN + 2
NP = NT * P
STEPS = NCH + N // P
RING = 3
STEPS += -STEPS % RING
TURNS = STEPS // RING
ALWAYS = -(-NCH // RING)
HALF = 4 * P
HW = DH + 2
AW = HEADS * HW + HEADS
RC = HEADS * HW
NEG = -1.0e30
PK = 5 * EPP
GROUPS = [(g * 4, min(4, NT - g * 4)) for g in range(-(-NT // 4))]
NG = len(GROUPS)
SUMW = D + 2
ID_LOADS = {"L0": 2, "L1": 2, "sum": 1}
LOADS = {"L0": 8, "L1": 5, "sum": 3}
GATHERS = {"L0": EPP + 1, "L1": EPP + 1, "sum": EPP}
PI = 3.141592653589793

OHT0, TR0, MM0, SM, AGG, HID0 = 0, 0, 2, 5, 6, 4


def build(nc, a, out):
    ctx = ExitStack()
    with ctx:
        def sb(name, shape, dt=F32):
            return ctx.enter_context(nc.sbuf_tensor(name, shape, dt))

        def sem(name):
            return ctx.enter_context(nc.semaphore(name))

        def dram(name, shape, dt=F32):
            return nc.dram_tensor(name, shape, dt, kind="Internal").ap()

        kvm_tab = dram("kvm_tab", (NP, 3 * D))
        qm_tab = dram("qm_tab", (NP, 2 * D))
        xl_tab = dram("xl_tab", (NP, D))
        xr_tab = dram("xr_tab", (NP, D))
        pk_tab = dram("pk_tab", (NCH, P, PK))
        g_tab = dram("g_tab", (2, P, P))
        step_tab = dram("step_tab", (P, 2), I32)
        node_tab = dram("node_tab", (P, P))
        place_tab = dram("place_tab", (P, P, 3), I32)

        def node_buf(name):
            return sb(name, [P, NT * D])

        X, H, A, B, C, T = (node_buf(n) for n in ("x_nodes", "h_nodes", "a_nodes", "b_nodes", "c_nodes", "t_chans"))

        def nodes(buf):
            return buf[:, :].rearrange("p (t d) -> p t d", d=D)

        rows = [buf[:, 0:EPP * 3 * D] for buf in (A, B, C)]
        onehot_space = sb("onehot", [P, NCH * PK])
        onehot = onehot_space[:, 0:RING * EPP * P].rearrange("p (b j n) -> p b j n", b=RING, n=P)
        onehot_t = sb("onehot_t", [P, EPP * P])
        weighted = sb("weighted", [P, EPP, AW])
        acc = sb("acc", [P, NT, AW])
        src_ids = sb("src_ids", [P, RING, EPP], I32)
        type_i = sb("type_i", [P, RING, EPP], I32)
        type_f = sb("type_f", [P, RING, EPP])
        pk = sb("pk", [P, RING, PK])
        gp = sb("gp", [P, RING, P])
        win = sb("win_rows", [P, RING, 2 * D])
        win_nodes = sb("win_nodes", [P, RING, P])
        places = sb("places", [P, RING, 3], I32)
        in_tile = sb("in_tile", [P, RING, 2])
        attr = sb("attr", [P, RING, CHUNK])
        chan = sb("chan", [P, 2, HALF])
        prod = sb("prod", [P, 2, HALF])
        sq = sb("sq", [P, 2, HALF])
        dec_h = T[:, 0:2 * HALF].rearrange("p (h e) -> p h e", h=2)
        S64 = EPP * HEADS
        small = {n: sb(n, [P, S64]) for n in ("pen_f", "pen_r", "logit", "run_f", "run_r", "m1", "m2", "dec", "dec2")}
        dist2 = sb("dist2", [P, EPP])
        dist = sb("dist", [P, EPP])
        ab = sb("ab", [P, 40])
        scans = sb("scans", [P, 130])
        delta = sb("delta", [P, S64 + HEADS])
        ex = sb("ex", [P, S64 + HEADS])
        grow = sb("grow", [P, 2, HEADS])
        ident = sb("ident", [P, P])
        iota = sb("iota", [P, P])
        blk = sb("blk", [P, HEADS])
        blk4 = sb("blk4", [P, HEADS])
        misc = sb("misc", [P, 8])
        steps_i = sb("steps_i", [1, 2 * P], I32)
        steps_left = sb("steps_left", [1, 1], I32)
        cols = sb("cols", [P, 36, NT])
        one_col = sb("one_col", [P, 16])

        def mat(name, k=P, n=D):
            return sb(name, [k, n])

        W = {n: mat("w_" + n) for n in ("Wq", "Wk", "Wv", "Wo", "Win", "Wl", "Wr", "L2_Wl1", "L2_Wr1", "L2_Wl2", "L2_Wr2", "L3_W")}
        Wf1 = mat("w_f1", P, 4 * D)
        Wf2 = sb("w_f2", [P, 4, D])
        bf1 = mat("b_f1", P, 4)
        wk34 = mat("w_k34", P, D)
        relq = mat("w_relq", P, D)
        relv = sb("w_relv", [P, 2, D])
        wd1t = mat("w_d1t", P, 64)
        bd1r = mat("b_d1r", 34, 64)
        bt34 = mat("b_t34", 34, D)
        wd2 = mat("w_d2", 65, HEADS)
        hp = sb("head_params", [P, 6, HEADS])
        cm = sb("c_params", [P, 8])
        V = {n: mat("v_" + n) for n in ("bo", "g1", "be1", "g2", "be2", "bf2", "Win_b", "ln_in_g", "ln_in_b",
                                          "ln_g", "ln_b", "Wl_b", "Wr_b", "conv_b", "g2_b", "fn_g", "fn_b",
                                          "L2_bl1", "L2_bl2", "L3_b")}
        We = mat("w_e", P, D)
        att = mat("att_col", P, 1)
        attb = mat("att_blk", P, HEADS)
        g1w = mat("w_g1", P, 64)
        g1b = mat("b_g1", 64, 1)
        g2w = mat("w_g2", 64, D)

        ps = ctx.enter_context(nc.psum_tensor("ps", [P, 8, 512], F32))

        loaded = sem("loaded")
        pre_asked = sem("pre_asked")
        pre_tr = sem("pre_tr")
        pre_done = sem("pre_done")
        steps_in = sem("steps_in")
        layer_in = sem("layer_in")
        layer_used = sem("layer_used")
        src_ready = sem("src_ready")
        tr_done, tr_copied = sem("tr_done"), sem("tr_copied")
        mm_done, mm_copied = sem("mm_done"), sem("mm_copied")
        hid_mm, hid_act = sem("hid_mm"), sem("hid_act")
        ask_act, act_gave = sem("ask_act"), sem("act_gave")
        store_ask, stored = sem("store_ask"), sem("stored")
        in_ready = {n: [[sem(f"in_{n}_{part}{b}") for b in range(RING)] for part in ("main", "more")] for n in ("L0", "L1", "sum")}
        ids_in = {n: [[sem(f"ids_{n}_{part}{b}") for b in range(RING)] for part in ("main", "more")] for n in ("L0", "L1", "sum")}
        gathered = {n: [[sem(f"gathered_{n}_{part}{b}") for b in range(RING)] for part in ("main", "more")] for n in ("edges", "sum")}
        PER_STEP = {"oh_ready": 1, "oht_mm": 2, "oht_ready": 2, "z_mm": 2, "z_copied": 2, "z_used": 2, "logit_mm": 1,
                    "ab_ready": 1, "ab_mm": 1, "scan_ready": 1, "back_mm": 1, "delta_ready": 1,
                    "ex_ready": 1, "pens_ready": 1, "grow_ready": 1, "weighted_ready": 1, "agg_mm": 1, "acc_done": 1, "types_ready": 1, "qk_mm": 2, "squared": 2, "dech_mm": 2,
                    "dech_ready": 2, "dec_mm": 1, "tanh_ready": 1, "decs_ready": 1, "decay_ready": 1, "dist_asked": 1, "dist_ready": 1}
        s = {n: sem(n) for n in PER_STEP}
        OF = {"sp": (), "act": ("oht_ready", "z_copied", "ex_ready", "pens_ready", "grow_ready", "squared", "dech_ready", "tanh_ready", "decay_ready", "dist_ready"),
              "pe": ("oht_mm", "z_mm", "logit_mm", "ab_mm", "back_mm", "agg_mm", "qk_mm", "dech_mm", "dec_mm"),
              "dve": ("oh_ready", "z_used", "ab_ready", "scan_ready", "delta_ready", "weighted_ready", "acc_done",
                      "types_ready", "decs_ready", "dist_asked")}

        def start_up(eng, who):
            for n in OF[who]:
                eng.sem_inc(s[n], RING * PER_STEP[n])

        def after(eng, name, k, part=None):
            n = PER_STEP[name]
            eng.wait_ge(s[name], k * n + (n if part is None else part + 1))

        def hold(eng, which, value):
            eng.wait_ge(which, value)
            eng.nop(nofuse=True)

        def first_step(edge_pass):
            return edge_pass * STEPS + RING

        def later(i, b, n):
            return i + (b + n) // RING, (b + n) % RING

        nothing = lambda i, section: None

        def turns(eng, one, begin=nothing, skip=None):
            def some(first, end, section):
                begin(first, section)
                with eng.Fori(first, end - 1) as i:
                    for b in range(RING):
                        one(i, b, 3, section)
                for b in range(RING):
                    one(end - 1, b, RING - 1 - b, section)

            some(0, ALWAYS, 0)
            left = eng.value_load(steps_left[0:1, 0:1], min_val=0, max_val=1)
            with eng.If(left > 0):
                some(ALWAYS, TURNS, 1)
            if skip:
                with eng.Else():
                    skip()

        SKIPPED = (TURNS - ALWAYS) * RING
        L0_ONLY = ("qk_mm", "squared", "dech_ready", "tanh_ready", "decay_ready", "dist_ready", "dech_mm", "dec_mm", "types_ready", "decs_ready", "dist_asked")

        def skip_steps(eng, who, kind):
            def skip():
                eng.drain()
                for n in OF[who]:
                    if kind == "L0" or kind == "L1" and n not in L0_ONLY or n in ("oh_ready", "acc_done", "agg_mm"):
                        eng.sem_inc(s[n], SKIPPED * PER_STEP[n])
            return skip

        def count(passes, i, more_turns):
            return passes * (TURNS - ALWAYS) + i - ALWAYS + 1 if more_turns else passes * ALWAYS + i + 1


        bcast = lambda ap: ap.partition_broadcast(P)
        vec = lambda name: bcast(a[name])
        lvec = lambda name, l: bcast(a[name][l])
        const_loads = [
            (ident[:, :], a["c_ident"]), (iota[:, :], a["c_iota"]), (blk[:, :], a["c_blk"]),
            (misc[:, :], a["c_misc"]),
            (X[:, :].rearrange("p (t d) -> p t d", d=D), a["x"].rearrange("(t p) d -> p t d", p=P)),
            (Wf1[:, :], a["L0_gnn_Wf1"]), (Wf2[:, :, :], a["L0_gnn_Wf2"].rearrange("(p k) n -> p k n", p=P)),
            (bf1[:, :], a["L0_gnn_bf1"].rearrange("(p k) -> p k", p=P)),
            (relv[:, 0, :], bcast(a["L0_gnn_rel_v"][0])), (relv[:, 1, :], bcast(a["L0_gnn_rel_v"][1])),
            (bd1r[32:34, :], a["L0_gnn_bd1"].partition_broadcast(2)),
            (bt34[32:34, :], a["L0_gnn_bt"].partition_broadcast(2)),
            (wd2[0:64, :], a["L0_gnn_Wd2"]), (wd2[64:65, :], a["L0_gnn_bd2"].partition_broadcast(1)),
            (hp[:, 0, :], vec("L0_gnn_decay_scale")), (hp[:, 1, :], vec("L0_gnn_hyp_beta")),
            (hp[:, 2, :], vec("L0_gnn_logit_alpha")),
            (cm[:, 0:1], bcast(a["L0_gnn_c_mag"])),
        ]
        row_loads = [
            (wk34[0:32, :], a["L0_gnn_Wt"]), (wk34[32:33, :], a["L0_gnn_rel_k"][1:2]),
            (wk34[33:34, :], a["L0_gnn_rel_k"][0:1]),
            (relq[32:33, :], a["L0_gnn_rel_q"][1:2]), (relq[33:34, :], a["L0_gnn_rel_q"][0:1]),
            (wd1t[32:33, :], a["L0_gnn_Wd1"][1:2]), (wd1t[34:35, :], a["L0_gnn_Wd1"][0:1]),
        ]
        for n in ("Wq", "Wk", "Wv", "Wo"):
            const_loads.append((W[n][:, :], a["L0_gnn_" + n]))
        const_loads.append((W["Win"][:, :], a["L1_gnn_Win_w"]))
        for n in ("Wl1", "Wr1", "Wl2", "Wr2"):
            const_loads.append((W["L2_" + n][:, :], a["L2_gnn_" + n + "_T"]))
        const_loads.append((W["L3_W"][:, :], a["L3_gnn_W_T"]))
        for n in ("bo", "g1", "be1", "g2", "be2", "bf2"):
            const_loads.append((V[n][:, :], vec("L0_gnn_" + n)))
        for n in ("Win_b", "ln_in_g", "ln_in_b", "fn_g", "fn_b"):
            const_loads.append((V[n][:, :], vec("L1_gnn_" + n)))
        for n in ("bl1", "bl2"):
            const_loads.append((V["L2_" + n][:, :], vec("L2_gnn_" + n)))
        const_loads.append((V["L3_b"][:, :], vec("L3_gnn_b")))

        dst_i = T[:, 0:NCH * (EPP + 2)].bitcast(I32).rearrange("p (c k) -> p c k", k=EPP + 2)
        dst_f = A[:, 0:NCH * (EPP + 2)].rearrange("p (c k) -> p c k", k=EPP + 2)
        same = B[:, 0:NCH * (EPP + 1)].rearrange("p (c k) -> p c k", k=EPP + 1)
        pk_all = onehot_space[:, :].rearrange("p (c k) -> p c k", k=PK)
        g_all = C[:, 0:2 * NCH].rearrange("p (g c) -> p g c", g=2)
        g_out = C[:, 1024:1024 + 2 * P].rearrange("p (g c) -> p g c", g=2)
        node_out = C[:, 1536:1536 + P]
        place_out = C[:, 1792:1792 + 3 * P].bitcast(I32).rearrange("p (n k) -> p n k", k=3)
        types_all = H[:, 0:NCH * EPP].bitcast(I32)
        ends_i = H[:, 1024:1024 + 2 * NCH].bitcast(I32).rearrange("p (g c) -> p g c", g=2)
        ends = H[:, 1280:1280 + 16 * P].rearrange("p (g c) -> p g c", g=16)
        pre_loads = [
            (dst_i, a["dst_win"]), (types_all.rearrange("p (c k) -> p c k", k=EPP), a["type_edges"].rearrange("c p k -> p c k")),
            (ends_i, a["dst_ends"].partition_broadcast(P)),
        ]

        block = ctx.enter_context(nc.Block())

        @block.sync
        def _(sp):
            for dst_ap, src_ap in const_loads + pre_loads:
                sp.dma_start(dst_ap, src_ap).then_inc(loaded, 16)
            sp.wait_ge(pre_asked, 1)
            for dst_ap, src_ap in row_loads:
                sp.dma_start(dst_ap, src_ap).then_inc(loaded, 16)
            sp.wait_ge(pre_asked, 3)
            sp.dma_start(pk_tab.rearrange("c p k -> p c k"), pk_all).then_inc(pre_done, 16)
            sp.dma_start(g_tab.rearrange("g c p -> c g p")[0:NCH], g_out[0:NCH]).then_inc(pre_done, 16)
            sp.dma_start(step_tab, ends[:, 15, 0:2].bitcast(I32)).then_inc(pre_done, 16)
            sp.dma_start(node_tab, node_out).then_inc(pre_done, 16)
            sp.dma_start(place_tab, place_out).then_inc(pre_done, 16)
            sp.wait_ge(pre_done, 5 * 16)
            sp.dma_start(steps_i[:, :], step_tab.rearrange("p k -> (p k)").partition_broadcast(1)).then_inc(steps_in, 16)

            def step_inputs(kind, k, turn, b, section):
                r = turn * RING + b
                if kind == "sum":
                    hold(sp, s["acc_done"], k - RING + 1)
                else:
                    hold(sp, s["z_mm"], (k - RING + 1) * PER_STEP["z_mm"])
                c = sp.value_load(steps_i[0:1, bass.ds(r * 2, 1)], min_val=0, max_val=NCH - 1)
                ready = in_ready[kind][section][b]
                places_in = ready if kind == "sum" else ids_in[kind][section][b]
                sp.dma_start(src_ids[:, b, :], a["src_edges"][c]).then_inc(ids_in[kind][section][b], 16)
                sp.dma_start(places[:, b, :], place_tab[r]).then_inc(places_in, 16)
                if kind != "sum":
                    hold(sp, s["delta_ready"], k - RING + 1)
                sp.dma_start(pk[:, b, :], pk_tab[c]).then_inc(ready, 16)
                sp.dma_start(win_nodes[:, b, :], node_tab[r].partition_broadcast(P)).then_inc(ready, 16)
                if kind == "sum":
                    return
                for g in range(2):
                    sp.dma_start(gp[32 * g:32 * g + HEADS, b, :], g_tab[g, c].partition_broadcast(HEADS)).then_inc(ready, 16)
                if kind == "L0":
                    sp.dma_start(attr[0:32, b, :], a["time_edges"][c]).then_inc(ready, 16)
                    sp.dma_start(attr[96:98, b, :].bitcast(I32), a["type_rows"][c].partition_broadcast(2)).then_inc(ready, 16)
                    sp.dma_start(type_i[:, b, :], a["type_edges"][c]).then_inc(ready, 16)
                    sp.dma_start(attr[34:35, b, :], a["weight_rows"][c].partition_broadcast(1)).then_inc(ready, 16)
                else:
                    sp.dma_start(attr[0:3, b, :], a["attr_edges"][c]).then_inc(ready, 16)

            sp.wait_ge(steps_in, 16)
            sp.wait_ge(store_ask, 1)
            for i, buf in enumerate((A, B, C)):
                sp.dma_start(kvm_tab.rearrange("(t p) d -> p t d", p=P)[:, :, i * D:(i + 1) * D], nodes(buf)).then_inc(stored, 16)
            for i, buf in enumerate((H, T)):
                sp.dma_start(qm_tab.rearrange("(t p) d -> p t d", p=P)[:, :, i * D:(i + 1) * D], nodes(buf)).then_inc(stored, 16)
            sp.wait_ge(stored, 5 * 16)
            turns(sp, lambda i, b, more, section: step_inputs("L0", first_step(0) + i * RING + b, i, b, section))

            with sp.Fori(0, LAYERS) as l:
                hold(sp, layer_used, l + 1)
                for dst_ap, src_ap in (
                    (W["Wl"][:, :], a["L1_gnn_Wl_w"][l]), (W["Wr"][:, :], a["L1_gnn_Wr_w"][l]), (We[0:3, :], a["L1_gnn_We_w"][l]),
                    (att[:, :], a["L1_gnn_att"][l]), (g1w[:, :], a["L1_gnn_g1_w"][l]), (g1b[:, :], a["L1_gnn_g1_b"][l]),
                    (g2w[:, :], a["L1_gnn_g2_w"][l]), (V["ln_g"][:, :], lvec("L1_gnn_ln_g", l)), (V["ln_b"][:, :], lvec("L1_gnn_ln_b", l)),
                    (V["Wl_b"][:, :], lvec("L1_gnn_Wl_b", l)), (V["Wr_b"][:, :], lvec("L1_gnn_Wr_b", l)),
                    (V["conv_b"][:, :], lvec("L1_gnn_conv_b", l)), (V["g2_b"][:, :], lvec("L1_gnn_g2_b", l))):
                    sp.dma_start(dst_ap, src_ap).then_inc(layer_in, 16)
                hold(sp, store_ask, l + 2)
                sp.dma_start(xl_tab.rearrange("(t p) d -> p t d", p=P), nodes(B)).then_inc(stored, 16)
                sp.dma_start(xr_tab.rearrange("(t p) d -> p t d", p=P), nodes(C)).then_inc(stored, 16)
                hold(sp, stored, (l + 1) * 32 + 5 * 16)
                turns(sp, lambda i, b, more, section: step_inputs("L1", first_step(1) + l * STEPS + i * RING + b, i, b, section))

            for n, buf in enumerate((X, H, X)):
                sp.wait_ge(store_ask, 2 + LAYERS + n)
                sp.dma_start(xl_tab.rearrange("(t p) d -> p t d", p=P), nodes(buf)).then_inc(stored, 16)
                sp.wait_ge(stored, 5 * 16 + LAYERS * 32 + (n + 1) * 16)
                turns(sp, lambda i, b, more, section: step_inputs("sum", first_step(1 + LAYERS + n) + i * RING + b, i, b, section))

            sp.wait_ge(store_ask, 2 + LAYERS + 3)
            sp.dma_start(out[0:LAST_WIN * P].rearrange("(t p) d -> p t d", p=P), nodes(X)[:, 0:LAST_WIN, :]).then_inc(stored, 16)
            sp.dma_start(out[LAST_WIN * P:N], X[0:N - LAST_WIN * P, LAST_WIN * D:(LAST_WIN + 1) * D]).then_inc(stored, 16)
            sp.wait_ge(stored, 5 * 16 + LAYERS * 32 + 3 * 16 + 32)

        @block.gpsimd
        def _(pool):
            def gather(kind, k, table, width, passes, i, b, section, pitch=None):
                pitch = pitch or width
                hold(pool, ids_in[kind][section][b], count(passes, i, section) * 16 * ID_LOADS[kind])
                if kind != "sum":
                    hold(pool, s["weighted_ready"], k - RING + 1)
                done = gathered["sum" if kind == "sum" else "edges"][section][b]
                if kind != "sum":
                    own, own_width = (qm_tab, 2 * D) if kind == "L0" else (xr_tab, D)
                    pool.indirect_dma_start(win[:, b, 0:own_width], None, own,
                                            bass.IndirectOffsetOnAxis(ap=places[:, b, 0:1], axis=0)).then_inc(done, 16)
                for j in range(EPP):
                    pool.indirect_dma_start(rows[b][:, j * pitch:j * pitch + width], None, table,
                                            bass.IndirectOffsetOnAxis(ap=src_ids[:, b, j:j + 1], axis=0)).then_inc(done, 16)

            turns(pool, lambda i, b, more, section: gather("L0", first_step(0) + i * RING + b, kvm_tab, 3 * D, 0, i, b, section))
            with pool.Fori(0, LAYERS) as l:
                turns(pool, lambda i, b, more, section: gather("L1", first_step(1) + l * STEPS + i * RING + b, xl_tab, D, l, i, b, section))
            for n in range(3):
                turns(pool, lambda i, b, more, section: gather("sum", None, xl_tab, D, n, i, b, section, SUMW))

        @block.scalar
        def _(act):
            start_up(act, "act")

            def copy_turned(n):
                for g, (t0, nt) in enumerate(GROUPS):
                    act.wait_ge(tr_done, n * NG + g + 1)
                    act.copy(T[:, t0 * D:(t0 + nt) * D], ps[:, TR0 + g % 2, 0:nt * D]).then_inc(tr_copied, 1)

            def asked(n):
                act.wait_ge(ask_act, n + 1)

            col = lambda i: cols[:, i, :]
            asked(0)
            act.activation(hp[:, 3, :], hp[:, 2, :], ACT.Sigmoid)
            act.activation(cm[:, 2:3], cm[:, 1:2], ACT.Sqrt)
            act.activation(col(1), col(0), ACT.Sqrt).then_inc(act_gave, 1)
            asked(1)
            act.activation(col(7), col(3), ACT.Tanh)
            act.activation(col(8), col(4), ACT.Sin)
            act.activation(col(9), col(5), ACT.Sin).then_inc(act_gave, 1)
            asked(2)
            act.activation(col(13), col(12), ACT.Sqrt).then_inc(act_gave, 1)
            copy_turned(0)

            def step_turned(k):
                for h in range(2):
                    after(act, "oht_mm", k, h)
                    act.copy(onehot_t[:, h * HALF:(h + 1) * HALF], ps[:, OHT0 + h, :]).then_inc(s["oht_ready"], 1)

            def penalties(kind, k, passes, i, b, section):
                act.wait_ge(in_ready[kind][section][b], count(passes, i, section) * 16 * LOADS[kind])
                for n, name in enumerate(("pen_f", "pen_r")):
                    ins = act.copy(small[name][:, :].rearrange("p (h j) -> p h j", j=EPP),
                                   pk[:, b, (n + 1) * EPP:(n + 2) * EPP].unsqueeze(1).broadcast_to([P, HEADS, EPP]))
                ins.then_inc(s["pens_ready"], 1)

            def growths(k, b):
                after(act, "agg_mm", k)
                for t in range(2):
                    ins = act.activation(grow[:, t, :], ps[:, AGG, RC:AW], ACT.Identity, bias=one_col[:, 0:1], scale=in_tile[:, b, t:t + 1])
                ins.then_inc(s["grow_ready"], 1)

            def exps(k):
                after(act, "delta_ready", k)
                act.activation(ex[:, :], delta[:, :], ACT.Exp).then_inc(s["ex_ready"], 1)

            def l0_relu(k):
                for h in range(2):
                    after(act, "dech_mm", k, h)
                    act.activation(dec_h[0:64, h, :], ps[0:64, OHT0 + h, :], ACT.Relu).then_inc(s["dech_ready"], 1)

            def l0_keys(k, h):
                after(act, "qk_mm", k, h)
                act.copy(chan[:, h, :], ps[:, MM0 + 1, :]).then_inc(s["z_copied"], 1)

            def l0_squares(k, h):
                after(act, "z_mm", k, h)
                act.activation(sq[:, h, :], ps[:, MM0 + 2, :], ACT.Square).then_inc(s["squared"], 1)

            def l0_tanh(k):
                after(act, "dec_mm", k)
                act.activation(small["dec"][:, :], ps[:, OHT0, 0:S64], ACT.Tanh).then_inc(s["tanh_ready"], 1)

            def l0_decay(k):
                after(act, "decs_ready", k)
                act.activation(small["dec"][:, :], small["dec2"][:, :], ACT.Exp).then_inc(s["decay_ready"], 1)

            def l0_dist(k):
                after(act, "dist_asked", k)
                act.activation(dist[:, :], dist2[:, :], ACT.Sqrt).then_inc(s["dist_ready"], 1)

            def l0_begin(i, section):
                k = first_step(0) + i * RING
                penalties("L0", k, 0, i, 0, section)
                step_turned(k)
                l0_relu(k)
                l0_keys(k, 0)
                l0_squares(k, 0)
                l0_tanh(k)
                l0_keys(k, 1)
                l0_squares(k, 1)
                l0_decay(k)
                step_turned(k + 1)
                l0_dist(k)

            def l0_step(i, b, more, section):
                k = first_step(0) + i * RING + b
                if more:
                    l0_relu(k + 1)
                    l0_keys(k + 1, 0)
                exps(k)
                if more:
                    i1, b1 = later(i, b, 1)
                    penalties("L0", k + 1, 0, i1, b1, section)
                    l0_squares(k + 1, 0)
                    l0_tanh(k + 1)
                    l0_keys(k + 1, 1)
                    l0_squares(k + 1, 1)
                    l0_decay(k + 1)
                if more > 1:
                    step_turned(k + 2)
                if more:
                    l0_dist(k + 1)
                growths(k, b)

            turns(act, l0_step, l0_begin, skip_steps(act, "act", "L0"))

            copy_turned(1)
            asked(3)
            act.activation(col(2), col(1), ACT.Sqrt).then_inc(act_gave, 1)
            copy_turned(2)
            for g, (t0, nt) in enumerate(GROUPS):
                act.wait_ge(hid_mm, g + 1)
                if g:
                    act.wait_ge(mm_done, 4 * NG + g)
                for c in range(4):
                    ins = act.activation(A[:, c * 512:c * 512 + nt * D], ps[:, HID0 + c, 0:nt * D], ACT.Gelu, bias=bf1[:, c:c + 1])
                ins.then_inc(hid_act, 1)
            for n in (4, 5):
                asked(n)
                act.activation(col(2), col(1), ACT.Sqrt).then_inc(act_gave, 1)
            copy_turned(3)
            asked(6)
            act.activation(A[:, :], A[:, :], ACT.Gelu_apprx_tanh).then_inc(act_gave, 1)
            asked(7)
            act.activation(col(2), col(1), ACT.Sqrt).then_inc(act_gave, 1)
            with act.Fori(0, LAYERS) as l:
                asked(8 + l * 3)
                act.activation(col(2), col(1), ACT.Sqrt).then_inc(act_gave, 1)
                copy_turned(4 + l * 2)

                def l1_scaled(k, h):
                    after(act, "z_mm", k, h)
                    act.activation(chan[:, h, :], ps[:, MM0 + h, :], ACT.Copy, scale=0.2).then_inc(s["z_copied"], 1)

                def l1_begin(i, section):
                    k = first_step(1) + l * STEPS + i * RING
                    penalties("L1", k, l, i, 0, section)
                    step_turned(k)
                    l1_scaled(k, 0)
                    l1_scaled(k, 1)
                    step_turned(k + 1)

                def l1_step(i, b, more, section):
                    k = first_step(1) + l * STEPS + i * RING + b
                    if more:
                        l1_scaled(k + 1, 0)
                    exps(k)
                    if more:
                        i1, b1 = later(i, b, 1)
                        penalties("L1", k + 1, l, i1, b1, section)
                        l1_scaled(k + 1, 1)
                    if more > 1:
                        step_turned(k + 2)
                    growths(k, b)

                turns(act, l1_step, l1_begin, skip_steps(act, "act", "L1"))
                asked(9 + l * 3)
                act.activation(A[:, :], A[:, :], ACT.Gelu_apprx_tanh).then_inc(act_gave, 1)
                copy_turned(5 + l * 2)
                for g, (t0, nt) in enumerate(GROUPS):
                    act.wait_ge(hid_mm, NG + l * NG + g + 1)
                    act.activation(C[0:64, t0 * D:(t0 + nt) * D], ps[0:64, HID0 + g % 2, 0:nt * D], ACT.Gelu_apprx_tanh,
                                   bias=g1b[:, 0:1]).then_inc(hid_act, 1)
                asked(10 + l * 3)
                act.activation(B[:, :], B[:, :], ACT.Sigmoid).then_inc(act_gave, 1)
            n0 = 8 + 3 * LAYERS
            for n in (n0, n0 + 1):
                asked(n)
                act.activation(col(2), col(1), ACT.Sqrt).then_inc(act_gave, 1)
            for n in range(3):
                t = 4 + 2 * LAYERS
                if n < 2:
                    for g, (t0, nt) in enumerate(GROUPS):
                        act.wait_ge(tr_done, (t + 2 * n) * NG + g + 1)
                        act.copy(T[:, t0 * D:(t0 + nt) * D], ps[:, TR0 + g % 2, 0:nt * D]).then_inc(tr_copied, 1)
                    for g, (t0, nt) in enumerate(GROUPS):
                        act.wait_ge(tr_done, (t + 2 * n + 1) * NG + g + 1)
                        act.copy(C[:, t0 * D:(t0 + nt) * D], ps[:, TR0 + g % 2, 0:nt * D]).then_inc(tr_copied, 1)
                else:
                    copy_turned(t + 4)
                if n:
                    asked(n0 + 1 + n)
                    act.activation(col(2), col(1), ACT.Sqrt).then_inc(act_gave, 1)

        @block.tensor
        def _(pe):
            start_up(pe, "pe")
            pe.wait_ge(loaded, 16 * len(const_loads + pre_loads + row_loads))

            def turn(n, buf):
                pe.wait_ge(src_ready, n + 1)
                for g, (t0, nt) in enumerate(GROUPS):
                    if g >= 2:
                        pe.wait_ge(tr_copied, n * NG + g - 1)
                    elif g == 0 and not (isinstance(n, int) and n == 0):
                        pe.wait_ge(tr_copied, n * NG)
                    for t in range(nt):
                        ins = pe.transpose(ps[:, TR0 + g % 2, t * D:(t + 1) * D], buf[:, (t0 + t) * D:(t0 + t + 1) * D], ident[:, :])
                    ins.then_inc(tr_done, 1)

            def product(n, pairs, turned):
                for g, (t0, nt) in enumerate(GROUPS):
                    pe.wait_ge(tr_copied, turned * NG + g + 1)
                    if g >= 2:
                        pe.wait_ge(mm_copied, n * NG + g - 1)
                    elif g == 0 and not (isinstance(n, int) and n == 0):
                        pe.wait_ge(mm_copied, n * NG)
                    for t in range(nt):
                        for i, (buf, w) in enumerate(pairs):
                            ins = pe.matmul(ps[:, MM0 + g % 2, t * D:(t + 1) * D], buf[:, (t0 + t) * D:(t0 + t + 1) * D], w[:, :],
                                            start=i == 0, stop=i == len(pairs) - 1)
                    ins.then_inc(mm_done, 1)

            def onehots_turned(kind, k, b):
                after(pe, "oh_ready", k)
                for h in range(2):
                    after(pe, "oht_ready", k - 1, h)
                    if kind == "L0" and h == 0:
                        after(pe, "tanh_ready", k - 1)
                    for r in range(4):
                        ins = pe.transpose(ps[:, OHT0 + h, r * P:(r + 1) * P], onehot[:, b, h * 4 + r, :], ident[:, :])
                    ins.then_inc(s["oht_mm"], 1)

            def spread(bank, b, h, c0, begins=False):
                return pe.matmul(ps[:, bank, :], win[:, b, c0:c0 + D], onehot_t[:, h * HALF:(h + 1) * HALF],
                                 start=begins, stop=not begins, skip_group_check=not begins)

            def add_rows(bank, b, h, width, c0):
                for r in range(4):
                    j = h * 4 + r
                    ins = pe.matmul(ps[:, bank, r * P:(r + 1) * P], rows[b][:, j * width + c0:j * width + c0 + D], ident[:, :],
                                    start=r == 0, stop=False, skip_group_check=True)

            def ends_turned(k):
                after(pe, "ab_ready", k)
                pe.nop(nofuse=True)
                pe.transpose(ps[0:40, SM, 64:192], ab[:, :], ident[:, :]).then_inc(s["ab_mm"], 1)

            def maxima_turned(k):
                after(pe, "scan_ready", k)
                pe.nop(nofuse=True)
                pe.transpose(ps[:, SM, 192:232], scans[0:40, 1:129], ident[0:40, 0:40]).then_inc(s["back_mm"], 1)

            def aggregate(k, b, width, src, ready, between=None):
                ready()
                for j in reversed(range(EPP)):
                    n = width if j == 0 else min(width, RC)
                    ins = pe.matmul(ps[:, AGG, 0:n], onehot[:, b, j, :], src(j, n), start=j == EPP - 1, stop=j == 0, skip_group_check=True)
                    if between and j == 2:
                        between()
                ins.then_inc(s["agg_mm"], 1)

            pe.wait_ge(pre_asked, 2)
            for g in range(2):
                ins = pe.transpose(ps[0:NCH, SM, g * P:(g + 1) * P], g_all[:, g, :], ident[:, :])
            pe.transpose(ps[0:1, SM, 256:384], cm[:, 3:4], ident[:, :]).then_inc(pre_tr, 1)
            pe.wait_ge(pre_asked, 3)
            pe.matmul(ps[:, SM, 400:401], one_col[0:1, 0:1].broadcast_to([1, P]), cm[0:1, 3:4], start=True, stop=True).then_inc(pre_tr, 1)

            turn(0, X)
            for n, w in enumerate(("Wq", "Wk", "Wv")):
                product(n, [(T, W[w])], 0)

            def l0_hidden(k, b):
                after(pe, "types_ready", k)
                for h in range(2):
                    after(pe, "oht_ready", k, h)
                    pe.nop(nofuse=True)
                    pe.matmul(ps[0:64, OHT0 + h, :], wd1t[:, :], attr[:, b, h * HALF:(h + 1) * HALF], start=True, stop=True).then_inc(s["dech_mm"], 1)

            def l0_z(k, i, b, h, section):
                if h == 0:
                    hold(pe, gathered["edges"][section][b], count(0, i, section) * 16 * GATHERS["L0"])
                e = slice(h * HALF, (h + 1) * HALF)
                after(pe, "z_used", k - 1 + h, 1 - h)
                spread(MM0, b, h, 0, True)
                pe.matmul(ps[:, MM0, :], relq[:, :], attr[:, b, e], start=False, stop=True)
                add_rows(MM0 + 1, b, h, 3 * D, 0)
                pe.matmul(ps[:, MM0 + 1, :], wk34[:, :], attr[:, b, e], start=False, stop=True, skip_group_check=True).then_inc(s["qk_mm"], 1)
                after(pe, "squared", k - 1 + h, 1 - h)
                add_rows(MM0 + 2, b, h, 3 * D, 2 * D)
                spread(MM0 + 2, b, h, D).then_inc(s["z_mm"], 1)

            def l0_decays(k):
                after(pe, "dech_ready", k)
                for j in range(EPP):
                    ins = pe.matmul(ps[:, OHT0, j:S64:EPP], dec_h[0:65, j // 4, j % 4 * P:(j % 4 + 1) * P], wd2[:, :], start=True, stop=True)
                ins.then_inc(s["dec_mm"], 1)

            def l0_scores(k):
                after(pe, "z_used", k)
                after(pe, "squared", k)
                for j in range(EPP):
                    h, t = j // 4, slice(j % 4 * P, (j % 4 + 1) * P)
                    pe.matmul(ps[:, SM, j:S64:EPP], prod[:, h, t], blk4[:, :], start=True, stop=True)
                    ins = pe.matmul(ps[:, SM, 320 + j:321 + j], sq[:, h, t], misc[:, 2:3], start=True, stop=True)
                ins.then_inc(s["logit_mm"], 1)

            def weighted_sums(k, b, between=None):
                aggregate(k, b, AW, lambda j, n: weighted[:, j, 0:n], lambda: after(pe, "weighted_ready", k), between)

            def l0_begin(i, section):
                k = first_step(0) + i * RING
                onehots_turned("L0", k, 0)
                l0_hidden(k, 0)
                l0_z(k, i, 0, 0, section)
                l0_decays(k)
                l0_z(k, i, 0, 1, section)
                onehots_turned("L0", k + 1, 1)
                l0_scores(k)
                ends_turned(k)

            def l0_step(i, b, more, section):
                k = first_step(0) + i * RING + b
                i1, b1 = later(i, b, 1)
                if more:
                    l0_hidden(k + 1, b1)
                maxima_turned(k)
                if more:
                    l0_z(k + 1, i1, b1, 0, section)
                    l0_decays(k + 1)
                    l0_z(k + 1, i1, b1, 1, section)
                if more > 1:
                    onehots_turned("L0", k + 2, later(i, b, 2)[1])
                if more:
                    l0_scores(k + 1)
                weighted_sums(k, b)
                if more:
                    ends_turned(k + 1)

            turns(pe, l0_step, l0_begin, skip_steps(pe, "pe", "L0"))

            turn(1, A)
            product(3, [(T, W["Wo"])], 1)
            turn(2, H)
            for g, (t0, nt) in enumerate(GROUPS):
                pe.wait_ge(tr_copied, 2 * NG + g + 1)
                if g:
                    pe.wait_ge(hid_act, g)
                for c in range(4):
                    ins = pe.matmul(ps[:, HID0 + c, 0:nt * D], Wf1[:, c:4 * D:4], T[:, t0 * D:(t0 + nt) * D], start=True, stop=True)
                ins.then_inc(hid_mm, 1)
                pe.wait_ge(hid_act, g + 1)
                pe.wait_ge(mm_copied, 4 * NG + max(g - 1, 0))
                for t in range(nt):
                    for c in range(4):
                        ins = pe.matmul(ps[:, MM0 + g % 2, t * D:(t + 1) * D], A[:, c * 512 + t * D:c * 512 + (t + 1) * D],
                                        Wf2[:, c, :], start=c == 0, stop=c == 3)
                ins.then_inc(mm_done, 1)

            turn(3, X)
            product(5, [(T, W["Win"])], 3)
            with pe.Fori(0, LAYERS) as l:
                pe.wait_ge(layer_in, (l + 1) * 16 * 13)
                turn(4 + l * 2, A)
                product(6 + l * 3, [(T, W["Wl"])], 4 + l * 2)
                product(7 + l * 3, [(T, W["Wr"])], 4 + l * 2)

                def l1_z(k, i, b, h, section, between=None):
                    if h == 0:
                        hold(pe, gathered["edges"][section][b], count(l + 1, i, section) * 16 * GATHERS["L1"])
                        after(pe, "oht_ready", k)
                        after(pe, "z_used", k - 1)
                    add_rows(MM0 + h, b, h, D, 0)
                    if between:
                        between()
                    pe.matmul(ps[:, MM0 + h, :], We[:, :], attr[:, b, h * HALF:(h + 1) * HALF], start=False, stop=False, skip_group_check=True)
                    spread(MM0 + h, b, h, 0).then_inc(s["z_mm"], 1)

                def l1_scores(k):
                    after(pe, "delta_ready", k - 1)
                    pe.nop(nofuse=True)
                    for h in range(2):
                        after(pe, "z_used", k, h)
                        for r in range(4):
                            j = h * 4 + r
                            ins = pe.matmul(ps[:, SM, j:S64:EPP], prod[:, h, r * P:(r + 1) * P], attb[:, :], start=True, stop=True)
                    ins.then_inc(s["logit_mm"], 1)

                def l1_begin(i, section):
                    k = first_step(1) + l * STEPS + i * RING
                    onehots_turned("L1", k, 0)
                    l1_z(k, i, 0, 0, section)
                    l1_z(k, i, 0, 1, section)
                    onehots_turned("L1", k + 1, 1)
                    l1_scores(k)
                    ends_turned(k)

                def l1_step(i, b, more, section):
                    k = first_step(1) + l * STEPS + i * RING + b
                    i1, b1 = later(i, b, 1)
                    if more:
                        l1_z(k + 1, i1, b1, 0, section, lambda: maxima_turned(k))
                        l1_z(k + 1, i1, b1, 1, section)
                    else:
                        maxima_turned(k)
                    if more > 1:
                        onehots_turned("L1", k + 2, later(i, b, 2)[1])
                    if more:
                        l1_scores(k + 1)
                    weighted_sums(k, b, (lambda: ends_turned(k + 1)) if more else None)

                turns(pe, l1_step, l1_begin, skip_steps(pe, "pe", "L1"))
                turn(5 + l * 2, A)
                for g, (t0, nt) in enumerate(GROUPS):
                    pe.wait_ge(tr_copied, (5 + l * 2) * NG + g + 1)
                    if g >= 2:
                        pe.wait_ge(hid_act, NG + l * NG + g - 1)
                    pe.matmul(ps[0:64, HID0 + g % 2, 0:nt * D], g1w[:, :], T[:, t0 * D:(t0 + nt) * D], start=True, stop=True).then_inc(hid_mm, 1)
                for g, (t0, nt) in enumerate(GROUPS):
                    pe.wait_ge(hid_act, NG + l * NG + g + 1)
                    pe.wait_ge(mm_copied, (8 + l * 3) * NG + max(g - 1, 0))
                    for t in range(nt):
                        ins = pe.matmul(ps[:, MM0 + g % 2, t * D:(t + 1) * D], C[0:64, (t0 + t) * D:(t0 + t + 1) * D], g2w[:, :], start=True, stop=True)
                    ins.then_inc(mm_done, 1)

            for n in range(3):
                def sum_step(i, b, more, section):
                    k = first_step(1 + LAYERS + n) + i * RING + b

                    def ready():
                        hold(pe, gathered["sum"][section][b], count(n, i, section) * 16 * GATHERS["sum"])
                        after(pe, "oh_ready", k)
                        after(pe, "acc_done", k - 1)
                    aggregate(k, b, D + 1, lambda j, m: rows[b][:, j * SUMW:j * SUMW + D + 1], ready)

                turns(pe, sum_step, nothing, skip_steps(pe, "pe", "sum"))
                t, m = 4 + 2 * LAYERS, 6 + 3 * LAYERS
                if n < 2:
                    turn(t + 2 * n, A)
                    turn(t + 2 * n + 1, (X, H)[n])
                    product(m + n, [(T, W[f"L2_Wl{n + 1}"]), (C, W[f"L2_Wr{n + 1}"])], t + 2 * n + 1)
                else:
                    turn(t + 4, A)
                    product(m + 2, [(T, W["L3_W"])], t + 4)

        @block.vector
        def _(dve):
            start_up(dve, "dve")
            v = nc.vector
            col = lambda i: cols[:, i, :]
            onto = lambda ap: ap.unsqueeze(2).broadcast_to([P, NT, D])
            along = lambda t: t[:, :].unsqueeze(1).broadcast_to([P, NT, D])

            def ask(n):
                dve.drain().then_inc(ask_act, 1)
                dve.wait_ge(act_gave, n + 1)

            def norm(dst, src, n, gain=None, shift=None):
                dve.drain()
                v.tensor_reduce(col(0), nodes(src), AX, ALU.add)
                dve.drain()
                v.tensor_scalar(col(0), col(0), -1.0 / D, None, ALU.mult)
                dve.drain()
                v.tensor_tensor(nodes(dst), nodes(src), onto(col(0)), ALU.add)
                dve.drain()
                v.tensor_tensor(T[:, :], dst[:, :], dst[:, :], ALU.mult)
                dve.drain()
                v.tensor_reduce(col(1), nodes(T), AX, ALU.add)
                dve.drain()
                v.tensor_scalar(col(1), col(1), 1.0 / D, 1e-5, ALU.mult, ALU.add)
                ask(n)
                v.reciprocal(col(2), col(2))
                dve.drain()
                v.tensor_tensor(nodes(dst), nodes(dst), onto(col(2)), ALU.mult)
                if gain is not None:
                    dve.drain()
                    v.tensor_tensor(nodes(dst), nodes(dst), along(gain), ALU.mult)
                    dve.drain()
                    v.tensor_tensor(nodes(dst), nodes(dst), along(shift), ALU.add)
                dve.drain()

            def give(what, _n=None):
                dve.drain().then_inc(what, 1)

            def evacuate(n, dst, plus):
                for g, (t0, nt) in enumerate(GROUPS):
                    dve.wait_ge(mm_done, n * NG + g + 1)
                    o = nodes(dst)[:, t0:t0 + nt, :]
                    i = ps[:, MM0 + g % 2, 0:nt * D].rearrange("p (t d) -> p t d", d=D)
                    if plus is None:
                        v.tensor_copy(o, i).then_inc(mm_copied, 1)
                    else:
                        v.tensor_tensor(o, i, plus(t0, nt), ALU.add).then_inc(mm_copied, 1)
                dve.drain()

            bias = lambda t: (lambda t0, nt: t[:, :].unsqueeze(1).broadcast_to([P, nt, D]))
            of = lambda buf: (lambda t0, nt: nodes(buf)[:, t0:t0 + nt, :])

            v.memset(wd1t[:, :], 0.0)
            v.memset(relq[:, :], 0.0)
            v.memset(wk34[:, :], 0.0)
            v.memset(We[:, :], 0.0)
            v.memset(attr[:, :, :], 0.0)
            v.memset(ab[:, :], 0.0)
            v.memset(scans[:, :], NEG)
            v.memset(one_col[:, :], 1.0)
            v.memset(weighted[:, :, :], 0.0)
            give(pre_asked)
            dve.wait_ge(loaded, 16 * len(const_loads + pre_loads + row_loads))
            v.tensor_copy(dst_f, dst_i)
            v.tensor_copy(types_all.bitcast(F32), types_all)
            v.tensor_copy(ends[:, 0:2, 0:NCH], ends_i)
            v.memset(g_out, 0.0)
            dve.drain()
            v.tensor_tensor(same, dst_f[:, :, 1:EPP + 2], dst_f[:, :, 0:EPP + 1], ALU.is_equal)
            v.tensor_copy(pk_all[:, :, 0:EPP], dst_f[:, :, 1:EPP + 1])
            ones = lambda ap, n: ap.broadcast_to([P, NCH, n])
            v.tensor_tensor(pk_all[:, :, 3 * EPP:4 * EPP], dst_f[:, :, 1:EPP + 1], ones(dst_f[:, :, 0:1], EPP), ALU.is_equal)
            v.tensor_tensor(pk_all[:, :, 4 * EPP:5 * EPP], dst_f[:, :, 1:EPP + 1], ones(dst_f[:, :, EPP + 1:EPP + 2], EPP), ALU.is_equal)
            v.tensor_tensor(g_all[:, 0, :], dst_f[:, :, EPP], dst_f[:, :, 0], ALU.is_equal)
            v.tensor_tensor(g_all[:, 1, :], dst_f[:, :, 1], dst_f[:, :, EPP + 1], ALU.is_equal)
            dve.drain()
            pen = lambda o, i: v.tensor_scalar(o, i, -1.0, -NEG, ALU.add, ALU.mult)
            pen(pk_all[:, :, EPP:2 * EPP], same[:, :, 0:EPP])
            pen(pk_all[:, :, 2 * EPP:3 * EPP], same[:, :, 1:EPP + 1])
            pen(pk_all[:, :, 3 * EPP:5 * EPP], pk_all[:, :, 3 * EPP:5 * EPP])
            pen(g_all, g_all)
            dve.drain()
            v.memset(pk_all[:, :, EPP:EPP + 1], NEG)
            v.memset(pk_all[:, :, 3 * EPP - 1:3 * EPP], NEG)
            E_ = lambda i: ends[:, i, 0:NCH]
            Ei = lambda i: ends[:, i, 0:NCH].bitcast(I32)
            v.tensor_tensor(E_(4), E_(1), E_(0), ALU.subtract)
            dve.drain()
            v.tensor_copy(Ei(5), E_(4))
            dve.drain()
            v.tensor_scalar(Ei(5), Ei(5), 7, None, ALU.arith_shift_right)
            dve.drain()
            v.tensor_copy(E_(6), Ei(5))
            dve.drain()
            v.tensor_scalar(E_(6), E_(6), 1.0, None, ALU.add)
            v.memset(E_(7), 1.0)
            dve.drain()
            v.tensor_tensor_scan(E_(8), E_(7), E_(6), 0.0, ALU.mult, ALU.add)
            dve.drain()
            v.tensor_tensor(E_(9), E_(8), E_(6), ALU.subtract)
            dve.drain()
            v.tensor_scalar(E_(10), E_(9), misc[:, 0:1], None, ALU.is_le)
            v.tensor_scalar(E_(11), E_(9), -float(P), None, ALU.mult)
            dve.drain()
            v.tensor_tensor(E_(11), E_(11), E_(0), ALU.add)
            v.tensor_copy(E_(12), E_(10))
            dve.drain()
            v.tensor_tensor(ends[:, 12, 0:NCH - 1], ends[:, 10, 0:NCH - 1], ends[:, 10, 1:NCH], ALU.subtract)
            v.tensor_reduce(ends[:, 14, 0:1], E_(10), AX, ALU.add)
            dve.drain()
            v.tensor_tensor(E_(13), E_(12), E_(11), ALU.mult)
            v.tensor_scalar(ends[:, 14, 0:1], ends[:, 14, 0:1], -1.0, None, ALU.add)
            dve.drain()
            v.tensor_reduce(ends[:, 14, 1:2], E_(13), AX, ALU.add)
            dve.drain()
            v.scalar_tensor_tensor(ends[:, 14, 2:3], misc[:, 0:1], float(P), ends[:, 14, 1:2], ALU.mult, ALU.add)
            dve.drain()
            v.tensor_copy(ends[:, 15, 8:9].bitcast(I32), ends[:, 14, 2:3])
            dve.drain()
            v.tensor_scalar(ends[:, 15, 8:9].bitcast(I32), ends[:, 15, 8:9].bitcast(I32), 7, None, ALU.arith_shift_right)
            dve.drain()
            v.tensor_copy(ends[:, 14, 3:4], ends[:, 15, 8:9].bitcast(I32))
            dve.drain()
            v.tensor_scalar(ends[:, 14, 4:5], ends[:, 14, 3:4], float(P), None, ALU.mult)
            v.tensor_scalar(ends[:, 14, 1:2], ends[:, 14, 3:4], float(LAST_WIN), None, ALU.min)
            dve.drain()
            v.tensor_tensor(ends[:, 14, 5:6], ends[:, 14, 2:3], ends[:, 14, 4:5], ALU.subtract)
            v.tensor_scalar(ends[:, 14, 6:7], ends[:, 14, 1:2], float(P), None, ALU.mult)
            v.tensor_copy(ends[:, 15, 0:2].bitcast(I32), ends[:, 14, 0:2])
            dve.drain()
            v.tensor_scalar(ends[:, 9, :], iota[:, :], ends[:, 14, 5:6], None, ALU.is_lt)
            v.tensor_scalar(ends[:, 10, :], iota[:, :], ends[:, 14, 5:6], None, ALU.is_ge)
            dve.drain()
            v.scalar_tensor_tensor(ends[:, 11, :], ends[:, 9, :], float(P), iota[:, :], ALU.mult, ALU.add)
            v.tensor_copy(place_out[:, :, 1], ends[:, 10, :])
            v.tensor_copy(place_out[:, :, 2], ends[:, 9, :])
            dve.drain()
            v.tensor_scalar(node_out, ends[:, 11, :], ends[:, 14, 4:5], None, ALU.add)
            v.tensor_scalar(ends[:, 12, :], ends[:, 11, :], ends[:, 14, 6:7], None, ALU.add)
            dve.drain()
            v.tensor_copy(place_out[:, :, 0], ends[:, 12, :])
            v.tensor_scalar(ends[0:1, 15, 4:5], ends[0:1, 8, NCH - 1:NCH], float(ALWAYS * RING), None, ALU.is_gt)
            dve.drain()
            v.tensor_copy(steps_left[:, :], ends[0:1, 15, 4:5])
            v.tensor_reduce(cm[:, 3:4], types_all.bitcast(F32), AX, ALU.max)
            v.tensor_tensor(wk34[32:34, :], wk34[32:34, :], bt34[32:34, :], ALU.add)
            v.tensor_scalar(blk4[:, :], blk[:, :], float(DH) ** -0.5, None, ALU.mult)
            v.tensor_scalar(cm[:, 4:5], cm[:, 0:1], -1.0, None, ALU.mult)
            dve.drain()
            v.tensor_tensor(cm[:, 1:2], cm[:, 0:1], cm[:, 4:5], ALU.max)
            dve.drain()
            v.tensor_scalar(cm[:, 5:6], cm[:, 1:2], 0.0, None, ALU.is_gt)
            v.tensor_scalar(cm[:, 6:7], cm[:, 1:2], 0.0, None, ALU.is_le)
            dve.drain()
            v.tensor_scalar(cm[:, 1:2], cm[:, 1:2], 1e-15, None, ALU.max)
            give(pre_asked)
            dve.wait_ge(pre_tr, 1)
            v.tensor_copy(g_out[0:NCH], ps[0:NCH, SM, 0:2 * P].rearrange("p (g c) -> p g c", g=2))
            v.tensor_reduce(cm[0:1, 3:4], ps[0:1, SM, 256:384], AX, ALU.max)
            give(pre_asked)
            dve.wait_ge(pre_tr, 2)
            v.tensor_scalar(cm[:, 7:8], ps[:, SM, 400:401], 1.0, 1.0, ALU.add, ALU.max)
            dve.drain()
            v.reciprocal(cm[:, 7:8], cm[:, 7:8])
            dve.wait_ge(steps_in, 16)
            dve.drain()
            v.tensor_scalar(wd1t[32:34, :], wd1t[32:34, :], cm[32:34, 7:8], None, ALU.mult)
            dve.drain()
            v.tensor_tensor(wd1t[32:34, :], wd1t[32:34, :], bd1r[32:34, :], ALU.add)
            v.tensor_tensor(B[:, :], X[:, :], X[:, :], ALU.mult)
            dve.drain().then_inc(src_ready, 1)
            v.tensor_reduce(col(0), nodes(B), AX, ALU.add)
            ask(0)
            v.tensor_scalar(col(1), col(1), 1e-15, None, ALU.max)
            v.tensor_scalar(hp[:, 5, :], hp[:, 3, :], -1.0, 1.0, ALU.mult, ALU.add)
            dve.drain()
            v.tensor_tensor(hp[:, 4, :], hp[:, 5, :], hp[:, 1, :], ALU.mult)
            v.tensor_scalar(col(3), col(1), cm[:, 2:3], None, ALU.mult)
            dve.drain()
            v.tensor_scalar(col(10), col(3), 1.0 / PI, None, ALU.mult)
            dve.drain()
            v.tensor_copy(col(14).bitcast(I32), col(10))
            dve.drain()
            v.tensor_copy(col(11), col(14).bitcast(I32))
            dve.drain()
            v.scalar_tensor_tensor(col(4), col(11), -PI, col(3), ALU.mult, ALU.add)
            dve.drain()
            v.tensor_scalar(col(4), col(4), 3.1415925, -3.1415925, ALU.min, ALU.max)
            dve.drain()
            v.scalar_tensor_tensor(col(6), col(4), -1.0, col(4), ALU.mult, ALU.max)
            dve.drain()
            v.tensor_scalar(col(5), col(6), -1.0, PI / 2, ALU.mult, ALU.add)
            ask(1)
            v.tensor_scalar(col(7), col(7), cm[:, 5:6], None, ALU.mult)
            v.tensor_scalar(col(8), col(8), cm[:, 6:7], None, ALU.mult)
            v.tensor_scalar(col(9), col(9), cm[:, 6:7], cm[:, 5:6], ALU.mult, ALU.add)
            dve.drain()
            v.tensor_tensor(col(7), col(7), col(8), ALU.add)
            v.tensor_tensor(col(9), col(9), col(3), ALU.mult)
            dve.drain()
            v.reciprocal(col(9), col(9))
            dve.drain()
            v.tensor_tensor(col(7), col(7), col(9), ALU.mult)
            dve.drain()
            v.tensor_tensor(nodes(C), nodes(X), onto(col(7)), ALU.mult)
            dve.drain()
            v.tensor_tensor(B[:, :], C[:, :], C[:, :], ALU.mult)
            dve.drain()
            v.tensor_reduce(col(12), nodes(B), AX, ALU.add)
            v.reciprocal(cm[:, 2:3], cm[:, 2:3])
            dve.drain()
            v.tensor_scalar(cm[:, 2:3], cm[:, 2:3], 1.0 - 1e-5, None, ALU.mult)
            ask(2)
            v.tensor_scalar(col(15), col(13), cm[:, 2:3], None, ALU.is_gt)
            v.tensor_scalar(col(16), col(13), cm[:, 2:3], None, ALU.max)
            dve.drain()
            v.reciprocal(col(16), col(16))
            dve.drain()
            v.tensor_scalar(col(16), col(16), cm[:, 2:3], -1.0, ALU.mult, ALU.add)
            dve.drain()
            v.tensor_tensor(col(16), col(16), col(15), ALU.mult)
            dve.drain()
            v.tensor_scalar(col(16), col(16), 1.0, None, ALU.add)
            dve.drain()
            v.tensor_tensor(nodes(C), nodes(C), onto(col(16)), ALU.mult)
            evacuate(0, H, None)
            evacuate(1, A, None)
            evacuate(2, B, None)
            v.tensor_scalar(T[:, :], C[:, :], -1.0, None, ALU.mult)
            give(store_ask)

            def onehots(kind, k, passes, i, b, section):
                dve.wait_ge(in_ready[kind][section][b], count(passes, i, section) * 16 * LOADS[kind])
                for j in range(EPP):
                    ins = v.tensor_scalar(onehot[:, b, j, :], win_nodes[:, b, :], pk[:, b, j:j + 1], None, ALU.is_equal)
                ins.then_inc(s["oh_ready"], 1)

            def tiles(kind, passes, i, b, section):
                if kind != "sum":
                    dve.wait_ge(ids_in[kind][section][b], count(passes, i, section) * 16 * ID_LOADS[kind])
                v.tensor_copy(in_tile[:, b, :], places[:, b, 1:3])

            heads_first = lambda t: t.rearrange("p (h j) -> p h j", j=EPP)
            per_edge = lambda ap: ap.unsqueeze(1).broadcast_to([P, HEADS, EPP])
            per_head = lambda ap: ap.unsqueeze(2).broadcast_to([P, HEADS, EPP])

            q = {n: t[:, :] for n, t in small.items()}

            def own_maxima(k, b):
                v.tensor_copy(scans[0:HEADS, 1:2], scans[0:HEADS, 129:130])
                dve.drain()
                after(dve, "pens_ready", k)
                v.tensor_tensor_scan(q["run_f"], q["pen_f"], q["logit"], NEG, ALU.add, ALU.max)
                dve.drain()
                v.tensor_tensor_scan(q["run_r"][:, ::-1], q["pen_r"][:, ::-1], q["run_f"][:, ::-1], NEG, ALU.add, ALU.max)
                dve.drain()
                v.tensor_copy(ab[:, 0:HEADS], heads_first(q["run_f"])[:, :, EPP - 1])
                v.tensor_copy(ab[:, 32:32 + HEADS], heads_first(q["run_r"])[:, :, 0])
                give(s["ab_ready"])

            def between(k, b):
                after(dve, "ab_mm", k)
                v.tensor_tensor_scan(scans[0:HEADS, 2:130], gp[0:HEADS, b, :], ps[0:HEADS, SM, 64:192],
                                     scans[0:HEADS, 1:2], ALU.add, ALU.max)
                v.tensor_tensor_scan(scans[32:32 + HEADS, 127::-1], gp[32:32 + HEADS, b, ::-1], ps[32:32 + HEADS, SM, 191:63:-1],
                                     NEG, ALU.add, ALU.max)
                give(s["scan_ready"])

            def less_maxima(k, b):
                after(dve, "back_mm", k)
                before, behind = ps[:, SM, 192:192 + HEADS], ps[:, SM, 224:224 + HEADS]
                v.tensor_tensor(heads_first(q["m1"]), per_head(before), per_edge(pk[:, b, 3 * EPP:4 * EPP]), ALU.add)
                v.tensor_tensor(heads_first(q["m2"]), per_head(behind), per_edge(pk[:, b, 4 * EPP:5 * EPP]), ALU.add)
                dve.drain()
                v.tensor_tensor(q["m1"], q["m1"], q["run_r"], ALU.max)
                dve.drain()
                v.tensor_tensor(q["m1"], q["m1"], q["m2"], ALU.max)
                dve.drain()
                v.tensor_tensor(delta[:, 0:S64], q["logit"], q["m1"], ALU.subtract)
                v.tensor_tensor(delta[:, S64:], before, heads_first(q["m1"])[:, :, 0], ALU.subtract)
                dve.drain()
                v.tensor_scalar(delta[:, S64:], delta[:, S64:], 0.0, None, ALU.min)
                give(s["delta_ready"])

            def rows_weighted(k, b, passes, i, section, width, c0, typed):
                after(dve, "ex_ready", k)
                dve.wait_ge(gathered["edges"][section][b], count(passes, i, section) * 16 * GATHERS["L1"])
                by_head = weighted[:, :, 0:RC].rearrange("p j (h c) -> p j h c", c=HW)
                e = ex[:, 0:S64].rearrange("p (h j) -> p j h", j=EPP)
                vals = rows[b][:, 0:EPP * width].rearrange("p (j r) -> p j r", r=width)[:, :, c0:c0 + D].rearrange("p j (h c) -> p j h c", c=DH)
                v.tensor_tensor(by_head[:, :, :, 0:DH], vals, e.unsqueeze(3).broadcast_to([P, EPP, HEADS, DH]), ALU.mult)
                v.tensor_scalar(weighted[:, 0, RC:AW], ex[:, S64:], -1.0, misc[:, 1:2], ALU.add, ALU.mult)
                if typed:
                    v.tensor_tensor(by_head[:, :, :, DH + 1], e, type_f[:, b, :].unsqueeze(2).broadcast_to([P, EPP, HEADS]), ALU.mult)
                    dve.drain()
                    v.tensor_tensor(by_head[:, :, :, DH], e, by_head[:, :, :, DH + 1], ALU.subtract)
                else:
                    v.tensor_copy(by_head[:, :, :, DH], e)
                give(s["weighted_ready"])

            def accumulate(k, r, b, width, rescaled):
                w = dve.value_load(steps_i[0:1, bass.ds(r * 2 + 1, 1)], min_val=0, max_val=LAST_WIN)
                after(dve, "agg_mm", k)
                own = acc[:, bass.ds(w, 2), :]
                if rescaled:
                    after(dve, "grow_ready", k)
                    by_head = own[:, :, 0:RC].rearrange("p w (h c) -> p w h c", c=HW)
                    v.tensor_tensor(by_head, by_head, grow[:, :, :].unsqueeze(3).broadcast_to([P, 2, HEADS, HW]), ALU.mult)
                    dve.drain()
                for t in range(2):
                    one = acc[:, bass.ds(w + t, 1), 0:width]
                    v.scalar_tensor_tensor(one, ps[:, AGG, 0:width].unsqueeze(1), in_tile[:, b, t:t + 1], one, ALU.mult, ALU.add)
                give(s["acc_done"])

            def clear(kind):
                v.memset(acc[:, :, :], 0.0)
                if kind == "sum":
                    for b in range(RING):
                        v.memset(rows[b][:, 0:EPP * SUMW].rearrange("p (j r) -> p j r", r=SUMW)[:, :, D:], 1.0)
                else:
                    v.memset(scans[0:HEADS, 129:130], NEG)
                    v.memset(weighted[:, :, :], 0.0)
                dve.drain()

            dve.wait_ge(stored, 5 * 16)
            v.memset(dec_h[64:65, :, :], 1.0)
            clear("L0")
            def l0_types(k, b):
                v.tensor_copy(type_f[:, b, :], type_i[:, b, :])
                v.tensor_scalar(attr[32:34, b, :], attr[96:98, b, :].bitcast(I32), misc[96:98, 3:4], misc[96:98, 4:5], ALU.mult, ALU.add)
                give(s["types_ready"])

            def l0_product(k, h):
                after(dve, "z_copied", k, h)
                v.tensor_tensor(prod[:, h, :], ps[:, MM0, :], chan[:, h, :], ALU.mult).then_inc(s["z_used"], 1)

            def l0_scaled_decay(k):
                after(dve, "tanh_ready", k)
                v.tensor_tensor(heads_first(q["dec2"]), heads_first(q["dec"]), per_head(hp[:, 0, :]), ALU.mult)
                give(s["decs_ready"])

            def l0_logits(k):
                after(dve, "logit_mm", k)
                v.tensor_copy(dist2[:, :], ps[:, SM, 320:320 + EPP])
                give(s["dist_asked"])
                v.tensor_tensor(heads_first(q["m1"]), heads_first(ps[:, SM, 0:S64]), per_head(hp[:, 3, :]), ALU.mult)
                after(dve, "decay_ready", k)
                after(dve, "dist_ready", k)
                v.tensor_tensor(heads_first(q["m2"]), per_head(hp[:, 4, :]), per_edge(dist[:, :]), ALU.mult)
                dve.drain()
                v.tensor_tensor(q["m1"], q["m1"], q["m2"], ALU.subtract)
                dve.drain()
                v.tensor_tensor(q["logit"], q["m1"], q["dec"], ALU.mult)
                dve.drain()

            def l0_begin(i, section):
                k = first_step(0) + i * RING
                for b in range(RING):
                    tiles("L0", 0, i, b, section)
                dve.drain()
                for b in range(RING):
                    onehots("L0", k + b, 0, i, b, section)
                    l0_types(k + b, b)
                l0_product(k, 0)
                l0_scaled_decay(k)
                l0_product(k, 1)
                l0_logits(k)
                own_maxima(k, 0)
                between(k, 0)

            def l0_step(i, b, more, section):
                k = first_step(0) + i * RING + b
                less_maxima(k, b)
                if more:
                    l0_product(k + 1, 0)
                if more:
                    l0_scaled_decay(k + 1)
                    l0_product(k + 1, 1)
                rows_weighted(k, b, 0, i, section, 3 * D, D, True)
                if more:
                    l0_logits(k + 1)
                    own_maxima(k + 1, later(i, b, 1)[1])
                    between(k + 1, later(i, b, 1)[1])
                if more > 2:
                    after(dve, "agg_mm", k)
                    onehots("L0", k + RING, 0, i + 1, b, section)
                accumulate(k, i * RING + b, b, RC, True)
                if more > 2:
                    tiles("L0", 0, i + 1, b, section)
                    l0_types(k + RING, b)

            turns(dve, l0_step, l0_begin, skip_steps(dve, "dve", "L0"))

            def head_means(dst):
                by_head = acc[:, :, 0:RC].rearrange("p t (h c) -> p t h c", c=HW)
                v.tensor_tensor(den, by_head[:, :, :, DH], by_head[:, :, :, DH + 1], ALU.add)
                dve.drain()
                v.tensor_scalar(den, den, 1e-30, None, ALU.max)
                dve.drain()
                v.reciprocal(den, den)
                dve.drain()
                v.tensor_tensor(dst[:, :].rearrange("p (t h c) -> p t h c", h=HEADS, c=DH), by_head[:, :, :, 0:DH],
                                den.unsqueeze(3).broadcast_to([P, NT, HEADS, DH]), ALU.mult)
                dve.drain()

            den = cols[:, 20:28, :].rearrange("p h t -> p (h t)").rearrange("p (t h) -> p t h", h=HEADS)
            part = cols[:, 28:36, :].rearrange("p h t -> p (h t)").rearrange("p (t h) -> p t h", h=HEADS)
            head_means(A)
            for t in range(2):
                v.tensor_tensor(part, acc[:, :, 0:RC].rearrange("p t (h c) -> p t h c", c=HW)[:, :, :, DH + t], den, ALU.mult)
                dve.drain()
                v.tensor_tensor(B[:, :].rearrange("p (t h c) -> p t h c", h=HEADS, c=DH),
                                relv[:, t, :].rearrange("p (h c) -> p h c", c=DH).unsqueeze(1).broadcast_to([P, NT, HEADS, DH]),
                                part.unsqueeze(3).broadcast_to([P, NT, HEADS, DH]), ALU.mult)
                dve.drain()
                v.tensor_tensor(A[:, :], A[:, :], B[:, :], ALU.add)
                dve.drain()
            give(src_ready)
            evacuate(3, B, of(X))
            v.tensor_tensor(nodes(B), nodes(B), along(V["bo"]), ALU.add)
            norm(H, B, 3, V["g1"], V["be1"])
            give(src_ready)
            evacuate(4, B, of(H))
            v.tensor_tensor(nodes(B), nodes(B), along(V["bf2"]), ALU.add)
            norm(H, B, 4, V["g2"], V["be2"])
            v.tensor_tensor(B[:, :], X[:, :], H[:, :], ALU.add)
            norm(X, B, 5)
            give(src_ready)
            evacuate(5, A, bias(V["Win_b"]))
            ask(6)
            norm(H, A, 7, V["ln_in_g"], V["ln_in_b"])
            with dve.Fori(0, LAYERS) as l:
                give(layer_used)
                dve.wait_ge(layer_in, (l + 1) * 16 * 13)
                v.tensor_scalar(attb[:, :], blk[:, :], att[:, 0:1], None, ALU.mult)
                norm(A, H, 8 + l * 3, V["ln_g"], V["ln_b"])
                give(src_ready)
                evacuate(6 + l * 3, B, bias(V["Wl_b"]))
                evacuate(7 + l * 3, C, bias(V["Wr_b"]))
                give(store_ask)
                clear("L1")

                def l1_leaky(k, h):
                    after(dve, "z_copied", k, h)
                    v.tensor_tensor(prod[:, h, :], ps[:, MM0 + h, :], chan[:, h, :], ALU.max).then_inc(s["z_used"], 1)

                def l1_logits(k):
                    after(dve, "logit_mm", k)
                    v.tensor_copy(q["logit"], ps[:, SM, 0:S64])

                def l1_begin(i, section):
                    k = first_step(1) + l * STEPS + i * RING
                    for b in range(RING):
                        tiles("L1", l, i, b, section)
                    dve.drain()
                    for b in range(RING):
                        onehots("L1", k + b, l, i, b, section)
                    l1_leaky(k, 0)
                    l1_leaky(k, 1)
                    l1_logits(k)
                    own_maxima(k, 0)
                    between(k, 0)

                def l1_step(i, b, more, section):
                    k = first_step(1) + l * STEPS + i * RING + b
                    less_maxima(k, b)
                    if more:
                        l1_leaky(k + 1, 0)
                    if more:
                        l1_leaky(k + 1, 1)
                    rows_weighted(k, b, l + 1, i, section, D, 0, False)
                    if more:
                        l1_logits(k + 1)
                        own_maxima(k + 1, later(i, b, 1)[1])
                        between(k + 1, later(i, b, 1)[1])
                    if more > 2:
                        after(dve, "agg_mm", k)
                        onehots("L1", k + RING, l, i + 1, b, section)
                    accumulate(k, i * RING + b, b, RC, True)
                    if more > 2:
                        tiles("L1", l, i + 1, b, section)

                turns(dve, l1_step, l1_begin, skip_steps(dve, "dve", "L1"))
                head_means(A)
                v.tensor_tensor(nodes(A), nodes(A), along(V["conv_b"]), ALU.add)
                ask(9 + l * 3)
                dve.sem_inc(src_ready, 1)
                evacuate(8 + l * 3, B, bias(V["g2_b"]))
                ask(10 + l * 3)
                v.tensor_tensor(B[:, :], B[:, :], A[:, :], ALU.mult)
                dve.drain()
                v.tensor_tensor(H[:, :], H[:, :], B[:, :], ALU.add)
                dve.drain()
            n0 = 8 + 3 * LAYERS
            norm(A, H, n0, V["fn_g"], V["fn_b"])
            v.tensor_tensor(B[:, :], X[:, :], A[:, :], ALU.add)
            norm(X, B, n0 + 1)
            for n in range(3):
                clear("sum")
                give(store_ask)
                def sum_begin(i, section):
                    onehots("sum", first_step(1 + LAYERS + n) + i * RING, n, i, 0, section)
                    tiles("sum", n, i, 0, section)
                    dve.drain()

                def sum_step(i, b, more, section):
                    k = first_step(1 + LAYERS + n) + i * RING + b
                    i1, b1 = later(i, b, 1)
                    if more:
                        onehots("sum", k + 1, n, i1, b1, section)
                        tiles("sum", n, i1, b1, section)
                    accumulate(k, i * RING + b, b, D + 1, False)

                turns(dve, sum_step, sum_begin, skip_steps(dve, "dve", "sum"))
                v.tensor_scalar(col(3), acc[:, :, D], 1.0, None, ALU.max)
                dve.drain()
                v.reciprocal(col(3), col(3))
                dve.drain()
                v.tensor_tensor(nodes(A), acc[:, :, 0:D], onto(col(3)), ALU.mult)
                if n == 2:
                    dve.drain()
                    v.tensor_tensor(A[:, :], A[:, :], X[:, :], ALU.add)
                give(src_ready)
                m = 6 + 3 * LAYERS + n
                if n < 2:
                    dve.sem_inc(src_ready, 1)
                evacuate(m, B if n else H, bias(V[("L2_bl1", "L2_bl2", "L3_b")[n]]))
                if n == 2:
                    v.tensor_scalar(B[:, :], B[:, :], 0.0, None, ALU.max)
                    dve.drain()
                if n:
                    v.tensor_tensor(B[:, :], B[:, :], X[:, :], ALU.add)
                    norm(X, B, n0 + 1 + n)
            give(store_ask)


NAMES = ["x", "src_edges", "type_edges", "dst_win", "dst_ends", "type_rows", "weight_rows", "time_edges", "attr_edges",
         "c_ident", "c_iota", "c_blk", "c_misc",
         "L0_gnn_Wq", "L0_gnn_Wk", "L0_gnn_Wv", "L0_gnn_rel_q", "L0_gnn_rel_k", "L0_gnn_rel_v", "L0_gnn_Wt", "L0_gnn_bt",
         "L0_gnn_Wd1", "L0_gnn_bd1", "L0_gnn_Wd2", "L0_gnn_bd2", "L0_gnn_decay_scale", "L0_gnn_c_mag", "L0_gnn_hyp_beta",
         "L0_gnn_logit_alpha", "L0_gnn_Wo", "L0_gnn_bo", "L0_gnn_g1", "L0_gnn_be1", "L0_gnn_g2", "L0_gnn_be2",
         "L0_gnn_Wf1", "L0_gnn_bf1", "L0_gnn_Wf2", "L0_gnn_bf2",
         "L1_gnn_Win_w", "L1_gnn_Win_b", "L1_gnn_ln_in_g", "L1_gnn_ln_in_b", "L1_gnn_ln_g", "L1_gnn_ln_b", "L1_gnn_Wl_w",
         "L1_gnn_Wl_b", "L1_gnn_Wr_w", "L1_gnn_Wr_b", "L1_gnn_We_w", "L1_gnn_att", "L1_gnn_conv_b", "L1_gnn_g1_w",
         "L1_gnn_g1_b", "L1_gnn_g2_w", "L1_gnn_g2_b", "L1_gnn_fn_g", "L1_gnn_fn_b",
         "L2_gnn_Wl1_T", "L2_gnn_bl1", "L2_gnn_Wr1_T", "L2_gnn_Wl2_T", "L2_gnn_bl2", "L2_gnn_Wr2_T", "L3_gnn_W_T", "L3_gnn_b"]


def lay_out(inputs):
    import numpy as np

    a = {k: np.asarray(v) for k, v in inputs.items()}
    extra = NCH * CHUNK - E

    def padded(v, fill=0):
        return np.concatenate([v, np.full((extra,) + v.shape[1:], fill, v.dtype)])

    def by_partition(v):
        return np.ascontiguousarray(padded(v).reshape(NCH, P, EPP))

    def by_tile(v):
        w = padded(v).reshape(NCH, P, EPP, v.shape[1])
        return np.ascontiguousarray(w.transpose(0, 3, 2, 1)).reshape(NCH, v.shape[1], CHUNK)

    o = dict(a)
    o["x"] = np.concatenate([a["x"], np.zeros((NP - N, D), a["x"].dtype)])
    o["src_edges"] = by_partition(a["src"])
    dst = padded(a["dst"], N)
    around = np.concatenate([np.full(1, -1, dst.dtype), dst, np.full(1, -1, dst.dtype)])
    windows = [around[k:k + NCH * CHUNK:EPP].reshape(NCH, P) for k in range(EPP + 2)]
    o["dst_win"] = np.ascontiguousarray(np.stack(windows, axis=-1).transpose(1, 0, 2))
    o["dst_ends"] = np.ascontiguousarray(dst.reshape(NCH, CHUNK)[:, [0, CHUNK - 1]].T)
    o["type_edges"] = by_partition(a["edge_type_2"])
    o["type_rows"] = by_tile(a["edge_type_2"][:, None])[:, 0]
    o["weight_rows"] = by_tile(a["edge_weight"][:, None])[:, 0]
    o["time_edges"] = by_tile(a["edge_attr_32"])
    o["attr_edges"] = by_tile(a["edge_attr_3"])
    o["L1_gnn_att"] = a["L1_gnn_att"].reshape(LAYERS, D, 1)
    o["L1_gnn_g1_b"] = a["L1_gnn_g1_b"].reshape(LAYERS, 64, 1)
    o["L0_gnn_c_mag"] = a["L0_gnn_c_mag"].reshape(1)
    for n in ("Wl1", "Wr1", "Wl2", "Wr2"):
        o[f"L2_gnn_{n}_T"] = np.ascontiguousarray(a["L2_gnn_" + n].T)
    o["L3_gnn_W_T"] = np.ascontiguousarray(a["L3_gnn_W"].T)
    p = np.arange(P)
    o["c_ident"] = np.eye(P, dtype=np.float32)
    o["c_iota"] = np.ascontiguousarray(np.broadcast_to(np.arange(P, dtype=np.float32), (P, P)))
    o["c_blk"] = (p[:, None] // DH == np.arange(HEADS)).astype(np.float32)
    misc = np.zeros((P, 8), np.float32)
    misc[:, 0] = p
    misc[0, 1] = 1
    misc[:, 2] = 1
    misc[96:98, 3] = (1, -1)
    misc[96:98, 4] = (0, 1)
    o["c_misc"] = misc
    return {n: o[n] for n in NAMES}


def program(nc, arrays):
    a = {n: nc.dram_tensor("in_" + n, v.shape, mybir.dt.from_np(v.dtype), kind="ExternalInput").ap() for n, v in arrays.items()}
    out = nc.dram_tensor("out_nodes", (N, D), F32, kind="ExternalOutput").ap()
    build(nc, a, out)


def kernel(**inputs):
    import concourse.bacc as bacc
    from concourse.bass_utils import run_bass_kernel_spmd

    arrays = lay_out(inputs)
    nc = bacc.Bacc("TRN2", target_bir_lowering=False, num_devices=1)
    program(nc, arrays)
    r = run_bass_kernel_spmd(nc, [{"in_" + n: v for n, v in arrays.items()}], core_ids=[0])
    return r.results[0]["out_nodes"]
```
